# Optimizing a Trainium2 kernel written in Bass

```python
import numpy as np
import jax
import jax.numpy as jnp

def _softmax(x, axis=-1):
    return jax.nn.softmax(x, axis=axis)

def _gelu(x):
    return jax.nn.gelu(x, approximate=True)

def _silu(x):
    return jax.nn.silu(x)

def _sigmoid(x):
    return jax.nn.sigmoid(x)

def _layernorm(x, axis=-1, eps=1e-05):
    m = jnp.mean(x, axis=axis, keepdims=True)
    v = jnp.var(x, axis=axis, keepdims=True)
    return (x - m) / jnp.sqrt(v + eps)

def _scatter_add(tgt, idx, src, axis=0):
    return tgt.at[idx].add(src)

def _segment_sum(src, seg, n):
    return jax.ops.segment_sum(src, seg, n)
kernel_name = 'mk_recurrent_d1_jaxref_r4_ec16e7'

def setup_inputs(seed: int=0):
    np.random.seed(seed)
    _w = jnp.asarray

    def _L0_attn_setup():
        import jax, jax.numpy as jnp
        import numpy as np
        B, T, C = (2, 512, 512)
        H, KVH = (8, 2)
        DH = C // H
        ROPE_BASE = 10000.0
        NEG = -1000000000.0

        def _rope_tables(t, d):
            inv = 1.0 / ROPE_BASE ** (jnp.arange(0, d, 2, dtype=jnp.float32) / d)
            f = jnp.arange(t, dtype=jnp.float32)[:, None] * inv[None, :]
            cos = jnp.concatenate([jnp.cos(f), jnp.cos(f)], axis=-1)
            sin = jnp.concatenate([jnp.sin(f), jnp.sin(f)], axis=-1)
            return (cos, sin)

        def _apply_rope(x, cos, sin):
            d = x.shape[-1] // 2
            x1, x2 = (x[..., :d], x[..., d:])
            rot = jnp.concatenate([-x2, x1], axis=-1)
            return x * cos + rot * sin

        def _head_dirs():
            trig = np.array([[sx, sy, sz] for sx in (1.0, -1.0) for sy in (1.0, -1.0) for sz in (1.0, -1.0)], dtype=np.float32)
            return jnp.asarray(trig / np.sqrt(3.0))
        key = jax.random.key(seed)
        ks = jax.random.split(key, 6)
        s = 0.02
        return {'x': jax.random.normal(ks[0], (B, T, C), jnp.float32), 'Wq': jax.random.normal(ks[1], (C, H * DH), jnp.float32) * s, 'Wk': jax.random.normal(ks[2], (C, KVH * DH), jnp.float32) * s, 'Wv': jax.random.normal(ks[3], (C, KVH * DH), jnp.float32) * s, 'Wo': jax.random.normal(ks[4], (C, C), jnp.float32) * s, 'head_scales': jax.random.normal(ks[5], (H,), jnp.float32) * 0.1}
    _L0_attn_in = _L0_attn_setup()

    def _L0_ffn_setup():
        import jax, jax.numpy as jnp
        import numpy as np
        TOP_K = 2
        key = jax.random.key(seed)
        ks = jax.random.split(key, 7)
        B, S, H = (2, 512, 512)
        E, A, NS = (8, 64, 4096)
        x = jax.random.normal(ks[0], (B, S, H), jnp.float32)
        gate_w = jax.random.normal(ks[1], (E, H), jnp.float32) * 0.01
        W = jax.random.normal(ks[2], (H, H), jnp.float32) * 0.02
        atoms = jax.random.normal(ks[3], (A, NS), jnp.float32) * 0.02
        expert_atom_weights = jax.random.normal(ks[4], (E, A), jnp.float32) * 0.1
        importance = jax.random.normal(ks[5], (E, NS), jnp.float32) * 0.1
        mask_idx = jax.random.randint(ks[6], (NS,), 0, H * H, jnp.int32)
        return dict(x=x, gate_w=gate_w, W=W, atoms=atoms, expert_atom_weights=expert_atom_weights, importance=importance, mask_idx=mask_idx)
    _L0_ffn_in = _L0_ffn_setup()
    _d = {'L0_attn_x': _L0_attn_in['x'], 'L0_attn_Wq': _L0_attn_in['Wq'], 'L0_attn_Wk': _L0_attn_in['Wk'], 'L0_attn_Wv': _L0_attn_in['Wv'], 'L0_attn_Wo': _L0_attn_in['Wo'], 'L0_attn_head_scales': _L0_attn_in['head_scales'], 'L0_ffn_gate_w': _L0_ffn_in['gate_w'], 'L0_ffn_W': _L0_ffn_in['W'], 'L0_ffn_atoms': _L0_ffn_in['atoms'], 'L0_ffn_expert_atom_weights': _L0_ffn_in['expert_atom_weights'], 'L0_ffn_importance': _L0_ffn_in['importance'], 'L0_ffn_mask_idx': _L0_ffn_in['mask_idx']}
    _x0 = _d['L0_attn_x']
    _d['L0_attn_x'] = jax.random.normal(jax.random.fold_in(jax.random.key(seed), 1), (8, 512, 512), dtype=_x0.dtype)
    del _x0
    return _d

def reference(L0_attn_x, L0_attn_Wq, L0_attn_Wk, L0_attn_Wv, L0_attn_Wo, L0_attn_head_scales, L0_ffn_gate_w, L0_ffn_W, L0_ffn_atoms, L0_ffn_expert_atom_weights, L0_ffn_importance, L0_ffn_mask_idx):

    def _L0_attn_ref(x, Wq, Wk, Wv, Wo, head_scales):
        import jax, jax.numpy as jnp
        import numpy as np
        B, T, C = (2, 512, 512)
        H, KVH = (8, 2)
        DH = C // H
        ROPE_BASE = 10000.0
        NEG = -1000000000.0

        def _rope_tables(t, d):
            inv = 1.0 / ROPE_BASE ** (jnp.arange(0, d, 2, dtype=jnp.float32) / d)
            f = jnp.arange(t, dtype=jnp.float32)[:, None] * inv[None, :]
            cos = jnp.concatenate([jnp.cos(f), jnp.cos(f)], axis=-1)
            sin = jnp.concatenate([jnp.sin(f), jnp.sin(f)], axis=-1)
            return (cos, sin)

        def _apply_rope(x, cos, sin):
            d = x.shape[-1] // 2
            x1, x2 = (x[..., :d], x[..., d:])
            rot = jnp.concatenate([-x2, x1], axis=-1)
            return x * cos + rot * sin

        def _head_dirs():
            trig = np.array([[sx, sy, sz] for sx in (1.0, -1.0) for sy in (1.0, -1.0) for sz in (1.0, -1.0)], dtype=np.float32)
            return jnp.asarray(trig / np.sqrt(3.0))
        Bn, Tn, Cn = x.shape
        q = (x @ Wq).reshape(Bn, Tn, H, DH).transpose(0, 2, 1, 3)
        k = (x @ Wk).reshape(Bn, Tn, KVH, DH).transpose(0, 2, 1, 3)
        v = (x @ Wv).reshape(Bn, Tn, KVH, DH).transpose(0, 2, 1, 3)
        cos, sin = _rope_tables(Tn, DH)
        q = _apply_rope(q, cos, sin)
        k = _apply_rope(k, cos, sin)
        rep = H // KVH
        k = jnp.repeat(k, rep, axis=1)
        v = jnp.repeat(v, rep, axis=1)
        causal = jnp.tril(jnp.ones((Tn, Tn), dtype=bool))
        scale = DH ** (-0.5)
        scores = jnp.einsum('bhtd,bhsd->bhts', q, k) * scale
        scores = jnp.where(causal, scores, NEG)
        out = jax.nn.softmax(scores, axis=-1) @ v
        dirs = _head_dirs()
        qp = jnp.einsum('bhtd,hd->bht', q[..., :3], dirs)
        kp = jnp.einsum('bhsd,hd->bhs', k[..., :3], dirs)
        geo = qp[..., :, None] * kp[..., None, :]
        geo = jnp.where(causal, geo, NEG)
        geo_out = jax.nn.softmax(geo, axis=-1) @ v
        scales = head_scales[None, :, None, None]
        out = out + scales * jax.lax.stop_gradient(geo_out - out)
        out = out.transpose(0, 2, 1, 3).reshape(Bn, Tn, Cn)
        return out @ Wo

    def _L0_ffn_ref(x, gate_w, W, atoms, expert_atom_weights, importance, mask_idx):
        import jax, jax.numpy as jnp
        import numpy as np
        TOP_K = 2
        B, S, H = x.shape
        xt = x.reshape(-1, H)
        logits = jnp.clip(xt @ gate_w.T, -50.0, 50.0)
        top_w, top_idx = jax.lax.top_k(logits, TOP_K)
        rw = jax.nn.softmax(top_w, axis=-1)
        deltas = jax.nn.softmax(expert_atom_weights, axis=-1) @ atoms
        weighted = deltas * jax.nn.sigmoid(importance)
        rows = mask_idx // H
        cols = mask_idx % H
        vals = jnp.einsum('tk,tks->ts', rw, weighted[top_idx])
        xg = xt[:, cols]
        contrib = jax.ops.segment_sum((xg * vals).T, rows, num_segments=H)
        out = xt @ W.T + contrib.T
        return out.reshape(B, S, H)
    x = L0_attn_x
    xn = _layernorm(x, axis=-1)
    s = _L0_attn_ref(xn, L0_attn_Wq, L0_attn_Wk, L0_attn_Wv, L0_attn_Wo, L0_attn_head_scales)
    g = _silu(_L0_ffn_ref(xn, L0_ffn_gate_w, L0_ffn_W, L0_ffn_atoms, L0_ffn_expert_atom_weights, L0_ffn_importance, L0_ffn_mask_idx))
    x = x + s * g
    return x

_drawn_inputs = setup_inputs


def setup_inputs(seed=0):
    import zlib

    import numpy as np

    out = dict(_drawn_inputs(seed))
    spreads = {}
    factors = {'L0_attn_Wq': 8.0,
     'L0_attn_Wk': 8.0,
     'L0_attn_Wv': 8.0,
     'L0_attn_Wo': 8.0,
     'L0_attn_head_scales': 8.0,
     'L0_ffn_gate_w': 64.0,
     'L0_ffn_W': 8.0,
     'L0_ffn_atoms': 41.533,
     'L0_ffn_expert_atom_weights': 63.023,
     'L0_ffn_importance': 64.0}
    for name, (base, spread) in spreads.items():
        noise = np.random.default_rng([zlib.crc32(name.encode()), seed]).standard_normal(out[name].shape)
        drawn = base * np.exp(spread * noise) if base else spread * noise
        out[name] = jnp.asarray(drawn.astype(out[name].dtype))
    for name, factor in factors.items():
        out[name] = (out[name] * factor).astype(out[name].dtype)
    return out
```

```python
from contextlib import ExitStack

import concourse.bass as bass
from concourse import mybir

F32 = mybir.dt.float32
F32R = mybir.dt.float32r
BF16 = mybir.dt.bfloat16
I32 = mybir.dt.int32
U32 = mybir.dt.uint32
ALU = mybir.AluOpType
ACT = mybir.ActivationFunctionType
AX = mybir.AxisListType.X

P = 128
B, T, C = 8, 512, 512
NI = T // P
NC = C // P
NT = B * NI
H, KVH, DH = 8, 2, 64
REP = H // KVH
HALF = DH // 2
QC, KC = H * DH, KVH * DH
E, A, NS = 8, 64, 4096
NSC = NS // P
TOPK = 2
NJ = TOPK * B * T // P + E
WCOLS = QC + 2 * KC + E
EPS = 1e-5
NEG = -1e30
QROWS = DH + 2
GROWS = 104
SOFF = [sum(T - P * m for m in range(j)) for j in range(NI + 1)]

WORK = [("xt", i) for i in range(NI)] + [("kt", v) for v in range(KVH)] + [("tk",), ("tq",)]
for _h in range(2):
    WORK += [("qa", _h)] + [("qm", _h, i) for i in range(NI)]
WORK += [("qb", 0)]
for _h in range(H):
    if _h + 1 < H:
        WORK += [("qb", _h + 1)]
    if _h + 2 < H:
        WORK += [("qa", _h + 2)] + [("qm", _h + 2, i) for i in range(NI)]
WORK += [("at", i) for i in range(NI)]
WORK_USE = {name: u for u, name in enumerate(WORK)}
NWORK = len(WORK)
PAIR = [("p", i) for i in range(NI)] + [("s", h, j) for h in range(H) for j in range(NI)] \
    + [("wo", i) for i in range(NI)]
PAIR_USE = {name: u for u, name in enumerate(PAIR)}
NPAIR = len(PAIR)
assert NWORK % 2 == 0 and NPAIR % 2 == 0


def build(nc, x, Wq, Wk, Wv, Wo, head_scales, gate_w, ffn_W, atoms, expert_atom_weights, importance,
          mask_idx, c_ident, c_rope, c_dirs, c_onehot, c_rows, out):
    xn_d = nc.dram_tensor("xn_d", (B * T, C), F32, kind="Internal").ap()
    s_d = nc.dram_tensor("s_d", (B * T, C), F32, kind="Internal").ap()
    y_d = nc.dram_tensor("y_d", (NJ * P, C), F32, kind="Internal").ap()
    pair_d = nc.dram_tensor("pair_d", (NJ * P, 2), F32, kind="Internal").ap()
    upd_d = nc.dram_tensor("upd_d", (C * C + P, E), F32, kind="Internal").ap()

    x_f = x.rearrange("b t c -> (b t) c")
    out_f = out.rearrange("b t c -> (b t) c")

    with ExitStack() as ctx:
        def sem(name):
            return ctx.enter_context(nc.semaphore(name))

        def psum(name, shape, dt=F32):
            return ctx.enter_context(nc.psum_tensor(name, shape, dt))

        def keep(name, shape, dt=F32):
            return ctx.enter_context(nc.sbuf_tensor(name, shape, dt))

        ident = keep("ident", [P, P])
        identb = keep("identb", [P, P], BF16)
        ones_f1 = keep("ones_f1", [P, 1])
        beforef = keep("beforef", [P, P])
        ones_row = keep("ones_row", [P, P], BF16)
        before = keep("before", [P, P], BF16)
        rows_f = keep("rows_f", [P, NJ + E + 2])
        WT = keep("WT", [P, NC, C])
        LG = keep("LG", [P, NT, E])
        UPD = keep("UPD", [P, NSC, E])
        DSTI = keep("DSTI", [P, NSC], I32)
        DP = keep("DP", [P, NC * E * C])
        DPv = DP[:].rearrange("p (c e r) -> p c e r", c=NC, e=E)
        idx_row = DP[:, 0:NS].bitcast(I32)
        EQ = DP[:, NS:2 * NS]
        at_sb = DP[0:A, 2 * NS:3 * NS]
        imp_sb = DP[0:E, 3 * NS:4 * NS]
        SIG = DP[:, 3 * NS:3 * NS + NSC * E]

        pair = [psum(f"pair{k}", [P, 2, 512]) for k in range(2)]
        work = [psum(f"work{k}", [P, 512]) for k in range(2)]
        O = psum("O", [P, 2, 512])

        attn = ExitStack()

        def sb(name, shape, dt=F32):
            return attn.enter_context(nc.sbuf_tensor(name, shape, dt))

        maskN = sb("maskN", [P, P], BF16)
        maskT = sb("maskT", [P, P], BF16)
        WX = sb("WX", [P, NC, WCOLS])
        WO = sb("WO", [P, NC, C])
        rope = sb("rope", [P, 2, NI, DH])
        dirs = sb("dirs", [P, 2, H, 3])
        onehot = sb("onehot", [P, H])
        hs = sb("hs", [P, 2, H])
        eaw = sb("eaw", [E, A])
        est = sb("est", [E, 4])
        awT = sb("awT", [A, E])
        idx_col = sb("idx_col", [P, NSC], I32)
        ibits = sb("ibits", [P, 2, NSC], I32)
        fcol = sb("fcol", [P, 4, NSC])
        gw = sb("gw", [E, C])
        X = [sb(f"X{k}", [P, C]) for k in range(2)]
        XN = [sb(f"XN{k}", [P, C]) for k in range(2)]
        XT = [sb(f"XT{k}", [P, NC, P]) for k in range(2)]
        bst = sb("bst", [P, 6])
        mv = [sb(f"mv{k}", [P, 2]) for k in range(2)]
        veps = [sb(f"veps{k}", [P, 1]) for k in range(2)]
        rstd = [sb(f"rstd{k}", [P, 1]) for k in range(2)]
        mhalf = sb("mhalf", [P, 1])
        rt1 = sb("rt1", [P, H + KVH, DH])
        rt2 = sb("rt2", [P, H + KVH, DH])
        at = [0]

        def carve(*shape):
            n = 1
            for m in shape:
                n *= m
            at[0] += n
            names = "abcd"[:len(shape)]
            return DP[:, at[0] - n:at[0]].rearrange(f"p ({' '.join(names)}) -> p {' '.join(names)}",
                                                    **dict(zip(names, shape)))

        QK = carve(NI, (H + KVH) * DH)
        QH = carve(NI, H, 2, DH)
        QL = carve(NI, H, QROWS)
        KHL = carve(NI, KVH, 2, DH)
        AO = carve(NI, C)
        V = sb("V", [P, NI, KVH, DH + 1])
        gt = [sb(f"gt{k}", [P, NI, H, 3]) for k in range(2)]
        TQ = sb("TQ", [P, NI, 72])
        TK = sb("TK", [P, NI, 72])
        QA = [sb(f"QA{k}", [P, T], F32R) for k in range(3)]
        KA = sb("KA", [P, KVH, T], F32R)
        KB = sb("KB", [QROWS, KVH, T], F32R)
        QB = [sb(f"QB{k}", [QROWS, T], F32R) for k in range(2)]
        KR = sb("KR", [GROWS, T])
        kpr = sb("kpr", [72, T])
        qpr = sb("qpr", [72, T])
        cmx = sb("cmx", [72, T])
        cmn = sb("cmn", [72, T])
        QG = sb("QG", [GROWS, T], F32R)
        KG = [sb(f"KG{k}", [GROWS, T], F32R) for k in range(2)]
        M = sb("M", [P, H, NI])
        PT = [sb(f"PT{k}", [P, 2, SOFF[NI]]) for k in range(2)]
        rl = sb("rl", [P, 2, NI])
        ab = sb("ab", [P, 2, NI])
        ow = sb("ow", [P, 2, NI, DH])
        AOT = [sb(f"AOT{k}", [P, NC, P]) for k in range(2)]
        SO = [sb(f"SO{k}", [P, C]) for k in range(2)]
        sci = [sb(f"sci{k}", [P, 1], I32) for k in range(2)]
        scv = [sb(f"scv{k}", [P, E]) for k in range(2)]
        attn.close()

        WF = PT[1][:].rearrange("p a n -> p (a n)")[:, 0:NC * C].rearrange("p (k c) -> p k c", k=NC)

        MX = keep("MX", [P, NT, E])
        IX = keep("IX", [P, NT, E], U32)
        gates = keep("gates", [P, 4, NT])
        OH = keep("OH", [P, TOPK, NT, E])
        CS = keep("CS", [P, NT, E], BF16)
        TOT = keep("TOT", [P, NT, E])
        INC = keep("INC", [P, NT, E])
        BASE = keep("BASE", [P, NT, E])
        ones_f = keep("ones_f", [P, NT])
        padc = keep("padc", [P, 4, E])
        padi = keep("padi", [P, E], I32)
        sel = keep("sel", [P, NT, E])
        posf = keep("posf", [P, TOPK, NT])
        posi = keep("posi", [P, TOPK, NT], I32)
        prow = keep("prow", [P, NT, TOPK, 2])
        cmpj = keep("cmpj", [P, NJ, E])
        ejf = keep("ejf", [P, NJ])
        eji = keep("eji", [P, NJ], I32)
        PL = keep("PL", [NJ, P, 2])
        TLI = keep("TLI", [P, NJ], I32)
        GL = keep("GL", [P, NJ])
        stage = [keep(f"stage{k}", [P, C, E]) for k in range(2)]
        GI = [keep(f"GI{k}", [P, 1], I32) for k in range(4)]
        GG = [keep(f"GG{k}", [P, 1]) for k in range(2)]
        XG = [keep(f"XG{k}", [P, C]) for k in range(4)]
        XGT = [keep(f"XGT{k}", [P, NC, P]) for k in range(2)]
        YG = [keep(f"YG{k}", [P, C]) for k in range(2)]
        FI = [[keep(f"FI{k}{m}", [P, 1], I32) for m in range(TOPK)] for k in range(2)]
        FY = [[keep(f"FY{k}{m}", [P, C]) for m in range(TOPK)] for k in range(2)]
        FX = [keep(f"FX{k}", [P, C]) for k in range(2)]
        FS = [keep(f"FS{k}", [P, C]) for k in range(2)]
        FO = [keep(f"FO{k}", [P, C]) for k in range(2)]

        consts_in = sem("consts_in")
        passed = sem("passed")
        weights_in = sem("weights_in")
        zero_made = sem("zero_made")
        zeroed = sem("zeroed")
        pre = {n: sem("pre_" + n) for n in ("pe", "act", "dve", "pool")}
        fills = sem("fills")
        x_in = [sem(f"x_in{k}") for k in range(2)]
        xn_out = [sem(f"xn_out{k}") for k in range(2)]
        so_out = [sem(f"so_out{k}") for k in range(2)]
        stats_made = sem("stats_made")
        bst_made = sem("bst_made")
        mv_made = sem("mv_made")
        rstd_made = sem("rstd_made")
        xn_made = sem("xn_made")
        work_full = [sem(f"work_full{k}") for k in range(2)]
        work_free = [sem(f"work_free{k}") for k in range(2)]
        pair_full = [sem(f"pair_full{k}") for k in range(2)]
        pair_free = [sem(f"pair_free{k}") for k in range(2)]
        rope_parts = sem("rope_parts")
        qk_made = sem("qk_made")
        v_made = sem("v_made")
        hi_made = sem("hi_made")
        lo_made = sem("lo_made")
        geo_a = sem("geo_a")
        geo_b = sem("geo_b")
        geo_cols = sem("geo_cols")
        cum_made = sem("cum_made")
        geo_max = sem("geo_max")
        kr_made = sem("kr_made")
        qg_made = sem("qg_made")
        kg_made = sem("kg_made")
        nmax_hi = sem("nmax_hi")
        nmax_made = sem("nmax_made")
        o_full = sem("o_full")
        o_free = sem("o_free")
        rl_made = sem("rl_made")
        ab_made = sem("ab_made")
        ao_made = sem("ao_made")
        sc_slot = sem("sc_slot")
        scattered = sem("scattered")
        routing = sem("routing")
        route_cs = sem("route_cs")
        route_pos = sem("route_pos")
        route_act = sem("route_act")
        route_pe = sem("route_pe")
        pairs_out = sem("pairs_out")
        pairs_in = sem("pairs_in")
        lists_made = sem("lists_made")
        stage_in = [sem(f"stage_in{k}") for k in range(2)]
        dp_made = sem("dp_made")
        gi_made = sem("gi_made")
        xg_in = [sem(f"xg_in{k}") for k in range(4)]
        xg_read = sem("xg_read")
        xgt_made = sem("xgt_made")
        gg_made = sem("gg_made")
        yg_made = sem("yg_made")
        y_full = sem("y_full")
        y_out = [sem(f"y_out{k}") for k in range(2)]
        fi_made = sem("fi_made")
        fy_in = [sem(f"fy_in{k}") for k in range(2)]
        fxs_in = [sem(f"fxs_in{k}") for k in range(2)]
        z_made = sem("z_made")
        g_made = sem("g_made")
        sg_made = sem("sg_made")
        fo_made = sem("fo_made")
        out_out = [sem(f"out_out{k}") for k in range(2)]

        block = ctx.enter_context(nc.Block())

        def work_wait(eng, sems, b, name):
            u = WORK_USE[name]
            eng.wait_ge(sems[u % 2], b * (NWORK // 2) + (u // 2 + 1))

        def pair_wait(eng, sems, b, name):
            u = PAIR_USE[name]
            eng.wait_ge(sems[u % 2], b * (NPAIR // 2) + (u // 2 + 1))

        def work_emptied(eng, b, name):
            u = WORK_USE[name]
            eng.wait_ge(work_free[u % 2], b * (NWORK // 2) + (u // 2 + 2))

        def pair_emptied(eng, b, name):
            u = PAIR_USE[name]
            eng.wait_ge(pair_free[u % 2], b * (NPAIR // 2) + (u // 2 + 2))

        def wbank(name):
            return work[WORK_USE[name] % 2]

        def pbank(name):
            return pair[PAIR_USE[name] % 2]

        DVE_SOFTMAX, DVE_VALUES, DVE_EARLIER, DVE_PLACES, PRE_DVE = 4, 8, 9, 18, 26
        ACT_SUM, ACT_AWT, ACT_SIG = 1, 2, 3
        PE_IMP, PE_AWT, PE_DELTA, PE_SUM, PE_COUNT, PE_GATE = 1, 2, 3, 4, 5, 6
        FILLS = 14
        LISTS = 3

        @block.sync
        def _(sp):
            for dst, src in ((ident[:], c_ident), (rows_f[:], c_rows),
                             (dirs[:], c_dirs.rearrange("p (a h d) -> p a h d", a=2, h=H)), (onehot[:], c_onehot),
                             (rope[:], c_rope.rearrange("p (a i d) -> p a i d", a=2, i=NI)),
                             (eaw[:], expert_atom_weights), (imp_sb, importance), (at_sb, atoms),
                             (hs[:, 1, :], head_scales.rearrange("(a h) -> a h", a=1).broadcast_to((P, H))),
                             (idx_row, mask_idx.rearrange("(a s) -> a s", a=1).broadcast_to((P, NS))),
                             ):
                sp.dma_start(dst, src).then_inc(consts_in, 16)
            with nc.allow_non_contiguous_dma(reason="4096 slot numbers, once"):
                sp.dma_start(idx_col[:], mask_idx.rearrange("(n p) -> p n", p=P)).then_inc(consts_in, 16)
            sp.dma_start(X[0][:], x_f[0:P, :]).then_inc(x_in[0], 16)
            sp.dma_start(X[1][:], x_f[P:2 * P, :]).then_inc(x_in[1], 16)
            for dst, src in ((gw[:], gate_w), (WF[:], ffn_W.rearrange("(k p) c -> p k c", p=P))):
                sp.dma_start(dst, src).then_inc(weights_in, 16)
            for dst, src in ((WX[:, :, 0:QC], Wq), (WX[:, :, QC:QC + KC], Wk),
                             (WX[:, :, QC + KC:QC + 2 * KC], Wv), (WO[:], Wo)):
                sp.dma_start(dst, src.rearrange("(k p) n -> p k n", p=P)).then_inc(weights_in, 16)
            sp.wait_ge(zero_made, 1)
            zsrc = PT[0][:].rearrange("p a n -> p (a n)")[:, 0:2048]
            for m in range(C * C * E // (P * 2048)):
                sp.dma_start(upd_d[m * 32768:(m + 1) * 32768, :].rearrange("(p n) e -> p (n e)", p=P),
                             zsrc).then_inc(zeroed, 16)
            sp.dma_start(pair_d.rearrange("(p n) e -> p (n e)", p=P), zsrc[:, 0:NJ * 2]).then_inc(zeroed, 16)

            with sp.Fori(0, B) as b:
                n1 = [sp.snap(b * NI + (i + 1)) for i in range(NI)]
                row = [sp.snap(b * T + i * P) for i in range(NI)]
                so = [sp.snap(b * (NPAIR // 2) + (PAIR_USE[("wo", i)] // 2 + 2)) for i in range(NI)]
                nxt = [sp.snap(((b * NI + (i + 2)) & (NT - 1)) * P) for i in range(NI)]
                for i in range(NI):
                    sp.wait_ge(xn_made, n1[i])
                    sp.dma_start(xn_d[bass.ds(row[i], P), :], XN[i % 2][:]).then_inc(xn_out[i % 2], 16)
                    sp.dma_start(X[i % 2][:], x_f[bass.ds(nxt[i], P), :]).then_inc(x_in[i % 2], 16)
                for i in range(NI):
                    sp.wait_ge(pair_free[PAIR_USE[("wo", i)] % 2], so[i])
                    sp.dma_start(s_d[bass.ds(row[i], P), :], SO[i % 2][:]).then_inc(so_out[i % 2], 16)

            for k in range(2):
                sp.wait_ge(xn_out[k], 16 * (NT // 2 + 1))
                sp.wait_ge(so_out[k], 16 * (NT // 2 + 1))
                sp.wait_ge(x_in[k], 16 * (NT // 2 + 1))
            sp.wait_ge(scattered, 16 * NSC)
            for k in range(2):
                sp.wait_ge(pair_free[k], B * (NPAIR // 2) + 1)
            for c in range(NC):
                if c >= 2:
                    sp.wait_ge(dp_made, c - 1)
                sp.dma_start(stage[c % 2][:], upd_d[c * P * C:(c + 1) * P * C, :]
                             .rearrange("(p r) e -> p r e", p=P)).then_inc(stage_in[c % 2], 16)
            sp.wait_ge(pairs_out, 16 * TOPK * NT)
            sp.dma_start(PL[:], pair_d.rearrange("(j p) e -> j p e", p=P)).then_inc(pairs_in, 16)

            with sp.Fori(0, NJ // 2) as q:
                made = [sp.snap(q * 2 + (k + 3)) for k in range(2)]
                row = [sp.snap(q * (2 * P) + k * P) for k in range(2)]
                for k in range(2):
                    sp.wait_ge(yg_made, made[k])
                    sp.dma_start(y_d[bass.ds(row[k], P), :], YG[k][:]).then_inc(y_out[k], 16)

            for k in range(2):
                sp.dma_start(FX[k][:], x_f[k * P:(k + 1) * P, :]).then_inc(fxs_in[k], 16)
                sp.dma_start(FS[k][:], s_d[k * P:(k + 1) * P, :]).then_inc(fxs_in[k], 16)
            with sp.Fori(1, NT // 2) as q:
                made = [sp.snap(q * 2 + (k - 1)) for k in range(2)]
                row = [sp.snap(q * (2 * P) + k * P) for k in range(2)]
                done = [sp.snap(q * (2 * P) + (k - 2) * P) for k in range(2)]
                for k in range(2):
                    sp.wait_ge(fo_made, made[k])
                    sp.dma_start(out_f[bass.ds(done[k], P), :], FO[k][:]).then_inc(out_out[k], 16)
                    sp.dma_start(FX[k][:], x_f[bass.ds(row[k], P), :]).then_inc(fxs_in[k], 16)
                    sp.dma_start(FS[k][:], s_d[bass.ds(row[k], P), :]).then_inc(fxs_in[k], 16)
            for k in range(2):
                n = NT - 2 + k
                sp.wait_ge(fo_made, n + 1)
                sp.dma_start(out_f[n * P:(n + 1) * P, :], FO[k][:]).then_inc(out_out[k], 16)
            for k in range(2):
                sp.wait_ge(out_out[k], 16 * (NT // 2 + 1))

        @block.gpsimd
        def _(pool):
            def low_parts(b, i):
                pool.wait_ge(hi_made, b * NI + (i + 1))
                pool.tensor_tensor(QL[:, i, :, 0:DH], QK[:, i, 0:QC].rearrange("p (h d) -> p h d", h=H),
                                   QH[:, i, :, 0, :],
                                   op=ALU.subtract).then_inc(lo_made, 1)
                pool.tensor_tensor(KHL[:, i, :, 1, :], QK[:, i, QC:].rearrange("p (v d) -> p v d", v=KVH),
                                   KHL[:, i, :, 0, :], op=ALU.subtract).then_inc(lo_made, 1)

            pool.memset(PT[0][:], 0.0).then_inc(zero_made, 1)
            for m in (maskN, maskT):
                pool.memset(m[:], 0.0).then_inc(pre["pool"], 1)
            for m in (beforef, before):
                pool.memset(m[:], 1.0).then_inc(pre["pool"], 1)
            pool.memset(KR[:], 0.0).then_inc(pre["pool"], 1)
            pool.wait_ge(pre["pool"], 5)
            pool.affine_select(out=maskN[:], in_=maskN[:], compare_op=ALU.is_ge, fill=NEG, base=0,
                               pattern=[[-1, P]], channel_multiplier=1).then_inc(fills, 1)
            pool.affine_select(out=maskT[:], in_=maskT[:], compare_op=ALU.is_ge, fill=NEG, base=0,
                               pattern=[[1, P]], channel_multiplier=-1).then_inc(fills, 1)
            for m in (beforef, before):
                pool.affine_select(out=m[:], in_=m[:], compare_op=ALU.is_gt, fill=0.0, base=0,
                                   pattern=[[1, P]], channel_multiplier=-1).then_inc(fills, 1)
            for n, (dst, value) in enumerate(((KR[64:72, :], 1.0), (KR[96:104, :], 1.0), (ones_row[:], 1.0), (ones_f1[:], 1.0),
                               (mhalf[:], -0.5), (TQ[:], 0.0), (TK[:], 0.0), (QG[:].bitcast(F32), 0.0),
                               (V[:, :, :, DH:DH + 1], 1.0), (KB[DH:QROWS, :, :].bitcast(F32), 1.0))):
                pool.wait_ge(fills, 4 + n)
                pool.memset(dst, value).then_inc(fills, 1)
            pool.wait_ge(fills, FILLS)
            pool.sem_inc(z_made, 2)
            pool.sem_inc(xg_read, 4)

            with pool.Fori(0, B) as b:
                for i in range(NI):
                    pool.wait_ge(stats_made, b * NI + (i + 1))
                    pool.tensor_tensor(rstd[i % 2][:], veps[i % 2][:], mhalf[:], op=ALU.pow).then_inc(rstd_made, 1)
                    if i >= 1:
                        low_parts(b, i - 1)
                low_parts(b, NI - 1)
                pool.wait_ge(zeroed, 16 * 9)
                pool.wait_ge(pre["dve"], DVE_PLACES)
                for i in range(NI):
                    n = b * NI + i
                    pool.tensor_copy(sci[i % 2][:], DSTI[:, bass.ds(n, 1)]).then_inc(sc_slot, 1)
                    pool.tensor_copy(scv[i % 2][:], UPD[:, bass.ds(n, 1), :].rearrange("p a e -> p (a e)")) \
                        .then_inc(sc_slot, 1)
                    pool.wait_ge(sc_slot, b * (2 * NI) + 2 * (i + 1))
                    pool.sem_inc(passed, 1)
                    pool.indirect_dma_start(
                        out=upd_d, out_offset=bass.IndirectOffsetOnAxis(ap=sci[i % 2][:, 0:1], axis=0),
                        in_=scv[i % 2][:], in_offset=None, compute_op=ALU.add).then_inc(scattered, 16)
                    pool.wait_ge(scattered, b * (NI * 16) + 16 * (i + 1))

            pool.wait_ge(route_pos, 2)
            for g in range(NT):
                for m in range(TOPK):
                    pool.indirect_dma_start(
                        out=pair_d, out_offset=bass.IndirectOffsetOnAxis(ap=posi[:, m, g:g + 1], axis=0),
                        in_=prow[:, g, m, :], in_offset=None).then_inc(pairs_out, 16)
            pool.wait_ge(lists_made, LISTS)
            with pool.Fori(0, NJ // 4) as q:
                for k in range(4):
                    pool.wait_ge(xg_read, q * 4 + (k + 1))
                    pool.tensor_copy(GI[k][:], TLI[:, bass.ds(q * 4 + k, 1)]).then_inc(gi_made, 1)
                    pool.wait_ge(gi_made, q * 4 + (k + 1))
                    pool.sem_inc(passed, 1)
                    pool.indirect_dma_start(
                        out=XG[k][:], out_offset=None, in_=xn_d,
                        in_offset=bass.IndirectOffsetOnAxis(ap=GI[k][:, 0:1], axis=0)).then_inc(xg_in[k], 16)
            for k in range(2):
                pool.wait_ge(y_out[k], 16 * (NJ // 2 + 1))
            with pool.Fori(0, NT // 2) as q:
                for k in range(2):
                    pool.wait_ge(z_made, q * 2 + (k + 1))
                    for m in range(TOPK):
                        pool.tensor_copy(FI[k][m][:], posi[:, m, bass.ds(q * 2 + k, 1)]).then_inc(fi_made, 1)
                    pool.wait_ge(fi_made, q * 4 + 2 * (k + 1))
                    pool.sem_inc(passed, 1)
                    for m in range(TOPK):
                        pool.indirect_dma_start(
                            out=FY[k][m][:], out_offset=None, in_=y_d,
                            in_offset=bass.IndirectOffsetOnAxis(ap=FI[k][m][:, 0:1], axis=0)).then_inc(fy_in[k], 16)

        @block.tensor
        def _(pe):
            def tr(dst, src, rows=P):
                return pe.transpose(dst, src, ident[0:rows, 0:rows])

            pe.wait_ge(consts_in, 16 * 11)
            for n in range(NSC):
                last = tr(O[:, 0, n * E:(n + 1) * E], imp_sb[:, n * P:(n + 1) * P], E)
            last.then_inc(pre["pe"], 1)
            pe.wait_ge(pre["dve"], DVE_SOFTMAX)
            tr(work[0][0:A, 0:E], eaw[:], E).then_inc(pre["pe"], 1)
            pe.wait_ge(pre["act"], ACT_AWT)
            for n in range(NSC):
                last = pe.matmul(O[:, 1, n * E:(n + 1) * E], at_sb[:, n * P:(n + 1) * P], awT[:],
                                 start=True, stop=True)
            last.then_inc(pre["pe"], 1)
            pe.wait_ge(pre["dve"], DVE_VALUES)
            for n in range(NSC):
                last = pe.matmul(pair[0][:, 0, n * E:(n + 1) * E], EQ[:, n * P:(n + 1) * P], UPD[:, n, :],
                                 start=True, stop=True)
            last.then_inc(pre["pe"], 1)
            pe.wait_ge(pre["dve"], DVE_EARLIER)
            pe.wait_ge(fills, FILLS)
            for n in range(NSC):
                last = pe.matmul(work[1][:, n:n + 1], EQ[:, n * P:(n + 1) * P], ones_f1[:], start=True, stop=True)
            last.then_inc(pre["pe"], 1)
            pe.wait_ge(weights_in, 16 * 6)
            for k in range(NC):
                last = tr(work[0][:, k * E:(k + 1) * E], gw[:, k * P:(k + 1) * P], E)
            last.then_inc(pre["pe"], 1)
            for k in range(NC):
                dst = (pair[1][:, 0, :], pair[1][:, 1, :], O[:, 0, :], pair[0][:, 1, :])[k]
                for r in range(NC):
                    last = tr(dst[:, r * P:(r + 1) * P], WF[:, r, k * P:(k + 1) * P])
                last.then_inc(pre["pe"], 1)
            pe.wait_ge(pre["dve"], PRE_DVE)

            with pe.Fori(0, B) as b:
                def transpose_x(i):
                    name = ("xt", i)
                    pe.wait_ge(xn_made, b * NI + (i + 1))
                    work_wait(pe, work_free, b, name)
                    for c in range(NC):
                        last = tr(wbank(name)[:, c * P:(c + 1) * P], XN[i % 2][:, c * P:(c + 1) * P])
                    last.then_inc(work_full[WORK_USE[name] % 2], 1)

                def project(i):
                    name = ("p", i)
                    work_emptied(pe, b, ("xt", i))
                    pair_wait(pe, pair_free, b, name)
                    dst = pbank(name)
                    for c in range(NC):
                        pe.matmul(dst[:, 0, :], XT[i % 2][:, c, :], WX[:, c, 0:512],
                                  start=c == 0, stop=c == NC - 1)
                    for c in range(NC):
                        last = pe.matmul(dst[:, 1, 0:WCOLS - 512], XT[i % 2][:, c, :], WX[:, c, 512:WCOLS],
                                         start=c == 0, stop=c == NC - 1)
                    last.then_inc(pair_full[PAIR_USE[name] % 2], 1)

                def to_rows(name, cols, rows):
                    work_wait(pe, work_free, b, name)
                    for i in range(NI):
                        last = tr(wbank(name)[0:rows, i * P:(i + 1) * P], cols(i))
                    last.then_inc(work_full[WORK_USE[name] % 2], 1)

                def q_rows(h):
                    to_rows(("qa", h), lambda i: QH[:, i, h, :, :].rearrange("p a d -> p (a d)"), P)

                def first_scores(h, i):
                    name = ("qm", h, i)
                    n = P * (i + 1)
                    if i == 0:
                        work_emptied(pe, b, ("qa", h))
                        if h == 0:
                            for v in range(KVH):
                                work_emptied(pe, b, ("kt", v))
                    work_wait(pe, work_free, b, name)
                    pe.matmul(wbank(name)[:, 0:n], QA[h % 3][:, i * P:(i + 1) * P], KA[:, h // REP, 0:n],
                              start=True, stop=False)
                    pe.matmul(wbank(name)[:, n - P:n], identb[:], maskN[:], start=False, stop=True) \
                        .then_inc(work_full[WORK_USE[name] % 2], 1)

                def rest_rows(h):
                    if h == 0:
                        pe.wait_ge(lo_made, b * (2 * NI) + 2 * NI)
                    pe.wait_ge(nmax_made, b * H + (h + 1))
                    to_rows(("qb", h), lambda i: QL[:, i, h, :], QROWS)

                def scores(h, j):
                    name = ("s", h, j)
                    n = T - P * j
                    v = h // REP
                    if j == 0:
                        work_emptied(pe, b, ("qb", h))
                        pe.wait_ge(kg_made, b * H + (h + 1))
                        if h == 0:
                            pe.wait_ge(qg_made, b * 3 + 3)
                    pair_wait(pe, pair_free, b, name)
                    dst = pbank(name)
                    st = slice(j * P, (j + 1) * P)
                    pe.matmul(dst[:, 0, 0:n], KA[:, v, st], QA[h % 3][:, j * P:T], start=True, stop=False)
                    pe.matmul(dst[:, 0, 0:n], KB[:, v, st], QB[h % 2][:, j * P:T], start=False, stop=False)
                    pe.matmul(dst[:, 0, 0:P], identb[:], maskT[:], start=False, stop=True)
                    pe.matmul(dst[:, 1, 0:n], KG[h % 2][:, st], QG[:, j * P:T], start=True, stop=False)
                    pe.matmul(dst[:, 1, 0:P], identb[:], maskT[:], start=False, stop=True) \
                        .then_inc(pair_full[PAIR_USE[name] % 2], 1)

                def values(h, i):
                    if i == 0:
                        pe.wait_ge(o_free, b * H + (h + 1))
                    pair_emptied(pe, b, ("s", h, i))
                    for m in range(2):
                        for j in range(i + 1):
                            o = SOFF[j] + P * (i - j)
                            last = pe.matmul(O[:, m, i * (DH + 1):(i + 1) * (DH + 1)],
                                             PT[h % 2][:, m, o:o + P], V[:, j, h // REP, :],
                                             start=j == 0, stop=j == i)
                    if i == NI - 1:
                        last.then_inc(o_full, 1)

                def transpose_out(i):
                    name = ("at", i)
                    if i == 0:
                        pe.wait_ge(ao_made, b * H + H)
                    work_wait(pe, work_free, b, name)
                    for c in range(NC):
                        last = tr(wbank(name)[:, c * P:(c + 1) * P], AO[:, i, c * P:(c + 1) * P])
                    last.then_inc(work_full[WORK_USE[name] % 2], 1)

                def project_out(i):
                    name = ("wo", i)
                    work_emptied(pe, b, ("at", i))
                    pair_wait(pe, pair_free, b, name)
                    for c in range(NC):
                        last = pe.matmul(pbank(name)[:, 0, :], AOT[i % 2][:, c, :], WO[:, c, :],
                                         start=c == 0, stop=c == NC - 1)
                    last.then_inc(pair_full[PAIR_USE[name] % 2], 1)

                transpose_x(0)
                transpose_x(1)
                project(0)
                transpose_x(2)
                project(1)
                transpose_x(3)
                project(2)
                project(3)
                pe.wait_ge(lo_made, b * (2 * NI) + 2 * NI)
                for v in range(KVH):
                    to_rows(("kt", v), lambda i: KHL[:, i, v, :, :].rearrange("p a d -> p (a d)"), P)
                pe.wait_ge(geo_cols, b * 2 + 2)
                to_rows(("tk",), lambda i: TK[:, i, :], 72)
                to_rows(("tq",), lambda i: TQ[:, i, :], 72)
                for h in range(2):
                    q_rows(h)
                    for i in range(NI):
                        first_scores(h, i)
                rest_rows(0)
                scores(0, 0)
                scores(0, 1)
                for h in range(H):
                    more, most = h + 1 < H, h + 2 < H
                    if more:
                        rest_rows(h + 1)
                    values(h, 0)
                    scores(h, 2)
                    if most:
                        q_rows(h + 2)
                    values(h, 1)
                    scores(h, 3)
                    if most:
                        first_scores(h + 2, 0)
                        first_scores(h + 2, 1)
                    values(h, 2)
                    if more:
                        scores(h + 1, 0)
                    if most:
                        first_scores(h + 2, 2)
                        first_scores(h + 2, 3)
                    values(h, 3)
                    if more:
                        scores(h + 1, 1)
                transpose_out(0)
                transpose_out(1)
                project_out(0)
                transpose_out(2)
                project_out(1)
                transpose_out(3)
                project_out(2)
                project_out(3)

            pe.wait_ge(route_cs, 1)
            cs = CS[:].rearrange("p g e -> p (g e)")
            pe.matmul(pair[0][:, 0, 0:NT * E], before[:], cs, start=True, stop=True).then_inc(route_pe, 1)
            pe.matmul(pair[0][:, 1, 0:NT * E], ones_row[:], cs, start=True, stop=True).then_inc(route_pe, 1)
            pe.wait_ge(pairs_in, 16)
            tr(work[0][:, 0:NJ], PL[:, :, 0], NJ)
            tr(work[0][:, 128:128 + NJ], PL[:, :, 1], NJ).then_inc(route_pe, 1)
            pe.wait_ge(lists_made, LISTS)
            pe.wait_ge(dp_made, NC)

            def gathered(q, k):
                pe.wait_ge(xg_in[k], q * 16 + 16)
                pe.wait_ge(xgt_made, q * 4 + (k + 1))
                for c in range(NC):
                    last = tr(work[k % 2][:, c * P:(c + 1) * P], XG[k][:, c * P:(c + 1) * P])
                last.then_inc(xg_read, 1)

            def expert(q, k):
                e = pe.value_load(eji[0:1, bass.ds(q * 4 + k, 1)], min_val=0, max_val=E - 1)
                pe.wait_ge(xgt_made, q * 4 + (k + 3))
                pe.wait_ge(yg_made, q * 4 + (k + 1))
                for c in range(NC):
                    last = pe.matmul(pair[k % 2][:, 0, :], XGT[k % 2][:, c, :],
                                     DPv[:, c, bass.ds(e, 1), :].rearrange("p a r -> p (a r)"),
                                     start=c == 0, stop=c == NC - 1)
                last.then_inc(y_full, 1)

            with pe.Fori(0, NJ // 4) as q:
                gathered(q, 0)
                gathered(q, 1)
                expert(q, 0)
                gathered(q, 2)
                expert(q, 1)
                gathered(q, 3)
                expert(q, 2)
                expert(q, 3)

        @block.scalar
        def _(act):
            act.sem_inc(xgt_made, 2)
            act.wait_ge(pre["dve"], 2)
            act.activation(eaw[:], eaw[:], ACT.Exp, bias=est[:, 1:2], accum_out=est[:, 2:3]).then_inc(pre["act"], 1)
            act.wait_ge(pre["pe"], PE_AWT)
            act.activation(awT[:], work[0][0:A, 0:E], ACT.Copy).then_inc(pre["act"], 1)
            act.activation(SIG, O[:, 0, 0:NSC * E], ACT.Exp, scale=-1.0).then_inc(pre["act"], 1)

            with act.Fori(0, B) as b:
                def x_columns(i):
                    name = ("xt", i)
                    work_wait(act, work_full, b, name)
                    act.activation(XT[i % 2][:].rearrange("p c t -> p (c t)"), wbank(name)[:], ACT.Copy) \
                        .then_inc(work_free[WORK_USE[name] % 2], 1)

                def leading(i):
                    act.wait_ge(qk_made, b * NI + (i + 2))
                    act.activation(QH[:, i, :, :, :].bitcast(F32R),
                                   QK[:, i, 0:QC].rearrange("p (h d) -> p h d", h=H).unsqueeze(2)
                                   .broadcast_to((P, H, 2, DH)), ACT.Copy)
                    act.activation(KHL[:, i, :, 0, :].bitcast(F32R),
                                   QK[:, i, QC:].rearrange("p (v d) -> p v d", v=KVH), ACT.Copy).then_inc(hi_made, 1)

                def rows(name, dst, n):
                    work_wait(act, work_full, b, name)
                    act.activation(dst, wbank(name)[0:n, :], ACT.Copy) \
                        .then_inc(work_free[WORK_USE[name] % 2], 1)

                def exps(h, j):
                    name = ("s", h, j)
                    n = T - P * j
                    pair_wait(act, pair_full, b, name)
                    act.activation(PT[h % 2][:, :, SOFF[j]:SOFF[j] + n], pbank(name)[:, :, 0:n], ACT.Exp) \
                        .then_inc(pair_free[PAIR_USE[name] % 2], 1)

                x_columns(0)
                x_columns(1)
                leading(0)
                x_columns(2)
                leading(1)
                x_columns(3)
                leading(2)
                leading(3)
                for v in range(KVH):
                    name = ("kt", v)
                    work_wait(act, work_full, b, name)
                    act.activation(KA[:, v, :], wbank(name)[:], ACT.Copy)
                    act.activation(KB[0:DH, v, :], wbank(name)[0:DH, :], ACT.Copy) \
                        .then_inc(work_free[WORK_USE[name] % 2], 1)
                rows(("qa", 0), QA[0][:], P)
                rows(("qa", 1), QA[1][:], P)
                rows(("qb", 0), QB[0][:], QROWS)
                act.wait_ge(zeroed, 16 * 9)
                for h in range(H):
                    exps(h, 0)
                    exps(h, 1)
                    if h + 1 < H:
                        rows(("qb", h + 1), QB[(h + 1) % 2][:], QROWS)
                    exps(h, 2)
                    if h + 2 < H:
                        rows(("qa", h + 2), QA[(h + 2) % 3][:], P)
                    exps(h, 3)
                for i in range(NI):
                    name = ("at", i)
                    work_wait(act, work_full, b, name)
                    act.activation(AOT[i % 2][:].rearrange("p c t -> p (c t)"), wbank(name)[:], ACT.Copy) \
                        .then_inc(work_free[WORK_USE[name] % 2], 1)

            act.wait_ge(route_act, 1)
            act.activation(gates[:, 0, :], gates[:, 1, :], ACT.Exp).then_inc(route_act, 1)
            act.wait_ge(lists_made, LISTS)
            with act.Fori(0, NJ // 4) as q:
                for k in range(4):
                    act.wait_ge(xg_read, q * 4 + (k + 5))
                    act.activation(XGT[k % 2][:].rearrange("p c t -> p (c t)"), work[k % 2][:], ACT.Copy) \
                        .then_inc(xgt_made, 1)
            with act.Fori(0, NT // 2) as q:
                for k in range(2):
                    act.wait_ge(z_made, q * 2 + (k + 3))
                    act.activation(FO[k][:], FO[k][:], ACT.Silu).then_inc(g_made, 1)

        @block.vector
        def _(dve):
            for s_, n in ((work_free[0], 1), (work_free[1], 1), (pair_free[0], 1), (pair_free[1], 1), (o_free, 1), (qk_made, 1),
                          (xn_out[0], 16), (xn_out[1], 16), (so_out[0], 16), (so_out[1], 16),
                          (yg_made, 2), (y_out[0], 16), (y_out[1], 16), (out_out[0], 16), (out_out[1], 16)):
                dve.sem_inc(s_, n)
            count = [0]

            def step(ins):
                count[0] += 1
                ins.then_inc(pre["dve"], 1)
                dve.wait_ge(pre["dve"], count[0])

            dve.wait_ge(consts_in, 16 * 11)
            step(dve.reduce_max(est[:, 0:1], eaw[:], AX))
            step(dve.tensor_scalar(est[:, 1:2], est[:, 0:1], -1.0, None, ALU.mult))
            dve.wait_ge(pre["act"], ACT_SUM)
            step(dve.reciprocal(est[:, 3:4], est[:, 2:3]))
            step(dve.tensor_scalar(eaw[:], eaw[:], est[:, 3:4], None, ALU.mult))
            step(dve.tensor_tensor(EQ.rearrange("p (n s) -> p n s", n=NSC),
                                   idx_row.rearrange("p (n s) -> p n s", n=NSC),
                                   idx_col[:].unsqueeze(2).broadcast_to((P, NSC, P)), op=ALU.is_equal))
            dve.wait_ge(pre["act"], ACT_SIG)
            step(dve.tensor_scalar(SIG, SIG, 1.0, None, ALU.add))
            step(dve.reciprocal(SIG, SIG))
            dve.wait_ge(pre["pe"], PE_DELTA)
            step(dve.tensor_tensor(UPD[:].rearrange("p n e -> p (n e)"), O[:, 1, 0:NSC * E], SIG, op=ALU.mult))
            assert count[0] == DVE_VALUES
            dve.wait_ge(pre["pe"], PE_SUM)
            dve.wait_ge(fills, FILLS)
            step(dve.tensor_tensor(EQ.rearrange("p (n s) -> p n s", n=NSC), EQ.rearrange("p (n s) -> p n s", n=NSC),
                                   beforef[:].unsqueeze(1).broadcast_to((P, NSC, P)), op=ALU.mult))
            step(dve.tensor_copy(UPD[:].rearrange("p n e -> p (n e)"), pair[0][:, 0, 0:NSC * E]))
            step(dve.tensor_scalar(ibits[:, 0, :], idx_col[:], C - 1, C.bit_length() - 1,
                                   ALU.bitwise_and, ALU.logical_shift_left))
            step(dve.tensor_scalar(ibits[:, 1, :], idx_col[:], C.bit_length() - 1, None, ALU.logical_shift_right))
            step(dve.tensor_tensor(fcol[:, 0, :], ibits[:, 0, :], ibits[:, 1, :], op=ALU.add))
            dve.wait_ge(pre["pe"], PE_COUNT)
            step(dve.tensor_scalar(fcol[:, 1, :], work[1][:, 0:NSC], 1.0, None, ALU.min))
            step(dve.tensor_scalar(fcol[:, 2, :], fcol[:, 0, :], -1.0, rows_f[:, NJ + E + 1:NJ + E + 2],
                                   ALU.mult, ALU.add))
            step(dve.tensor_tensor(fcol[:, 2, :], fcol[:, 2, :], fcol[:, 1, :], op=ALU.mult))
            step(dve.tensor_tensor(fcol[:, 0, :], fcol[:, 0, :], fcol[:, 2, :], op=ALU.add))
            step(dve.tensor_copy(DSTI[:], fcol[:, 0, :]))
            assert count[0] == DVE_PLACES
            dve.wait_ge(weights_in, 16 * 6)
            step(dve.tensor_scalar(WX[:, :, 0:QC], WX[:, :, 0:QC], DH ** -0.5, None, ALU.mult))
            dve.wait_ge(pre["pe"], PE_GATE)
            step(dve.tensor_copy(WX[:, :, WCOLS - E:WCOLS], work[0][:, 0:NC * E].rearrange("p (k e) -> p k e", k=NC)))
            for k in range(NC):
                src = (pair[1][:, 0, :], pair[1][:, 1, :], O[:, 0, :], pair[0][:, 1, :])[k]
                dve.wait_ge(pre["pe"], PE_GATE + k + 1)
                step(dve.tensor_copy(WT[:, k, :], src))
            step(dve.tensor_scalar(hs[:, 0, :], hs[:, 1, :], -1.0, 1.0, ALU.mult, ALU.add))
            step(dve.tensor_copy(identb[:], ident[:]))
            assert count[0] == PRE_DVE

            def stats(slot, arrived, n):
                dve.wait_ge(x_in[slot], arrived)
                dve.bn_stats(bst[:], X[slot][:]).then_inc(bst_made, 1)
                dve.wait_ge(bst_made, n)
                dve.sem_inc(passed, 1)
                dve.bn_aggr(mv[slot][:], bst[:]).then_inc(mv_made, 1)
                dve.wait_ge(mv_made, n)
                dve.tensor_scalar(veps[slot][:], mv[slot][:, 1:2], EPS, None, ALU.add).then_inc(stats_made, 1)

            stats(0, 16, 1)
            with dve.Fori(0, B) as b:
                def normalise(i):
                    dve.wait_ge(rstd_made, b * NI + (i + 1))
                    dve.wait_ge(xn_out[i % 2], b * (8 * NI) + 16 * (i // 2 + 1))
                    dve.tensor_scalar(XN[i % 2][:], X[i % 2][:], mv[i % 2][:, 0:1], rstd[i % 2][:, 0:1],
                                      ALU.subtract, ALU.mult).then_inc(xn_made, 1)

                def rotate(i):
                    name = ("p", i)
                    pair_wait(dve, pair_full, b, name)
                    flat = pbank(name)[:].rearrange("p a n -> p (a n)")
                    qk = flat[:, 0:QC + KC].rearrange("p (h d) -> p h d", d=DH)

                    def table(a, lo, hi):
                        return rope[:, a, i, lo:hi].unsqueeze(1).broadcast_to((P, H + KVH, hi - lo))

                    dve.wait_ge(qk_made, b * NI + (i + 1))
                    dve.tensor_tensor(rt1[:], qk, table(0, 0, DH), op=ALU.mult).then_inc(rope_parts, 1)
                    dve.tensor_tensor(rt2[:, :, 0:HALF], qk[:, :, HALF:DH], table(1, 0, HALF),
                                      op=ALU.mult).then_inc(rope_parts, 1)
                    dve.tensor_tensor(rt2[:, :, HALF:DH], qk[:, :, 0:HALF], table(1, HALF, DH),
                                      op=ALU.mult).then_inc(rope_parts, 1)
                    dve.tensor_copy(V[:, i, :, 0:DH],
                                    flat[:, QC + KC:QC + 2 * KC].rearrange("p (v d) -> p v d", v=KVH)).then_inc(v_made, 1)
                    dve.tensor_scalar(LG[:, bass.ds(b * NI + i, 1), :].rearrange("p a e -> p (a e)"),
                                      flat[:, WCOLS - E:WCOLS], 50.0, -50.0, ALU.min, ALU.max) \
                        .then_inc(pair_free[PAIR_USE[name] % 2], 1)
                    dve.wait_ge(rope_parts, b * (3 * NI) + 3 * (i + 1))
                    dve.tensor_tensor(QK[:, i, :].rearrange("p (h d) -> p h d", d=DH), rt1[:], rt2[:],
                                      op=ALU.add).then_inc(qk_made, 1)

                for i in range(NI):
                    normalise(i)
                    nxt = i + 1
                    dve.wait_ge(xn_made, b * NI + (i + 1))
                    dve.wait_ge(stats_made, b * NI + (i + 1))
                    stats(nxt % 2, b * (8 * NI) + 16 * (nxt // 2 + 1), b * NI + (nxt + 1))
                    if i >= 1:
                        rotate(i - 1)
                rotate(NI - 1)

                dve.wait_ge(qk_made, b * NI + NI + 1)
                GA = 9
                q3 = QK[:, :, 0:QC].rearrange("p i (h d) -> p i h d", d=DH)[:, :, :, 0:3]
                dve.tensor_tensor(gt[0][:], q3, dirs[:, 1, :, :].unsqueeze(1).broadcast_to((P, NI, H, 3)),
                                  op=ALU.mult).then_inc(geo_a, 1)
                for v in range(KVH):
                    k3 = QK[:, :, QC + v * DH:QC + v * DH + 3].unsqueeze(2).broadcast_to((P, NI, REP, 3))
                    dve.tensor_tensor(gt[1][:, :, v * REP:(v + 1) * REP, :], k3,
                                      dirs[:, 0, v * REP:(v + 1) * REP, :].unsqueeze(1)
                                      .broadcast_to((P, NI, REP, 3)), op=ALU.mult).then_inc(geo_a, 1)
                dve.wait_ge(geo_a, b * GA + 3)
                dve.reduce_sum(TQ[:, :, 64:72], gt[0][:], AX).then_inc(geo_a, 1)
                dve.reduce_sum(TK[:, :, 64:72], gt[1][:], AX).then_inc(geo_a, 1)
                dve.wait_ge(geo_a, b * GA + 5)
                for t, two in ((TQ, 8), (TK, 16)):
                    dve.tensor_copy(t[:, :, 0:8].bitcast(F32R), t[:, :, 64:72]).then_inc(geo_a, 1)
                    dve.tensor_copy(t[:, :, two:two + 8].bitcast(F32R), t[:, :, 64:72]).then_inc(geo_a, 1)
                dve.wait_ge(geo_a, b * GA + 9)
                for t, rest in ((TQ, 16), (TK, 8)):
                    dve.tensor_tensor(t[:, :, rest:rest + 8], t[:, :, 64:72], t[:, :, 0:8],
                                      op=ALU.subtract).then_inc(geo_cols, 1)

                work_wait(dve, work_full, b, ("tk",))
                bank = wbank(("tk",))
                dve.tensor_copy(KR[0:24, :], bank[0:24, :]).then_inc(kr_made, 1)
                dve.tensor_copy(kpr[64:72, :], bank[64:72, :]) \
                    .then_inc(work_free[WORK_USE[("tk",)] % 2], 1)
                work_wait(dve, work_full, b, ("tq",))
                bank = wbank(("tq",))
                dve.tensor_copy(QG[0:24, :], bank[0:24, :]).then_inc(qg_made, 1)
                dve.tensor_copy(qpr[64:72, :], bank[64:72, :]) \
                    .then_inc(work_free[WORK_USE[("tq",)] % 2], 1)
                work_emptied(dve, b, ("tk",))
                work_emptied(dve, b, ("tq",))
                dve.tensor_tensor_scan(cmx[64:72, :], kpr[64:72, :], kpr[64:72, :], -3e38, ALU.max, ALU.max) \
                    .then_inc(cum_made, 1)
                dve.tensor_tensor_scan(cmn[64:72, :], kpr[64:72, :], kpr[64:72, :], 3e38, ALU.min, ALU.min) \
                    .then_inc(cum_made, 1)
                dve.wait_ge(cum_made, b * 2 + 2)
                dve.tensor_tensor(cmx[64:72, :], cmx[64:72, :], qpr[64:72, :], op=ALU.mult).then_inc(geo_b, 1)
                dve.tensor_tensor(cmn[64:72, :], cmn[64:72, :], qpr[64:72, :], op=ALU.mult).then_inc(geo_b, 1)
                dve.wait_ge(geo_b, b * 2 + 2)
                dve.tensor_tensor(cmx[64:72, :], cmx[64:72, :], cmn[64:72, :], op=ALU.max).then_inc(geo_max, 1)
                dve.wait_ge(geo_max, b + 1)
                dve.tensor_scalar(QG[64:72, :], cmx[64:72, :], -1.0, None, ALU.mult).then_inc(qg_made, 1)
                dve.wait_ge(qg_made, b * 3 + 2)
                dve.scalar_tensor_tensor(QG[96:104, :], cmx[64:72, :], -1.0, QG[64:72, :].bitcast(F32),
                                         ALU.mult, ALU.subtract).then_inc(qg_made, 1)
                dve.wait_ge(kr_made, b + 1)

                def geo_rows(h):
                    dve.tensor_scalar(KG[h % 2][:], KR[:], onehot[0:GROWS, h:h + 1], None, ALU.mult) \
                        .then_inc(kg_made, 1)

                def row_max(h, i):
                    name = ("qm", h, i)
                    work_wait(dve, work_full, b, name)
                    dve.reduce_max(M[:, h, i:i + 1], wbank(name)[:, 0:P * (i + 1)], AX) \
                        .then_inc(work_free[WORK_USE[name] % 2], 1)

                def minus_max(h):
                    if h == 0:
                        dve.wait_ge(lo_made, b * (2 * NI) + 2 * NI)
                    work_emptied(dve, b, ("qm", h, NI - 2))
                    work_emptied(dve, b, ("qm", h, NI - 1))
                    dve.tensor_scalar(QL[:, :, h, DH].bitcast(F32R), M[:, h, :], -1.0, None, ALU.mult) \
                        .then_inc(nmax_hi, 1)
                    dve.wait_ge(nmax_hi, b * H + (h + 1))
                    dve.scalar_tensor_tensor(QL[:, :, h, DH + 1], M[:, h, :], -1.0, QL[:, :, h, DH],
                                             ALU.mult, ALU.subtract).then_inc(nmax_made, 1)

                def mix(h):
                    dve.wait_ge(o_full, b * H + (h + 1))
                    oh = O[:, :, 0:NI * (DH + 1)].rearrange("p m (i d) -> p m i d", d=DH + 1)
                    dve.reciprocal(rl[:], oh[:, :, :, DH]).then_inc(rl_made, 1)
                    dve.wait_ge(rl_made, b * H + (h + 1))
                    dve.tensor_tensor(ab[:], rl[:], hs[:, :, h].unsqueeze(2).broadcast_to((P, 2, NI)),
                                      op=ALU.mult).then_inc(ab_made, 1)
                    dve.wait_ge(ab_made, b * H + (h + 1))
                    if h >= 1:
                        dve.wait_ge(ao_made, b * H + h)
                    dve.tensor_tensor(ow[:], oh[:, :, :, 0:DH], ab[:].unsqueeze(3).broadcast_to((P, 2, NI, DH)),
                                      op=ALU.mult).then_inc(o_free, 1)
                    dve.wait_ge(o_free, b * H + (h + 2))
                    dve.tensor_tensor(AO[:, :, h * DH:(h + 1) * DH], ow[:, 0, :, :], ow[:, 1, :, :],
                                      op=ALU.add).then_inc(ao_made, 1)

                geo_rows(0)
                for i in range(NI):
                    row_max(0, i)
                minus_max(0)
                geo_rows(1)
                for i in range(NI):
                    row_max(1, i)
                minus_max(1)
                for h in range(H):
                    if h >= 1:
                        mix(h - 1)
                        if h + 1 < H:
                            geo_rows(h + 1)
                    if h + 2 < H:
                        for i in range(NI):
                            row_max(h + 2, i)
                        minus_max(h + 2)
                mix(H - 1)
                for i in range(NI):
                    name = ("wo", i)
                    pair_wait(dve, pair_full, b, name)
                    dve.wait_ge(so_out[i % 2], b * (8 * NI) + 16 * (i // 2 + 1))
                    dve.tensor_copy(SO[i % 2][:], pbank(name)[:, 0, :]) \
                        .then_inc(pair_free[PAIR_USE[name] % 2], 1)

            for k in range(2):
                dve.wait_ge(xn_out[k], 16 * (NT // 2 + 1))
                dve.wait_ge(so_out[k], 16 * (NT // 2 + 1))
                dve.wait_ge(x_in[k], 16 * (NT // 2 + 1))
            dve.wait_ge(scattered, 16 * NSC)
            for k in range(2):
                dve.wait_ge(pair_free[k], B * (NPAIR // 2) + 1)
            rc = [0]

            def route(ins):
                rc[0] += 1
                ins.then_inc(routing, 1)
                dve.wait_ge(routing, rc[0])

            for g in range(NT):
                last = dve.max(MX[:, g, :], LG[:, g, :])
            route(last)
            for g in range(NT):
                last = dve.max_index(IX[:, g, :], MX[:, g, :], LG[:, g, :])
            route(last)
            dve.tensor_tensor(gates[:, 1, :], MX[:, :, 1], MX[:, :, 0], op=ALU.subtract).then_inc(route_act, 1)
            enum = rows_f[:, NJ:NJ + E].unsqueeze(1).broadcast_to((P, NT, E))
            for m in range(TOPK):
                route(dve.tensor_tensor(OH[:, m, :, :], IX[:, :, m:m + 1].broadcast_to((P, NT, E)), enum,
                                        op=ALU.is_equal))
            dve.tensor_tensor(CS[:], OH[:, 0, :, :], OH[:, 1, :, :], op=ALU.add).then_inc(route_cs, 1)
            dve.wait_ge(route_act, 2)
            route(dve.tensor_scalar(gates[:, 1, :], gates[:, 0, :], 1.0, None, ALU.add))
            route(dve.reciprocal(gates[:, 2, :], gates[:, 1, :]))
            route(dve.tensor_tensor(gates[:, 3, :], gates[:, 0, :], gates[:, 2, :], op=ALU.mult))
            for m in range(TOPK):
                route(dve.tensor_copy(prow[:, :, m, 1], gates[:, 2 + m, :]))
                route(dve.tensor_scalar(prow[:, :, m, 0], rows_f[:, 0:NT], rows_f[:, NJ + E:NJ + E + 1], None, ALU.add))
            route(dve.memset(ones_f[:], 1.0))
            dve.wait_ge(route_pe, 2)
            flat = TOT[:].rearrange("p g e -> p (g e)")
            route(dve.tensor_copy(flat, pair[0][:, 1, 0:NT * E]))
            for e in range(E):
                route(dve.tensor_tensor_scan(INC[:, :, e], ones_f[:], TOT[:, :, e], 0.0, ALU.mult, ALU.add))
            route(dve.tensor_scalar(padi[:], INC[:, NT - 1, :], float(P - 1), None, ALU.add))
            route(dve.tensor_scalar(padi[:], padi[:], -P, None, ALU.bitwise_and))
            route(dve.tensor_copy(padc[:, 0, :], padi[:]))
            route(dve.tensor_tensor_scan(padc[:, 1, :], ones_f[:, 0:E], padc[:, 0, :], 0.0, ALU.mult, ALU.add))
            route(dve.tensor_tensor(padc[:, 2, :], padc[:, 1, :], padc[:, 0, :], op=ALU.subtract))
            route(dve.tensor_tensor(BASE[:], INC[:], TOT[:], op=ALU.subtract))
            route(dve.tensor_tensor(BASE[:], BASE[:], padc[:, 2, :].unsqueeze(1).broadcast_to((P, NT, E)), op=ALU.add))
            route(dve.tensor_tensor(BASE[:].rearrange("p g e -> p (g e)"), pair[0][:, 0, 0:NT * E],
                                    BASE[:].rearrange("p g e -> p (g e)"), op=ALU.add))
            for m in range(TOPK):
                route(dve.tensor_tensor(sel[:], BASE[:], OH[:, m, :, :], op=ALU.mult))
                route(dve.reduce_sum(posf[:, m, :], sel[:], AX))
                dve.tensor_copy(posi[:, m, :], posf[:, m, :]).then_inc(route_pos, 1)
            route(dve.tensor_tensor(cmpj[:], rows_f[:, 0:NJ].unsqueeze(2).broadcast_to((P, NJ, E)),
                                    padc[:, 1, :].unsqueeze(1).broadcast_to((P, NJ, E)), op=ALU.is_ge))
            route(dve.reduce_sum(ejf[:], cmpj[:], AX))
            dve.tensor_scalar(eji[:], ejf[:], float(E - 1), None, ALU.min).then_inc(lists_made, 1)
            for c in range(NC):
                dve.wait_ge(stage_in[c % 2], 16 * (c // 2 + 1))
                dve.tensor_tensor(DPv[:, c, :, :], stage[c % 2][:].rearrange("p r e -> p e r"),
                                  WT[:, c, :].unsqueeze(1).broadcast_to((P, E, C)), op=ALU.add).then_inc(dp_made, 1)
            dve.wait_ge(route_pe, 3)
            dve.tensor_copy(TLI[:], work[0][:, 0:NJ]).then_inc(lists_made, 1)
            dve.tensor_copy(GL[:], work[0][:, 128:128 + NJ]).then_inc(lists_made, 1)
            dve.wait_ge(lists_made, LISTS)

            with dve.Fori(0, NJ // 2) as q:
                for k in range(2):
                    dve.wait_ge(yg_made, q * 2 + (k + 1))
                    dve.tensor_copy(GG[k][:], GL[:, bass.ds(q * 2 + k, 1)]).then_inc(gg_made, 1)
                    dve.wait_ge(gg_made, q * 2 + (k + 1))
                    dve.wait_ge(y_full, q * 2 + (k + 1))
                    dve.wait_ge(y_out[k], q * 16 + 16)
                    dve.tensor_scalar(YG[k][:], pair[k][:, 0, :], GG[k][:, 0:1], None, ALU.mult).then_inc(yg_made, 1)

            with dve.Fori(0, NT // 2) as q:
                for k in range(2):
                    dve.wait_ge(fy_in[k], q * 32 + 32)
                    dve.wait_ge(out_out[k], q * 16 + 16)
                    dve.tensor_tensor(FO[k][:], FY[k][0][:], FY[k][1][:], op=ALU.add).then_inc(z_made, 1)
                for k in range(2):
                    dve.wait_ge(g_made, q * 2 + (k + 1))
                    dve.wait_ge(fxs_in[k], q * 32 + 32)
                    dve.tensor_tensor(FO[k][:], FO[k][:], FS[k][:], op=ALU.mult).then_inc(sg_made, 1)
                for k in range(2):
                    dve.wait_ge(sg_made, q * 2 + (k + 1))
                    dve.tensor_tensor(FO[k][:], FO[k][:], FX[k][:], op=ALU.add).then_inc(fo_made, 1)


_INS = ["L0_attn_x", "L0_attn_Wq", "L0_attn_Wk", "L0_attn_Wv", "L0_attn_Wo", "L0_attn_head_scales",
        "L0_ffn_gate_w", "L0_ffn_W", "L0_ffn_atoms", "L0_ffn_expert_atom_weights", "L0_ffn_importance",
        "L0_ffn_mask_idx"]


def constants():
    import numpy as np
    p = np.arange(P)
    inv = (np.float32(1.0) / (10000.0 ** (np.arange(0, DH, 2, dtype=np.float32).astype(np.float64) / DH))
           .astype(np.float32)).astype(np.float32)
    ang = (np.arange(T, dtype=np.float32)[:, None] * inv[None, :]).astype(np.float64)
    cos, sin = np.cos(ang), np.sin(ang)
    rope = np.stack([np.concatenate([cos, cos], -1), np.concatenate([-sin, sin], -1)])
    rope = rope.reshape(2, NI, P, DH).transpose(2, 0, 1, 3).reshape(P, -1).astype(np.float32)
    trig = np.array([[a, b, c] for a in (1.0, -1.0) for b in (1.0, -1.0) for c in (1.0, -1.0)], np.float32)
    dirs = (trig / np.sqrt(3.0)).astype(np.float32)
    dirs = np.broadcast_to(np.stack([dirs, dirs * np.float32(DH ** 0.5)]).reshape(1, -1), (P, 2 * H * 3))
    onehot = np.zeros((P, H), np.float32)
    for r in list(range(24)) + list(range(64, 72)) + list(range(96, 104)):
        onehot[r, r % 8] = 1.0
    rows = np.zeros((P, NJ + E + 2), np.float32)
    rows[:, 0:NJ] = P * np.arange(NJ)
    rows[:, NJ:NJ + E] = np.arange(E)
    rows[:, NJ + E] = p
    rows[:, NJ + E + 1] = C * C + p
    return {"c_ident": np.eye(P, dtype=np.float32), "c_rope": rope, "c_dirs": np.ascontiguousarray(dirs),
            "c_onehot": onehot, "c_rows": rows}


def kernel(**inputs):
    import numpy as np
    import concourse.bacc as bacc
    from concourse.bass_utils import run_bass_kernel_spmd

    nc = bacc.Bacc("TRN2", target_bir_lowering=False, num_devices=1)
    arrays, args = {}, []
    data = [(n, np.ascontiguousarray(inputs[n])) for n in _INS] + list(constants().items())
    for name, a in data:
        arrays[f"in_{name}"] = a
        args.append(nc.dram_tensor(f"in_{name}", a.shape, mybir.dt.from_np(a.dtype), kind="ExternalInput").ap())
    args.append(nc.dram_tensor("out_0", (B, T, C), F32, kind="ExternalOutput").ap())
    build(nc, *args)
    r = run_bass_kernel_spmd(nc, [arrays], core_ids=[0])
    return r.results[0]["out_0"]
```

```python
from collections import namedtuple
from contextlib import ExitStack

import concourse.bass as bass
from concourse import mybir

F32 = mybir.dt.float32
F32R = mybir.dt.float32r
BF16 = mybir.dt.bfloat16
I32 = mybir.dt.int32
U32 = mybir.dt.uint32
ALU = mybir.AluOpType
ACT = mybir.ActivationFunctionType
AX = mybir.AxisListType.X

P = 128
B, T, C = 8, 512, 512
NI = T // P
NC = C // P
NT = B * NI
H, KVH, DH = 8, 2, 64
REP = H // KVH
HALF = DH // 2
QC, KC = H * DH, KVH * DH
E, A, NS = 8, 64, 4096
NSC = NS // P
TOPK = 2
NJ = TOPK * B * T // P + E
WCOLS = QC + 2 * KC + E
EPS = 1e-5
NEG = -1e30
QROWS = DH + 2
GROWS = 104
SOFF = [sum(T - P * m for m in range(j)) for j in range(NI + 1)]

ROUTE_STEP = 0


def _qm(h, *tiles):
    return [("qm", h % H, i) for i in tiles]


def _s(h, *tiles):
    return [("s", h % H, j) for j in tiles]


def _head_uses(full):
    work_uses, pair_uses = [], []
    for h in range(H):
        more, most = full or h + 1 < H, full or h + 2 < H
        work_uses += [("qb", (h + 1) % H)] if more else []
        work_uses += [("kt", 0)] if full and h == H - 2 else []
        pair_uses += _s(h, 2)
        work_uses += [("qa", (h + 2) % H)] if most else []
        pair_uses += _s(h, 3)
        work_uses += [("xt", h)] if full and h < NI else []
        work_uses += _qm(h + 2, 0, 1) if most else []
        pair_uses += [("p", h - 1)] if full and 1 <= h <= NI else []
        work_uses += [("route",)] if not full and h == ROUTE_STEP else []
        pair_uses += _s(h + 1, 0) if more else []
        work_uses += _qm(h + 2, 2, 3) if most else []
        work_uses += [("kt", 1)] if full and h == H - 1 else []
        work_uses += [("tk",), ("tq",)] if full and h == H - 3 else []
        pair_uses += _s(h + 1, 1) if more else []
    return work_uses, pair_uses


START_WORK = [("xt", i) for i in range(NI)] + [("w", k) for k in range(NC)] + [("tk",), ("tq",), ("kt", 0), ("kt", 1), ("qa", 0), ("qa", 1)] \
    + _qm(0, 0, 1, 2, 3) + [("qb", 0)] + _qm(1, 0, 1, 2, 3)
START_PAIR = [("p", i) for i in range(NI)] + _s(0, 0, 1)
BODY_WORK, BODY_PAIR = _head_uses(True)
LAST_WORK, LAST_PAIR = _head_uses(False)
NWORK, NPAIR = len(BODY_WORK), len(BODY_PAIR)
assert NWORK % 2 == 0 and NPAIR % 2 == 0
Part = namedtuple("Part", "work pair work_ahead pair_ahead b")
START = Part(START_WORK, START_PAIR, 0, 0, 0)


def body_part(b):
    return Part(BODY_WORK, BODY_PAIR, len(START_WORK), len(START_PAIR), b)


LAST = Part(LAST_WORK, LAST_PAIR, len(START_WORK), len(START_PAIR), B - 1)
ALL_WORK = [(len(START_WORK) + (B - 1) * NWORK + len(LAST_WORK) + 1 - k) // 2 for k in range(2)]
ALL_PAIR = [(len(START_PAIR) + (B - 1) * NPAIR + len(LAST_PAIR) + 1 - k) // 2 for k in range(2)]


def build(nc, x, Wq, Wk, Wv, Wo, head_scales, gate_w, ffn_W, atoms, expert_atom_weights, importance,
          mask_idx, c_ident, c_rope, c_dirs, c_onehot, c_rows, out):
    xn_d = nc.dram_tensor("xn_d", (B * T, C), F32, kind="Internal").ap()
    ao_d = nc.dram_tensor("ao_d", (B * T, C), F32, kind="Internal").ap()
    y_d = nc.dram_tensor("y_d", (NJ * P, C), F32, kind="Internal").ap()
    pair_d = nc.dram_tensor("pair_d", (NJ * P, 2), F32, kind="Internal").ap()
    upd_d = nc.dram_tensor("upd_d", (C * C + P, E), F32, kind="Internal").ap()

    x_f = x.rearrange("b t c -> (b t) c")
    out_f = out.rearrange("b t c -> (b t) c")

    with ExitStack() as ctx:
        def sem(name):
            return ctx.enter_context(nc.semaphore(name))

        def psum(name, shape, dt=F32):
            return ctx.enter_context(nc.psum_tensor(name, shape, dt))

        def keep(name, shape, dt=F32):
            return ctx.enter_context(nc.sbuf_tensor(name, shape, dt))

        ident = keep("ident", [P, P])
        identb = keep("identb", [P, P], BF16)
        ones_row = keep("ones_row", [P, P], BF16)
        before = keep("before", [P, P], BF16)
        rows_f = keep("rows_f", [P, NJ + E + 2])
        WT = keep("WT", [P, NC, C])
        WO = keep("WO", [P, NC, C])
        LG = keep("LG", [P, NI, E])
        MXB = keep("MXB", [P, NI, E])
        IXB = keep("IXB", [P, NI, E], U32)
        MX = keep("MX", [P, NT, E])
        IX = keep("IX", [P, NT, E], U32)
        UPD = keep("UPD", [P, NSC, E])
        DSTI = keep("DSTI", [P, NSC], I32)
        DP = keep("DP", [P, NC * E * C])
        DPv = DP[:].rearrange("p (c e r) -> p c e r", c=NC, e=E)
        idx_row = DP[:, 0:NS].bitcast(I32)
        EQ = DP[:, NS:NS + NS // 2].bitcast(BF16)
        at_sb = DP[0:A, 2 * NS:3 * NS]
        imp_sb = DP[A:A + E, 2 * NS:3 * NS]
        EQB = DP[:, 2 * NS:2 * NS + NS // 2].bitcast(BF16)
        SIG = DP[:, 3 * NS:3 * NS + NSC * E]
        QK_AT = 3 * NS + 512

        pair = [psum(f"pair{k}", [P, 2, 512]) for k in range(2)]
        work = [psum(f"work{k}", [P, 512]) for k in range(2)]
        O = psum("O", [P, 2, 512])

        attn = ExitStack()

        def sb(name, shape, dt=F32):
            return attn.enter_context(nc.sbuf_tensor(name, shape, dt))

        proj = ExitStack()
        top = [0]

        def pb(name, shape, dt=F32):
            n = 1
            for m in shape[1:]:
                n *= m
            top[0] += -(-n * (2 if dt == BF16 else 4) // 32) * 32
            return proj.enter_context(nc.sbuf_tensor(name, shape, dt))

        WX = pb("WX", [P, NC, WCOLS])
        rope = pb("rope", [P, 2, NI, DH])
        eaw = pb("eaw", [E, A])
        est = pb("est", [E, 4])
        awT = pb("awT", [A, E])
        idx_col = pb("idx_col", [P, NSC], I32)
        ibits = pb("ibits", [P, 2, NSC], I32)
        fcol = pb("fcol", [P, 4, NSC])
        idx_t = pb("idx_t", [NSC, 2, P], I32)
        UPR = pb("UPR", [P, NSC, 3, E], BF16)
        gw = pb("gw", [E, C])
        X = [pb(f"X{k}", [P, C]) for k in range(2)]
        XN = [pb(f"XN{k}", [P, C]) for k in range(2)]
        XT = [pb(f"XT{k}", [P, NC, P]) for k in range(2)]
        bst = pb("bst", [P, 6])
        mv = [pb(f"mv{k}", [P, 2]) for k in range(2)]
        veps = [pb(f"veps{k}", [P, 1]) for k in range(2)]
        rstd = [pb(f"rstd{k}", [P, 1]) for k in range(2)]
        rt1 = pb("rt1", [P, H + KVH, DH])
        rt2 = pb("rt2", [P, H + KVH, DH])
        proj.close()
        proj_end = top[0]

        top[0] = 0

        def rb(name, shape, dt=F32):
            n = 1
            for m in shape[1:]:
                n *= m
            top[0] += -(-n * (2 if dt == BF16 else 4) // 32) * 32
            return keep(name, shape, dt)

        gates = rb("gates", [P, 4, NT])
        OH = rb("OH", [P, TOPK, NT, E])
        CS = rb("CS", [P, NT, E], BF16)
        CNT = rb("CNT", [P, 2, NT, E])
        INC = rb("INC", [P, NT, E])
        BASE = rb("BASE", [P, NT, E])
        ones_f = rb("ones_f", [P, NT])
        padc = rb("padc", [P, 4, E])
        padi = rb("padi", [P, E], I32)
        sel = rb("sel", [P, NT, E])
        posf = rb("posf", [P, TOPK, NT])
        posi = rb("posi", [P, TOPK, NT], I32)
        prow = rb("prow", [P, NT, TOPK, 2])
        cmpj = rb("cmpj", [P, NJ, E])
        ejf = rb("ejf", [P, NJ])
        eji = rb("eji", [P, NJ], I32)
        stage = rb("stage", [P, C, E])
        assert top[0] <= proj_end
        keep("rest_of_proj", [P, (proj_end - top[0]) // 4])

        maskN = sb("maskN", [P, P], BF16)
        maskT = sb("maskT", [P, P], BF16)
        dirs = sb("dirs", [P, 2, H, 3])
        onehot = sb("onehot", [P, H])
        hs = sb("hs", [P, 2, H])
        mhalf = sb("mhalf", [P, 1])
        at = [0]

        def carve(*shape):
            n = 1
            for m in shape:
                n *= m
            at[0] += n
            names = "abcd"[:len(shape)]
            return DP[:, at[0] - n:at[0]].rearrange(f"p ({' '.join(names)}) -> p {' '.join(names)}",
                                                    **dict(zip(names, shape)))

        QK = DP[:, QK_AT:QK_AT + NI * (H + KVH) * DH].rearrange("p (i n) -> p i n", i=NI)
        QH = carve(NI, H, 2, DH)
        QL = carve(NI, H, QROWS)
        KHL = carve(NI, KVH, 2, DH)
        at[0] = 2 * NS
        AO = carve(NI, C)
        V = sb("V", [P, NI, KVH, DH + 1])
        VN = sb("VN", [P, NI, KVH, DH])
        gt = [sb(f"gt{k}", [P, NI, H, 3]) for k in range(2)]
        TQ = sb("TQ", [P, NI, 72])
        TK = sb("TK", [P, NI, 72])
        QA = [sb(f"QA{k}", [P, T], F32R) for k in range(4)]
        KA = sb("KA", [P, KVH, T], F32R)
        KB = sb("KB", [QROWS, KVH, T], F32R)
        QB = [sb(f"QB{k}", [QROWS, T], F32R) for k in range(2)]
        KR = sb("KR", [GROWS, T])
        kpr = sb("kpr", [72, T])
        qpr = sb("qpr", [72, T])
        cmx = sb("cmx", [72, T])
        cmn = sb("cmn", [72, T])
        QG = sb("QG", [GROWS, T], F32R)
        KG = [sb(f"KG{k}", [GROWS, T], F32R) for k in range(2)]
        M = sb("M", [P, H, NI])
        PT = [sb(f"PT{k}", [P, 2, SOFF[NI]]) for k in range(2)]
        rl = sb("rl", [P, 2, NI])
        ab = sb("ab", [P, 2, NI])
        ow = sb("ow", [P, 2, NI, DH])
        sci = [sb(f"sci{k}", [P, 1], I32) for k in range(2)]
        scv = [sb(f"scv{k}", [P, E]) for k in range(2)]
        attn.close()

        WF = PT[1][:].rearrange("p a n -> p (a n)")[:, 0:NC * C].rearrange("p (k c) -> p k c", k=NC)

        PL = keep("PL", [NJ, P, 2])
        TLI = keep("TLI", [P, NJ], I32)
        GL = keep("GL", [P, NJ])
        GI = [keep(f"GI{k}", [P, 1], I32) for k in range(4)]
        GG = [keep(f"GG{k}", [P, 1]) for k in range(2)]
        XG = [keep(f"XG{k}", [P, C]) for k in range(4)]
        XGT = [keep(f"XGT{k}", [P, NC, P]) for k in range(2)]
        YG = [keep(f"YG{k}", [P, C]) for k in range(2)]
        FI = [[keep(f"FI{k}{m}", [P, 1], I32) for m in range(TOPK)] for k in range(2)]
        FY = [[keep(f"FY{k}{m}", [P, C]) for m in range(TOPK)] for k in range(2)]
        FX = [keep(f"FX{k}", [P, C]) for k in range(2)]
        FA = [keep(f"FA{k}", [P, C]) for k in range(2)]
        FAT = [keep(f"FAT{k}", [P, NC, P]) for k in range(2)]
        FO = [keep(f"FO{k}", [P, C]) for k in range(2)]

        early_in = sem("early_in")
        consts_in = sem("consts_in")
        late_in = sem("late_in")
        passed = sem("passed")
        weights_in = sem("weights_in")
        zero_made = sem("zero_made")
        zeroed = sem("zeroed")
        pre = {n: sem("pre_" + n) for n in ("pe", "act", "dve", "pool")}
        fills = sem("fills")
        x_in = [sem(f"x_in{k}") for k in range(2)]
        xn_out = [sem(f"xn_out{k}") for k in range(2)]
        ao_out = sem("ao_out")
        stats_made = sem("stats_made")
        bst_made = sem("bst_made")
        mv_made = sem("mv_made")
        rstd_made = sem("rstd_made")
        xn_made = sem("xn_made")
        work_full = [sem(f"work_full{k}") for k in range(2)]
        work_free = [sem(f"work_free{k}") for k in range(2)]
        pair_full = [sem(f"pair_full{k}") for k in range(2)]
        pair_free = [sem(f"pair_free{k}") for k in range(2)]
        rope_parts = sem("rope_parts")
        top_made = sem("top_made")
        qk_made = sem("qk_made")
        v_made = sem("v_made")
        khi_made = sem("khi_made")
        klo_made = sem("klo_made")
        qhi_made = sem("qhi_made")
        qlo_made = sem("qlo_made")
        geo_a = sem("geo_a")
        geo_b = sem("geo_b")
        geo_cols = sem("geo_cols")
        cum_made = sem("cum_made")
        geo_max = sem("geo_max")
        kr_made = sem("kr_made")
        qpr_made = sem("qpr_made")
        qg_made = sem("qg_made")
        kg_made = sem("kg_made")
        nmax_hi = sem("nmax_hi")
        nmax_made = sem("nmax_made")
        o_full = sem("o_full")
        o_free = sem("o_free")
        rl_made = sem("rl_made")
        ab_made = sem("ab_made")
        ao_made = sem("ao_made")
        sc_slot = sem("sc_slot")
        scattered = sem("scattered")
        routing = sem("routing")
        route_cs = sem("route_cs")
        route_pos = sem("route_pos")
        route_act = sem("route_act")
        route_pe = sem("route_pe")
        pairs_out = sem("pairs_out")
        pairs_in = sem("pairs_in")
        lists_made = sem("lists_made")
        stage_in = sem("stage_in")
        dp_made = sem("dp_made")
        gi_made = sem("gi_made")
        xg_in = [sem(f"xg_in{k}") for k in range(4)]
        xg_read = sem("xg_read")
        xgt_made = sem("xgt_made")
        gg_made = sem("gg_made")
        yg_made = sem("yg_made")
        y_full = sem("y_full")
        y_out = [sem(f"y_out{k}") for k in range(2)]
        fi_made = sem("fi_made")
        fy_in = [sem(f"fy_in{k}") for k in range(2)]
        fx_in = [sem(f"fx_in{k}") for k in range(2)]
        fa_in = [sem(f"fa_in{k}") for k in range(2)]
        fa_read = sem("fa_read")
        fat_made = sem("fat_made")
        s_full = sem("s_full")
        z_made = sem("z_made")
        g_made = sem("g_made")
        sg_made = sem("sg_made")
        fo_made = sem("fo_made")
        out_out = [sem(f"out_out{k}") for k in range(2)]

        block = ctx.enter_context(nc.Block())

        def use(part, kind, name):
            u = (part.work.index(name) + part.work_ahead) if kind == "work" \
                else (part.pair.index(name) + part.pair_ahead)
            per_run = (NWORK if kind == "work" else NPAIR) // 2
            return u % 2, lambda more: part.b * per_run + (u // 2 + more)

        def work_wait(eng, sems, part, name):
            k, number = use(part, "work", name)
            eng.wait_ge(sems[k], number(1))

        def pair_wait(eng, sems, part, name):
            k, number = use(part, "pair", name)
            eng.wait_ge(sems[k], number(1))

        def work_emptied(eng, part, name):
            k, number = use(part, "work", name)
            eng.wait_ge(work_free[k], number(2))

        def pair_emptied(eng, part, name):
            k, number = use(part, "pair", name)
            eng.wait_ge(pair_free[k], number(2))

        def wsem(part, name, sems):
            return sems[use(part, "work", name)[0]]

        def psem(part, name, sems):
            return sems[use(part, "pair", name)[0]]

        def wbank(part, name):
            return work[use(part, "work", name)[0]]

        def pbank(part, name):
            return pair[use(part, "pair", name)[0]]

        DVE_SLOTS, DVE_SOFTMAX, DVE_WEIGHTS, DVE_VALUES, DVE_EARLIER, DVE_PLACES = 1, 5, 11, 18, 25, 32
        ACT_SUM, ACT_AWT, ACT_SIG = 1, 2, 3
        PE_SLOTS, PE_AWT, PE_GATE, PE_IMP, PE_DELTA, PE_SUM, PE_COUNT = 1, 2, 3, 4, 5, 6, 7
        FILLS = 12
        DP_ORDER = (3, 0, 1, 2)
        LISTS = 3

        @block.sync
        def _(sp):
            for dst, src in ((ident[:], c_ident), (eaw[:], expert_atom_weights),
                             (idx_t[:, 0, :], mask_idx.rearrange("(n p) -> n p", p=P)),
                             (idx_row, mask_idx.rearrange("(a s) -> a s", a=1).broadcast_to((P, NS)))):
                sp.dma_start(dst, src).then_inc(early_in, 16)
            sp.dma_start(X[0][:], x_f[0:P, :]).then_inc(x_in[0], 16)
            sp.dma_start(X[1][:], x_f[P:2 * P, :]).then_inc(x_in[1], 16)
            sp.dma_start(gw[:], gate_w).then_inc(weights_in, 16)
            for dst, src in ((WX[:, :, 0:QC], Wq), (WX[:, :, QC:QC + KC], Wk), (WX[:, :, QC + KC:QC + 2 * KC], Wv)):
                sp.dma_start(dst, src.rearrange("(k p) n -> p k n", p=P)).then_inc(weights_in, 16)
            for dst, src in ((imp_sb, importance), (at_sb, atoms), (rope[:], c_rope.rearrange("p (a i d) -> p a i d", a=2, i=NI)),
                             (rows_f[:], c_rows), (hs[:, 1, :], head_scales.rearrange("(a h) -> a h", a=1).broadcast_to((P, H))),
                             (dirs[:], c_dirs.rearrange("p (a h d) -> p a h d", a=2, h=H)), (onehot[:], c_onehot)):
                sp.dma_start(dst, src).then_inc(consts_in, 16)
            sp.dma_start(WF[:], ffn_W.rearrange("(k p) c -> p k c", p=P)).then_inc(late_in, 16)
            sp.dma_start(WO[:], Wo.rearrange("(k p) n -> p k n", p=P)).then_inc(late_in, 16)
            sp.wait_ge(zero_made, 1)
            zsrc = PT[0][:].rearrange("p a n -> p (a n)")[:, 0:2048]
            for m in range(C * C * E // (P * 2048)):
                sp.dma_start(upd_d[m * 32768:(m + 1) * 32768, :].rearrange("(p n) e -> p (n e)", p=P),
                             zsrc).then_inc(zeroed, 16)
            sp.dma_start(pair_d.rearrange("(p n) e -> p (n e)", p=P), zsrc[:, 0:NJ * 2]).then_inc(zeroed, 16)

            def project_traffic(n):
                made = [sp.snap(n * NI + (i + 1)) for i in range(NI)]
                row = [sp.snap(n * T + i * P) for i in range(NI)]
                nxt = [sp.snap(((n * NI + (i + 2)) & (NT - 1)) * P) for i in range(NI)]
                for i in range(NI):
                    sp.wait_ge(xn_made, made[i])
                    sp.dma_start(xn_d[bass.ds(row[i], P), :], XN[i % 2][:]).then_inc(xn_out[i % 2], 16)
                    sp.dma_start(X[i % 2][:], x_f[bass.ds(nxt[i], P), :]).then_inc(x_in[i % 2], 16)

            for i in range(NI):
                sp.wait_ge(xn_made, i + 1)
                sp.dma_start(xn_d[i * P:(i + 1) * P, :], XN[i % 2][:]).then_inc(xn_out[i % 2], 16)
                sp.dma_start(X[i % 2][:], x_f[(i + 2) * P:(i + 3) * P, :]).then_inc(x_in[i % 2], 16)
            with sp.Fori(0, B - 1) as b:
                ao_done = sp.snap(b * H + H)
                first = sp.snap(b * T)
                project_traffic(b + 1)
                sp.wait_ge(ao_made, ao_done)
                sp.dma_start(ao_d[bass.ds(first, T), :].rearrange("(i p) c -> p i c", p=P), AO).then_inc(ao_out, 16)

            for k in range(2):
                sp.wait_ge(xn_out[k], 16 * (NT // 2 + 1))
                sp.wait_ge(x_in[k], 16 * (NT // 2 + 1))
            sp.wait_ge(scattered, 16 * NSC)
            sp.wait_ge(work_full[use(LAST, "work", ("qb", 1))[0]], use(LAST, "work", ("qb", 1))[1](1))
            for n, c in enumerate(DP_ORDER):
                if n >= 1:
                    sp.wait_ge(dp_made, n)
                sp.dma_start(stage[:], upd_d[c * P * C:(c + 1) * P * C, :]
                             .rearrange("(p r) e -> p r e", p=P)).then_inc(stage_in, 16)
            sp.wait_ge(ao_made, B * H)
            sp.dma_start(ao_d[(B - 1) * T:B * T, :].rearrange("(i p) c -> p i c", p=P), AO).then_inc(ao_out, 16)
            for k in range(2):
                sp.wait_ge(pair_free[k], ALL_PAIR[k] + 1)
            sp.wait_ge(pairs_out, 16 * TOPK * NT)
            sp.dma_start(PL[:], pair_d.rearrange("(j p) e -> j p e", p=P)).then_inc(pairs_in, 16)

            with sp.Fori(0, NJ // 2) as q:
                made = [sp.snap(q * 2 + (k + 3)) for k in range(2)]
                row = [sp.snap(q * (2 * P) + k * P) for k in range(2)]
                for k in range(2):
                    sp.wait_ge(yg_made, made[k])
                    sp.dma_start(y_d[bass.ds(row[k], P), :], YG[k][:]).then_inc(y_out[k], 16)

            sp.wait_ge(ao_out, 16 * (B + 1))
            for k in range(2):
                sp.dma_start(FA[k][:], ao_d[k * P:(k + 1) * P, :]).then_inc(fa_in[k], 16)
                sp.dma_start(FX[k][:], x_f[k * P:(k + 1) * P, :]).then_inc(fx_in[k], 16)
            with sp.Fori(1, NT // 2) as q:
                made = [sp.snap(q * 2 + (k - 1)) for k in range(2)]
                row = [sp.snap(q * (2 * P) + k * P) for k in range(2)]
                done = [sp.snap(q * (2 * P) + (k - 2) * P) for k in range(2)]
                for k in range(2):
                    sp.wait_ge(fa_read, made[k])
                    sp.dma_start(FA[k][:], ao_d[bass.ds(row[k], P), :]).then_inc(fa_in[k], 16)
                for k in range(2):
                    sp.wait_ge(fo_made, made[k])
                    sp.dma_start(out_f[bass.ds(done[k], P), :], FO[k][:]).then_inc(out_out[k], 16)
                    sp.dma_start(FX[k][:], x_f[bass.ds(row[k], P), :]).then_inc(fx_in[k], 16)
            for k in range(2):
                n = NT - 2 + k
                sp.wait_ge(fo_made, n + 1)
                sp.dma_start(out_f[n * P:(n + 1) * P, :], FO[k][:]).then_inc(out_out[k], 16)
            for k in range(2):
                sp.wait_ge(out_out[k], 16 * (NT // 2 + 1))

        @block.gpsimd
        def _(pool):
            def low_k(n, i):
                pool.wait_ge(khi_made, n * NI + (i + 1))
                pool.tensor_tensor(KHL[:, i, :, 1, :], QK[:, i, QC:].rearrange("p (v d) -> p v d", v=KVH),
                                   KHL[:, i, :, 0, :], op=ALU.subtract).then_inc(klo_made, 1)

            def low_q(n, i):
                pool.wait_ge(qhi_made, n * NI + (i + 1))
                pool.tensor_tensor(QL[:, i, :, 0:DH], QK[:, i, 0:QC].rearrange("p (h d) -> p h d", h=H),
                                   QH[:, i, :, 0, :],
                                   op=ALU.subtract).then_inc(qlo_made, 1)

            def inverse_deviation(n, i):
                pool.wait_ge(stats_made, n * NI + (i + 1))
                pool.tensor_tensor(rstd[i % 2][:], veps[i % 2][:], mhalf[:], op=ALU.pow).then_inc(rstd_made, 1)

            def take_v(n, v):
                pool.wait_ge(qk_made, n * NI + (NI + 1))
                pool.sem_inc(passed, 1)
                pool.tensor_copy(V[:, :, v, 0:DH], VN[:, :, v, :]).then_inc(v_made, 1)

            def scatter(b, i):
                c = b * NI + i
                if isinstance(c, int):
                    idx, val = DSTI[:, c:c + 1], UPD[:, c, :]
                else:
                    idx, val = DSTI[:, bass.ds(c, 1)], UPD[:, bass.ds(c, 1), :].rearrange("p a e -> p (a e)")
                pool.tensor_copy(sci[i % 2][:], idx).then_inc(sc_slot, 1)
                pool.tensor_copy(scv[i % 2][:], val).then_inc(sc_slot, 1)
                pool.wait_ge(sc_slot, b * (2 * NI) + 2 * (i + 1))
                pool.sem_inc(passed, 1)
                pool.indirect_dma_start(
                    out=upd_d, out_offset=bass.IndirectOffsetOnAxis(ap=sci[i % 2][:, 0:1], axis=0),
                    in_=scv[i % 2][:], in_offset=None, compute_op=ALU.add).then_inc(scattered, 16)
                pool.wait_ge(scattered, b * (NI * 16) + 16 * (i + 1))

            pool.memset(PT[0][:], 0.0).then_inc(zero_made, 1)
            for m in (maskN, maskT):
                pool.memset(m[:], 0.0).then_inc(pre["pool"], 1)
            pool.memset(before[:], 1.0).then_inc(pre["pool"], 1)
            pool.memset(KR[:], 0.0).then_inc(pre["pool"], 1)
            pool.wait_ge(pre["pool"], 4)
            pool.affine_select(out=maskN[:], in_=maskN[:], compare_op=ALU.is_ge, fill=NEG, base=0,
                               pattern=[[-1, P]], channel_multiplier=1).then_inc(fills, 1)
            pool.affine_select(out=maskT[:], in_=maskT[:], compare_op=ALU.is_ge, fill=NEG, base=0,
                               pattern=[[1, P]], channel_multiplier=-1).then_inc(fills, 1)
            pool.affine_select(out=before[:], in_=before[:], compare_op=ALU.is_gt, fill=0.0, base=0,
                               pattern=[[1, P]], channel_multiplier=-1).then_inc(fills, 1)
            for n, (dst, value) in enumerate(((KR[64:72, :], 1.0), (KR[96:104, :], 1.0), (ones_row[:], 1.0),
                               (mhalf[:], -0.5), (TQ[:], 0.0), (TK[:], 0.0), (QG[:].bitcast(F32), 0.0),
                               (V[:, :, :, DH:DH + 1], 1.0), (KB[DH:QROWS, :, :].bitcast(F32), 1.0))):
                pool.wait_ge(fills, 3 + n)
                pool.memset(dst, value).then_inc(fills, 1)
            pool.wait_ge(fills, FILLS)
            pool.sem_inc(z_made, 2)
            pool.sem_inc(xg_read, 4)

            for i in range(NI):
                inverse_deviation(0, i)
            pool.wait_ge(pre["dve"], DVE_EARLIER)
            for i in range(NI):
                low_k(0, i)
                low_q(0, i)
            inverse_deviation(1, 0)
            for v in range(KVH):
                take_v(0, v)
            pool.wait_ge(zeroed, 16 * 9)
            pool.wait_ge(pre["dve"], DVE_PLACES)
            for i in range(NI):
                scatter(0, i)
            with pool.Fori(0, B - 1) as b:
                for i in range(NI):
                    if i + 1 < NI:
                        inverse_deviation(b + 1, i + 1)
                    scatter(b + 1, i)
                for i in range(NI):
                    low_k(b + 1, i)
                take_v(b + 1, 0)
                work_wait(pool, work_full, body_part(b), ("qb", H - 1))
                pool.sem_inc(passed, 1)
                for i in range(NI):
                    low_q(b + 1, i)
                inverse_deviation(b + 2, 0)
                pool.wait_ge(o_full, b * H + H)
                pool.sem_inc(passed, 1)
                take_v(b + 1, 1)
            pool.wait_ge(route_pos, 2)
            for g in range(NT):
                for m in range(TOPK):
                    pool.indirect_dma_start(
                        out=pair_d, out_offset=bass.IndirectOffsetOnAxis(ap=posi[:, m, g:g + 1], axis=0),
                        in_=prow[:, g, m, :], in_offset=None).then_inc(pairs_out, 16)
            pool.wait_ge(lists_made, LISTS)
            pool.wait_ge(ao_made, B * H)
            with pool.Fori(0, NJ // 4) as q:
                for k in range(4):
                    pool.wait_ge(xg_read, q * 4 + (k + 1))
                    pool.tensor_copy(GI[k][:], TLI[:, bass.ds(q * 4 + k, 1)]).then_inc(gi_made, 1)
                    pool.wait_ge(gi_made, q * 4 + (k + 1))
                    pool.sem_inc(passed, 1)
                    pool.indirect_dma_start(
                        out=XG[k][:], out_offset=None, in_=xn_d,
                        in_offset=bass.IndirectOffsetOnAxis(ap=GI[k][:, 0:1], axis=0)).then_inc(xg_in[k], 16)
            for k in range(2):
                pool.wait_ge(y_out[k], 16 * (NJ // 2 + 1))
            with pool.Fori(0, NT // 2) as q:
                for k in range(2):
                    pool.wait_ge(z_made, q * 2 + (k + 1))
                    for m in range(TOPK):
                        pool.tensor_copy(FI[k][m][:], posi[:, m, bass.ds(q * 2 + k, 1)]).then_inc(fi_made, 1)
                    pool.wait_ge(fi_made, q * 4 + 2 * (k + 1))
                    pool.sem_inc(passed, 1)
                    for m in range(TOPK):
                        pool.indirect_dma_start(
                            out=FY[k][m][:], out_offset=None, in_=y_d,
                            in_offset=bass.IndirectOffsetOnAxis(ap=FI[k][m][:, 0:1], axis=0)).then_inc(fy_in[k], 16)

        @block.tensor
        def _(pe):
            def tr(dst, src, rows=P):
                return pe.transpose(dst, src, ident[0:rows, 0:rows])

            def transpose_x(part, n, i):
                name = ("xt", i)
                pe.wait_ge(xn_made, n * NI + (i + 1))
                work_wait(pe, work_free, part, name)
                for c in range(NC):
                    last = tr(wbank(part, name)[:, c * P:(c + 1) * P], XN[i % 2][:, c * P:(c + 1) * P])
                last.then_inc(wsem(part, name, work_full), 1)

            def project(part, i):
                name = ("p", i)
                work_emptied(pe, part, ("xt", i))
                pair_wait(pe, pair_free, part, name)
                dst = pbank(part, name)
                for c in range(NC):
                    pe.matmul(dst[:, 0, :], XT[i % 2][:, c, :], WX[:, c, 0:512],
                              start=c == 0, stop=c == NC - 1)
                for c in range(NC):
                    last = pe.matmul(dst[:, 1, 0:WCOLS - 512], XT[i % 2][:, c, :], WX[:, c, 512:WCOLS],
                                     start=c == 0, stop=c == NC - 1)
                last.then_inc(psem(part, name, pair_full), 1)

            def to_rows(part, name, cols, rows):
                work_wait(pe, work_free, part, name)
                for i in range(NI):
                    last = tr(wbank(part, name)[0:rows, i * P:(i + 1) * P], cols(i))
                last.then_inc(wsem(part, name, work_full), 1)

            def k_rows(part, n, v):
                pe.wait_ge(klo_made, n * NI + NI)
                to_rows(part, ("kt", v), lambda i: KHL[:, i, v, :, :].rearrange("p a d -> p (a d)"), P)

            def geo_k_rows(part, n):
                pe.wait_ge(geo_cols, n * 2 + 2)
                to_rows(part, ("tk",), lambda i: TK[:, i, :], 72)

            def geo_q_rows(part):
                to_rows(part, ("tq",), lambda i: TQ[:, i, :], 72)

            def q_rows(part, n, h):
                if h == 0:
                    pe.wait_ge(qhi_made, n * NI + NI)
                to_rows(part, ("qa", h), lambda i: QH[:, i, h, :, :].rearrange("p a d -> p (a d)"), P)

            def first_scores(part, h, i):
                name = ("qm", h, i)
                n = P * (i + 1)
                if i == 0:
                    work_emptied(pe, part, ("qa", h))
                    if h == 0:
                        work_emptied(pe, part, ("kt", 0))
                work_wait(pe, work_free, part, name)
                pe.matmul(wbank(part, name)[:, 0:n], QA[h % 4][:, i * P:(i + 1) * P], KA[:, h // REP, 0:n],
                          start=True, stop=False)
                pe.matmul(wbank(part, name)[:, n - P:n], identb[:], maskN[:], start=False, stop=True) \
                    .then_inc(wsem(part, name, work_full), 1)

            def rest_rows(part, n, h):
                if h == 0:
                    pe.wait_ge(qlo_made, n * NI + NI)
                pe.wait_ge(nmax_made, n * H + (h + 1))
                to_rows(part, ("qb", h), lambda i: QL[:, i, h, :], QROWS)

            def scores(part, n, h, j):
                name = ("s", h, j)
                w = T - P * j
                v = h // REP
                if j == 0:
                    work_emptied(pe, part, ("qb", h))
                    pe.wait_ge(kg_made, n * H + (h + 1))
                    if h == 0:
                        pe.wait_ge(qg_made, n * 3 + 3)
                pair_wait(pe, pair_free, part, name)
                dst = pbank(part, name)
                st = slice(j * P, (j + 1) * P)
                pe.matmul(dst[:, 0, 0:w], KA[:, v, st], QA[h % 4][:, j * P:T], start=True, stop=False)
                pe.matmul(dst[:, 0, 0:w], KB[:, v, st], QB[h % 2][:, j * P:T], start=False, stop=False)
                pe.matmul(dst[:, 0, 0:P], identb[:], maskT[:], start=False, stop=True)
                pe.matmul(dst[:, 1, 0:w], KG[h % 2][:, st], QG[:, j * P:T], start=True, stop=False)
                pe.matmul(dst[:, 1, 0:P], identb[:], maskT[:], start=False, stop=True) \
                    .then_inc(psem(part, name, pair_full), 1)

            def values(part, b, h, i):
                if i == 0:
                    pe.wait_ge(o_free, b * H + (h + 1))
                if h == 0 and i == 0:
                    pe.wait_ge(v_made, b * KVH + 1)
                if h == REP and i == 0:
                    pe.wait_ge(v_made, b * KVH + 2)
                if h == 0 and i < 2:
                    u = START_PAIR.index(("s", 0, i))
                    pe.wait_ge(pair_free[u % 2], b * (NPAIR // 2) + (u // 2 + 2))
                else:
                    pair_emptied(pe, part, ("s", h, i))
                for m in range(2):
                    for j in range(i + 1):
                        o = SOFF[j] + P * (i - j)
                        last = pe.matmul(O[:, m, i * (DH + 1):(i + 1) * (DH + 1)],
                                         PT[h % 2][:, m, o:o + P], V[:, j, h // REP, :],
                                         start=j == 0, stop=j == i)
                if i == NI - 1:
                    last.then_inc(o_full, 1)

            def heads(part, b, full):
                for h in range(H):
                    more, most = full or h + 1 < H, full or h + 2 < H
                    n1, h1 = (b, h + 1) if h + 1 < H else (b + 1, h + 1 - H)
                    n2, h2 = (b, h + 2) if h + 2 < H else (b + 1, h + 2 - H)
                    if more:
                        rest_rows(part, n1, h1)
                    if full and h == H - 2:
                        k_rows(part, b + 1, 0)
                    scores(part, b, h, 2)
                    values(part, b, h, 0)
                    if most:
                        q_rows(part, n2, h2)
                    values(part, b, h, 1)
                    scores(part, b, h, 3)
                    if full and h < NI:
                        transpose_x(part, b + 1, h)
                    if most:
                        first_scores(part, h2, 0)
                        first_scores(part, h2, 1)
                    if full and 1 <= h <= NI:
                        project(part, h - 1)
                    else:
                        values(part, b, h, 2)
                    if not full and h == ROUTE_STEP:
                        route_counts(part)
                    if most:
                        first_scores(part, h2, 2)
                        first_scores(part, h2, 3)
                    if full and h == H - 1:
                        k_rows(part, b + 1, 1)
                    if full and 1 <= h <= NI:
                        values(part, b, h, 2)
                    if more and h + 1 < H:
                        scores(part, n1, h1, 0)
                    values(part, b, h, 3)
                    if full and h == H - 3:
                        geo_k_rows(part, b + 1)
                        geo_q_rows(part)
                    if more and h + 1 == H:
                        scores(part, n1, h1, 0)
                    if more:
                        scores(part, n1, h1, 1)

            def route_counts(part):
                name = ("route",)
                pe.wait_ge(route_cs, 1)
                work_wait(pe, work_free, part, name)
                cs = CS[:].rearrange("p g e -> p (g e)")
                pe.matmul(wbank(part, name)[:, 0:NT * E], before[:], cs, start=True, stop=True)
                pe.matmul(wbank(part, name)[:, NT * E:2 * NT * E], ones_row[:], cs, start=True, stop=True) \
                    .then_inc(wsem(part, name, work_full), 1)

            pe.wait_ge(early_in, 16 * 4)
            pe.wait_ge(pre["dve"], DVE_SLOTS)
            tr(pair[1][:, 1, 0:NSC], idx_t[:, 1, :].bitcast(F32), NSC).then_inc(pre["pe"], 1)
            pe.wait_ge(pre["dve"], DVE_SOFTMAX)
            tr(pair[0][0:A, 0, 0:E], eaw[:], E).then_inc(pre["pe"], 1)
            pe.wait_ge(weights_in, 16 * 4)
            pe.wait_ge(pre["dve"], DVE_SOFTMAX + 1)
            for k in range(NC):
                last = tr(pair[1][:, 1, 64 + k * E:64 + (k + 1) * E], gw[:, k * P:(k + 1) * P], E)
            last.then_inc(pre["pe"], 1)
            transpose_x(START, 0, 0)
            pe.wait_ge(consts_in, 16 * 7)
            for n in range(NSC):
                last = pe.transpose(O[:, 0, n * E:(n + 1) * E], imp_sb[:, n * P:(n + 1) * P], ident[A:A + E, A:A + E])
            last.then_inc(pre["pe"], 1)
            transpose_x(START, 0, 1)
            pe.wait_ge(pre["dve"], DVE_WEIGHTS)
            pe.wait_ge(pre["act"], ACT_AWT)
            project(START, 0)
            for n in range(NSC):
                last = pe.matmul(O[:, 1, n * E:(n + 1) * E], at_sb[:, n * P:(n + 1) * P], awT[:],
                                 start=True, stop=True)
            last.then_inc(pre["pe"], 1)
            transpose_x(START, 0, 2)
            project(START, 1)
            pe.wait_ge(pre["dve"], DVE_VALUES)
            for n in range(NSC):
                m, o = n // (NSC // 2), n % (NSC // 2) * 3 * E
                last = pe.matmul(O[:, m, o:o + 3 * E], EQ[:, n * P:(n + 1) * P],
                                 UPR[:, n, :, :].rearrange("p a e -> p (a e)"), start=True, stop=True)
            last.then_inc(pre["pe"], 1)
            transpose_x(START, 0, 3)
            project(START, 2)
            pe.wait_ge(pre["dve"], DVE_EARLIER)
            pe.wait_ge(fills, FILLS)
            for n in range(NSC):
                last = pe.matmul(O[:, 1, n:n + 1], EQB[:, n * P:(n + 1) * P], ones_row[:, 0:1], start=True, stop=True)
            last.then_inc(pre["pe"], 1)
            project(START, 3)
            pe.wait_ge(late_in, 16 * 2)
            for k in range(NC):
                work_wait(pe, work_free, START, ("w", k))
                for r in range(NC):
                    last = tr(wbank(START, ("w", k))[:, r * P:(r + 1) * P], WF[:, r, k * P:(k + 1) * P])
                last.then_inc(wsem(START, ("w", k), work_full), 1)
            geo_k_rows(START, 0)
            geo_q_rows(START)
            for v in range(KVH):
                k_rows(START, 0, v)
            q_rows(START, 0, 0)
            q_rows(START, 0, 1)
            for i in range(NI):
                first_scores(START, 0, i)
            rest_rows(START, 0, 0)
            for i in range(NI):
                first_scores(START, 1, i)
            scores(START, 0, 0, 0)
            scores(START, 0, 0, 1)

            with pe.Fori(0, B - 1) as b:
                heads(body_part(b), b, True)
            heads(LAST, B - 1, False)

            pe.wait_ge(pairs_in, 16)
            for k in range(2):
                pe.wait_ge(work_free[k], ALL_WORK[k] + 1)
            tr(work[0][:, 0:NJ], PL[:, :, 0], NJ)
            tr(work[0][:, 128:128 + NJ], PL[:, :, 1], NJ).then_inc(route_pe, 1)
            pe.wait_ge(lists_made, LISTS)
            for k in range(2):
                pe.wait_ge(pair_free[k], ALL_PAIR[k] + 1)
            pe.wait_ge(dp_made, NC)

            def gathered(q, k):
                pe.wait_ge(xg_in[k], q * 16 + 16)
                pe.wait_ge(xgt_made, q * 4 + (k + 1))
                for c in range(NC):
                    last = tr(work[k % 2][:, c * P:(c + 1) * P], XG[k][:, c * P:(c + 1) * P])
                last.then_inc(xg_read, 1)

            def expert(q, k):
                e = pe.value_load(eji[0:1, bass.ds(q * 4 + k, 1)], min_val=0, max_val=E - 1)
                pe.wait_ge(xgt_made, q * 4 + (k + 3))
                pe.wait_ge(yg_made, q * 4 + (k + 1))
                for c in range(NC):
                    last = pe.matmul(pair[k % 2][:, 0, :], XGT[k % 2][:, c, :],
                                     DPv[:, c, bass.ds(e, 1), :].rearrange("p a r -> p (a r)"),
                                     start=c == 0, stop=c == NC - 1)
                last.then_inc(y_full, 1)

            with pe.Fori(0, NJ // 4) as q:
                gathered(q, 0)
                gathered(q, 1)
                expert(q, 0)
                gathered(q, 2)
                expert(q, 1)
                gathered(q, 3)
                expert(q, 2)
                expert(q, 3)

            pe.wait_ge(xgt_made, NJ + 2)
            pe.wait_ge(yg_made, NJ + 2)
            with pe.Fori(0, NT // 2) as q:
                for k in range(2):
                    pe.wait_ge(fa_in[k], q * 16 + 16)
                    pe.wait_ge(fat_made, q * 2 + (k + 1))
                    for c in range(NC):
                        last = tr(work[k][:, c * P:(c + 1) * P], FA[k][:, c * P:(c + 1) * P])
                    last.then_inc(fa_read, 1)
                for k in range(2):
                    pe.wait_ge(fat_made, q * 2 + (k + 3))
                    pe.wait_ge(sg_made, q * 2 + (k + 1))
                    for c in range(NC):
                        last = pe.matmul(pair[k][:, 0, :], FAT[k][:, c, :], WO[:, c, :],
                                         start=c == 0, stop=c == NC - 1)
                    last.then_inc(s_full, 1)

        @block.scalar
        def _(act):
            act.sem_inc(xgt_made, 2)
            def x_columns(part, i):
                name = ("xt", i)
                work_wait(act, work_full, part, name)
                act.activation(XT[i % 2][:].rearrange("p c t -> p (c t)"), wbank(part, name)[:], ACT.Copy) \
                    .then_inc(wsem(part, name, work_free), 1)

            def leading_k(n, i):
                act.wait_ge(qk_made, n * NI + (i + 2))
                act.activation(KHL[:, i, :, 0, :].bitcast(F32R),
                               QK[:, i, QC:].rearrange("p (v d) -> p v d", v=KVH), ACT.Copy).then_inc(khi_made, 1)

            def leading_q(n, i):
                act.wait_ge(qk_made, n * NI + (i + 2))
                act.activation(QH[:, i, :, :, :].bitcast(F32R),
                               QK[:, i, 0:QC].rearrange("p (h d) -> p h d", h=H).unsqueeze(2)
                               .broadcast_to((P, H, 2, DH)), ACT.Copy).then_inc(qhi_made, 1)

            def rows(part, name, dst, n):
                work_wait(act, work_full, part, name)
                act.activation(dst, wbank(part, name)[0:n, :], ACT.Copy) \
                    .then_inc(wsem(part, name, work_free), 1)

            def k_copies(part, v):
                name = ("kt", v)
                work_wait(act, work_full, part, name)
                act.activation(KA[:, v, :], wbank(part, name)[:], ACT.Copy)
                act.activation(KB[0:DH, v, :], wbank(part, name)[0:DH, :], ACT.Copy) \
                    .then_inc(wsem(part, name, work_free), 1)

            def exps(part, h, j):
                name = ("s", h, j)
                w = T - P * j
                pair_wait(act, pair_full, part, name)
                act.activation(PT[h % 2][:, :, SOFF[j]:SOFF[j] + w], pbank(part, name)[:, :, 0:w], ACT.Exp) \
                    .then_inc(psem(part, name, pair_free), 1)

            def heads(part, b, full):
                for h in range(H):
                    more, most = full or h + 1 < H, full or h + 2 < H
                    h1, h2 = (h + 1) % H, (h + 2) % H
                    if more:
                        rows(part, ("qb", h1), QB[h1 % 2][:], QROWS)
                    if full and h == H - 2:
                        k_copies(part, 0)
                    exps(part, h, 2)
                    if most:
                        rows(part, ("qa", h2), QA[h2 % 4][:], P)
                    exps(part, h, 3)
                    if full and h < NI:
                        x_columns(part, h)
                    if full and 2 <= h < NI + 2:
                        leading_k(b + 1, h - 2)
                    if full and h == H - 1:
                        k_copies(part, 1)
                    if not full and h == ROUTE_STEP:
                        act.wait_ge(route_act, 1)
                        act.activation(gates[:, 0, :], gates[:, 1, :], ACT.Exp).then_inc(route_act, 1)
                    if more:
                        exps(part, h1, 0)
                    if full and h == H - 3:
                        for i in range(NI):
                            leading_q(b + 1, i)
                    if more:
                        exps(part, h1, 1)

            act.wait_ge(pre["dve"], DVE_SOFTMAX - 2)
            act.activation(eaw[:], eaw[:], ACT.Exp, bias=est[:, 1:2], accum_out=est[:, 2:3]).then_inc(pre["act"], 1)
            act.wait_ge(pre["pe"], PE_AWT)
            act.activation(awT[:], pair[0][0:A, 0, 0:E], ACT.Copy).then_inc(pre["act"], 1)
            x_columns(START, 0)
            act.wait_ge(pre["pe"], PE_IMP)
            act.activation(SIG, O[:, 0, 0:NSC * E], ACT.Exp, scale=-1.0).then_inc(pre["act"], 1)
            x_columns(START, 1)
            x_columns(START, 2)
            leading_q(0, 0)
            x_columns(START, 3)
            leading_q(0, 1)
            leading_k(0, 0)
            leading_k(0, 1)
            leading_q(0, 2)
            leading_k(0, 2)
            leading_q(0, 3)
            leading_k(0, 3)
            for k in range(NC):
                work_wait(act, work_full, START, ("w", k))
                act.activation(WT[:, k, :], wbank(START, ("w", k))[:], ACT.Copy) \
                    .then_inc(wsem(START, ("w", k), work_free), 1)
            for v in range(KVH):
                k_copies(START, v)
            rows(START, ("qa", 0), QA[0][:], P)
            rows(START, ("qa", 1), QA[1][:], P)
            rows(START, ("qb", 0), QB[0][:], QROWS)
            act.wait_ge(zeroed, 16 * 9)
            exps(START, 0, 0)
            exps(START, 0, 1)
            with act.Fori(0, B - 1) as b:
                heads(body_part(b), b, True)
            heads(LAST, B - 1, False)

            act.wait_ge(lists_made, LISTS)
            with act.Fori(0, NJ // 4) as q:
                for k in range(4):
                    act.wait_ge(xg_read, q * 4 + (k + 5))
                    act.activation(XGT[k % 2][:].rearrange("p c t -> p (c t)"), work[k % 2][:], ACT.Copy) \
                        .then_inc(xgt_made, 1)
            act.sem_inc(fat_made, 2)
            with act.Fori(0, NT // 2) as q:
                for k in range(2):
                    act.wait_ge(fa_read, q * 2 + (k + 1))
                    act.activation(FAT[k][:].rearrange("p c t -> p (c t)"), work[k][:], ACT.Copy) \
                        .then_inc(fat_made, 1)
                for k in range(2):
                    act.wait_ge(z_made, q * 2 + (k + 3))
                    act.activation(FO[k][:], FO[k][:], ACT.Silu).then_inc(g_made, 1)

        @block.vector
        def _(dve):
            for s_, n in ((work_free[0], 1), (work_free[1], 1), (pair_free[0], 1), (pair_free[1], 1), (o_free, 1), (qk_made, 1),
                          (xn_out[0], 16), (xn_out[1], 16), (ao_out, 16), (sg_made, 2),
                          (yg_made, 2), (y_out[0], 16), (y_out[1], 16), (out_out[0], 16), (out_out[1], 16)):
                dve.sem_inc(s_, n)
            count = [0]

            def step(ins):
                count[0] += 1
                ins.then_inc(pre["dve"], 1)
                dve.wait_ge(pre["dve"], count[0])

            def stats(slot, arrived, n):
                dve.wait_ge(x_in[slot], arrived)
                dve.bn_stats(bst[:], X[slot][:]).then_inc(bst_made, 1)
                dve.wait_ge(bst_made, n)
                dve.sem_inc(passed, 1)
                dve.bn_aggr(mv[slot][:], bst[:]).then_inc(mv_made, 1)
                dve.wait_ge(mv_made, n)
                dve.tensor_scalar(veps[slot][:], mv[slot][:, 1:2], EPS, None, ALU.add).then_inc(stats_made, 1)

            def normalise(n, i):
                dve.wait_ge(rstd_made, n * NI + (i + 1))
                dve.wait_ge(xn_out[i % 2], n * (8 * NI) + 16 * (i // 2 + 1))
                dve.tensor_scalar(XN[i % 2][:], X[i % 2][:], mv[i % 2][:, 0:1], rstd[i % 2][:, 0:1],
                                  ALU.subtract, ALU.mult).then_inc(xn_made, 1)
                nxt = i + 1
                dve.wait_ge(xn_made, n * NI + (i + 1))
                dve.wait_ge(stats_made, n * NI + (i + 1))
                stats(nxt % 2, n * (8 * NI) + 16 * (nxt // 2 + 1), n * NI + (nxt + 1))

            def rotate(part, n, i):
                name = ("p", i)
                pair_wait(dve, pair_full, part, name)
                flat = pbank(part, name)[:].rearrange("p a n -> p (a n)")
                qk = flat[:, 0:QC + KC].rearrange("p (h d) -> p h d", d=DH)

                def table(a, lo, hi):
                    return rope[:, a, i, lo:hi].unsqueeze(1).broadcast_to((P, H + KVH, hi - lo))

                dve.wait_ge(qk_made, n * NI + (i + 1))
                if i == 0 and not isinstance(n, int):
                    dve.wait_ge(v_made, n * KVH)
                dve.tensor_tensor(rt1[:], qk, table(0, 0, DH), op=ALU.mult).then_inc(rope_parts, 1)
                dve.tensor_tensor(rt2[:, :, 0:HALF], qk[:, :, HALF:DH], table(1, 0, HALF),
                                  op=ALU.mult).then_inc(rope_parts, 1)
                dve.tensor_tensor(rt2[:, :, HALF:DH], qk[:, :, 0:HALF], table(1, HALF, DH),
                                  op=ALU.mult).then_inc(rope_parts, 1)
                dve.tensor_copy(VN[:, i, :, :],
                                flat[:, QC + KC:QC + 2 * KC].rearrange("p (v d) -> p v d", v=KVH))
                dve.tensor_scalar(LG[:, i, :], flat[:, WCOLS - E:WCOLS], 50.0, -50.0, ALU.min, ALU.max) \
                    .then_inc(psem(part, name, pair_free), 1)
                dve.wait_ge(rope_parts, n * (3 * NI) + 3 * (i + 1))
                dve.tensor_tensor(QK[:, i, :].rearrange("p (h d) -> p h d", d=DH), rt1[:], rt2[:],
                                  op=ALU.add).then_inc(qk_made, 1)

            def geo_columns(n):
                dve.wait_ge(qk_made, n * NI + (NI + 1))
                GA = 9
                q3 = QK[:, :, 0:QC].rearrange("p i (h d) -> p i h d", d=DH)[:, :, :, 0:3]
                dve.tensor_tensor(gt[0][:], q3, dirs[:, 1, :, :].unsqueeze(1).broadcast_to((P, NI, H, 3)),
                                  op=ALU.mult).then_inc(geo_a, 1)
                for v in range(KVH):
                    k3 = QK[:, :, QC + v * DH:QC + v * DH + 3].unsqueeze(2).broadcast_to((P, NI, REP, 3))
                    dve.tensor_tensor(gt[1][:, :, v * REP:(v + 1) * REP, :], k3,
                                      dirs[:, 0, v * REP:(v + 1) * REP, :].unsqueeze(1)
                                      .broadcast_to((P, NI, REP, 3)), op=ALU.mult).then_inc(geo_a, 1)
                dve.wait_ge(geo_a, n * GA + 3)
                dve.reduce_sum(TQ[:, :, 64:72], gt[0][:], AX).then_inc(geo_a, 1)
                dve.reduce_sum(TK[:, :, 64:72], gt[1][:], AX).then_inc(geo_a, 1)
                dve.wait_ge(geo_a, n * GA + 5)
                for t, two in ((TQ, 8), (TK, 16)):
                    dve.tensor_copy(t[:, :, 0:8].bitcast(F32R), t[:, :, 64:72]).then_inc(geo_a, 1)
                    dve.tensor_copy(t[:, :, two:two + 8].bitcast(F32R), t[:, :, 64:72]).then_inc(geo_a, 1)
                dve.wait_ge(geo_a, n * GA + 9)
                for t, rest in ((TQ, 16), (TK, 8)):
                    dve.tensor_tensor(t[:, :, rest:rest + 8], t[:, :, 64:72], t[:, :, 0:8],
                                      op=ALU.subtract).then_inc(geo_cols, 1)

            def geo_take(part, n):
                if not isinstance(n, int):
                    dve.wait_ge(kr_made, n)
                    dve.wait_ge(qg_made, n * 3)
                for name, rows_ in (("tk", kpr), ("tq", qpr)):
                    work_wait(dve, work_full, part, (name,))
                    dve.tensor_copy(rows_[:], wbank(part, (name,))[0:72, :]) \
                        .then_inc(wsem(part, (name,), work_free), 1)
                work_emptied(dve, part, ("tk",))
                work_emptied(dve, part, ("tq",))

            def geo_extremes(n):
                dve.tensor_tensor_scan(cmx[64:72, :], kpr[64:72, :], kpr[64:72, :], -3e38, ALU.max, ALU.max) \
                    .then_inc(cum_made, 1)
                dve.tensor_tensor_scan(cmn[64:72, :], kpr[64:72, :], kpr[64:72, :], 3e38, ALU.min, ALU.min) \
                    .then_inc(cum_made, 1)

            def geo_maxima(n):
                dve.wait_ge(cum_made, n * 2 + 2)
                dve.tensor_tensor(cmx[64:72, :], cmx[64:72, :], qpr[64:72, :], op=ALU.mult).then_inc(geo_b, 1)
                dve.tensor_tensor(cmn[64:72, :], cmn[64:72, :], qpr[64:72, :], op=ALU.mult).then_inc(geo_b, 1)
                dve.wait_ge(geo_b, n * 2 + 2)
                dve.tensor_tensor(cmx[64:72, :], cmx[64:72, :], cmn[64:72, :], op=ALU.max).then_inc(geo_max, 1)

            def geo_k(n):
                if not isinstance(n, int):
                    dve.wait_ge(kg_made, n * H)
                dve.tensor_copy(KR[0:24, :], kpr[0:24, :]).then_inc(kr_made, 1)

            def geo_q(n):
                dve.wait_ge(geo_max, n + 1)
                dve.tensor_copy(QG[0:24, :], qpr[0:24, :]).then_inc(qg_made, 1)
                dve.tensor_scalar(QG[64:72, :], cmx[64:72, :], -1.0, None, ALU.mult).then_inc(qg_made, 1)
                dve.wait_ge(qg_made, n * 3 + 2)
                dve.scalar_tensor_tensor(QG[96:104, :], cmx[64:72, :], -1.0, QG[64:72, :].bitcast(F32),
                                         ALU.mult, ALU.subtract).then_inc(qg_made, 1)

            def geo_rows(n, h):
                if h == 0:
                    dve.wait_ge(kr_made, n + 1)
                dve.tensor_scalar(KG[h % 2][:], KR[:], onehot[0:GROWS, h:h + 1], None, ALU.mult) \
                    .then_inc(kg_made, 1)

            def row_max(part, h, i):
                name = ("qm", h, i)
                work_wait(dve, work_full, part, name)
                dve.reduce_max(M[:, h, i:i + 1], wbank(part, name)[:, 0:P * (i + 1)], AX) \
                    .then_inc(wsem(part, name, work_free), 1)

            def minus_max(part, n, h):
                work_emptied(dve, part, ("qm", h, NI - 2))
                work_emptied(dve, part, ("qm", h, NI - 1))
                dve.tensor_scalar(QL[:, :, h, DH].bitcast(F32R), M[:, h, :], -1.0, None, ALU.mult) \
                    .then_inc(nmax_hi, 1)
                dve.wait_ge(nmax_hi, n * H + (h + 1))
                dve.scalar_tensor_tensor(QL[:, :, h, DH + 1], M[:, h, :], -1.0, QL[:, :, h, DH],
                                         ALU.mult, ALU.subtract).then_inc(nmax_made, 1)

            def mix(b, h):
                if h == 0:
                    dve.wait_ge(ao_out, b * 16 + 16)
                dve.wait_ge(o_full, b * H + (h + 1))
                oh = O[:, :, 0:NI * (DH + 1)].rearrange("p m (i d) -> p m i d", d=DH + 1)
                dve.reciprocal(rl[:], oh[:, :, :, DH]).then_inc(rl_made, 1)
                dve.wait_ge(rl_made, b * H + (h + 1))
                dve.tensor_tensor(ab[:], rl[:], hs[:, :, h].unsqueeze(2).broadcast_to((P, 2, NI)),
                                  op=ALU.mult).then_inc(ab_made, 1)
                dve.wait_ge(ab_made, b * H + (h + 1))
                if h >= 1:
                    dve.wait_ge(ao_made, b * H + h)
                dve.tensor_tensor(ow[:], oh[:, :, :, 0:DH], ab[:].unsqueeze(3).broadcast_to((P, 2, NI, DH)),
                                  op=ALU.mult).then_inc(o_free, 1)
                dve.wait_ge(o_free, b * H + (h + 2))
                dve.tensor_tensor(AO[:, :, h * DH:(h + 1) * DH], ow[:, 0, :, :], ow[:, 1, :, :],
                                  op=ALU.add).then_inc(ao_made, 1)

            rc = [0]

            def route(ins):
                rc[0] += 1
                ins.then_inc(routing, 1)
                dve.wait_ge(routing, rc[0])

            def choose(n):
                dve.wait_ge(qk_made, n * NI + (NI + 1))
                dve.sem_inc(passed, 1)
                for i in range(NI):
                    last = dve.max(MXB[:, i, :], LG[:, i, :])
                last.then_inc(top_made, 1)
                dve.wait_ge(top_made, n * 3 + 1)
                dve.sem_inc(passed, 1)
                for i in range(NI):
                    last = dve.max_index(IXB[:, i, :], MXB[:, i, :], LG[:, i, :])
                last.then_inc(top_made, 1)
                dve.wait_ge(top_made, n * 3 + 2)
                at_ = slice(n * NI, n * NI + NI) if isinstance(n, int) else bass.ds(n * NI, NI)
                dve.tensor_copy(MX[:, at_, :], MXB[:])
                dve.tensor_copy(IX[:, at_, :], IXB[:]).then_inc(top_made, 1)

            def gate_parts():
                for k in range(2):
                    dve.wait_ge(xn_out[k], 16 * (NT // 2 + 1))
                    dve.wait_ge(x_in[k], 16 * (NT // 2 + 1))
                dve.wait_ge(top_made, 3 * B)
                dve.tensor_tensor(gates[:, 1, :], MX[:, :, 1], MX[:, :, 0], op=ALU.subtract).then_inc(route_act, 1)
                enum = rows_f[:, NJ:NJ + E].unsqueeze(1).broadcast_to((P, NT, E))
                for m in range(TOPK):
                    route(dve.tensor_tensor(OH[:, m, :, :], IX[:, :, m:m + 1].broadcast_to((P, NT, E)), enum,
                                            op=ALU.is_equal))
                dve.tensor_tensor(CS[:], OH[:, 0, :, :], OH[:, 1, :, :], op=ALU.add).then_inc(route_cs, 1)
            def gate_values():
                dve.wait_ge(route_act, 2)
                route(dve.tensor_scalar(gates[:, 1, :], gates[:, 0, :], 1.0, None, ALU.add))
                route(dve.reciprocal(gates[:, 2, :], gates[:, 1, :]))
                route(dve.tensor_tensor(gates[:, 3, :], gates[:, 0, :], gates[:, 2, :], op=ALU.mult))
                for m in range(TOPK):
                    route(dve.tensor_copy(prow[:, :, m, 1], gates[:, 2 + m, :]))
                    route(dve.tensor_scalar(prow[:, :, m, 0], rows_f[:, 0:NT], rows_f[:, NJ + E:NJ + E + 1], None, ALU.add))
            def take_counts(part):
                work_wait(dve, work_full, part, ("route",))
                dve.tensor_copy(CNT[:].rearrange("p a g e -> p (a g e)"), wbank(part, ("route",))[:]) \
                    .then_inc(wsem(part, ("route",), work_free), 1)
                work_emptied(dve, part, ("route",))

            def list_places():
                route(dve.memset(ones_f[:], 1.0))
                TOT = CNT[:, 1, :, :]
                for e in range(E):
                    route(dve.tensor_tensor_scan(INC[:, :, e], ones_f[:], TOT[:, :, e], 0.0, ALU.mult, ALU.add))
                route(dve.tensor_scalar(padi[:], INC[:, NT - 1, :], float(P - 1), None, ALU.add))
                route(dve.tensor_scalar(padi[:], padi[:], -P, None, ALU.bitwise_and))
                route(dve.tensor_copy(padc[:, 0, :], padi[:]))
                route(dve.tensor_tensor_scan(padc[:, 1, :], ones_f[:, 0:E], padc[:, 0, :], 0.0, ALU.mult, ALU.add))
                route(dve.tensor_tensor(padc[:, 2, :], padc[:, 1, :], padc[:, 0, :], op=ALU.subtract))
                route(dve.tensor_tensor(BASE[:], INC[:], TOT, op=ALU.subtract))
                route(dve.tensor_tensor(BASE[:], BASE[:], padc[:, 2, :].unsqueeze(1).broadcast_to((P, NT, E)), op=ALU.add))
                route(dve.tensor_tensor(BASE[:].rearrange("p g e -> p (g e)"), CNT[:, 0, :, :].rearrange("p g e -> p (g e)"),
                                        BASE[:].rearrange("p g e -> p (g e)"), op=ALU.add))
                for m in range(TOPK):
                    route(dve.tensor_tensor(sel[:], BASE[:], OH[:, m, :, :], op=ALU.mult))
                    route(dve.reduce_sum(posf[:, m, :], sel[:], AX))
                    dve.tensor_copy(posi[:, m, :], posf[:, m, :]).then_inc(route_pos, 1)
            def tile_experts():
                route(dve.tensor_tensor(cmpj[:], rows_f[:, 0:NJ].unsqueeze(2).broadcast_to((P, NJ, E)),
                                        padc[:, 1, :].unsqueeze(1).broadcast_to((P, NJ, E)), op=ALU.is_ge))
                route(dve.reduce_sum(ejf[:], cmpj[:], AX))
                dve.tensor_scalar(eji[:], ejf[:], float(E - 1), None, ALU.min).then_inc(lists_made, 1)
            def chunk_matrix(n):
                c = DP_ORDER[n]
                dve.wait_ge(stage_in, 16 * (n + 1))
                dve.tensor_tensor(DPv[:, c, :, :], stage[:].rearrange("p r e -> p e r"),
                                  WT[:, c, :].unsqueeze(1).broadcast_to((P, E, C)), op=ALU.add).then_inc(dp_made, 1)

            def heads(part, b, full):
                for h in range(H):
                    n1, h1 = (b, h + 1) if h + 1 < H else (b + 1, h + 1 - H)
                    n2, h2 = (b, h + 2) if h + 2 < H else (b + 1, h + 2 - H)
                    if h >= 1:
                        mix(b, h - 1)
                        if full or h + 1 < H:
                            geo_rows(n1, h1)
                    if full and h == H - 2:
                        geo_k(b + 1)
                        geo_extremes(b + 1)
                    if full and h == H - 1:
                        geo_maxima(b + 1)
                    if full and h < NI:
                        normalise(b + 1, h)
                    if full and h == H - 3:
                        geo_columns(b + 1)
                        choose(b + 1)
                    if not full and h == ROUTE_STEP:
                        gate_parts()
                    if full or h + 2 < H:
                        for i in range(NI):
                            if full and 1 <= h <= NI and i == 2:
                                rotate(part, b + 1, h - 1)
                            if not full and h == ROUTE_STEP and i == 2:
                                take_counts(part)
                            if full and h == H - 1 and i == 2:
                                pair_wait(dve, pair_full, part, ("s", H - 1, NI - 1))
                                geo_q(b + 1)
                            row_max(part, h2, i)
                        minus_max(part, n2, h2)
                    if full and h == H - 3:
                        geo_take(part, b + 1)
                    if not full and h == ROUTE_STEP:
                        gate_values()
                        list_places()
                    if not full and h == ROUTE_STEP + 1:
                        tile_experts()
                    if not full and h == H - 2:
                        chunk_matrix(0)
                    if not full and h == H - 1:
                        chunk_matrix(1)
                mix(b, H - 1)
                if full:
                    geo_rows(b + 1, 1)

            dve.wait_ge(early_in, 16 * 4)
            step(dve.tensor_copy(idx_t[:, 1, :].bitcast(F32), idx_t[:, 0, :]))
            step(dve.reduce_max(est[:, 0:1], eaw[:], AX))
            step(dve.tensor_scalar(est[:, 1:2], est[:, 0:1], -1.0, None, ALU.mult))
            dve.wait_ge(pre["act"], ACT_SUM)
            step(dve.reciprocal(est[:, 3:4], est[:, 2:3]))
            step(dve.tensor_scalar(eaw[:], eaw[:], est[:, 3:4], None, ALU.mult))
            assert count[0] == DVE_SOFTMAX
            dve.wait_ge(pre["pe"], PE_SLOTS)
            step(dve.tensor_copy(idx_col[:], pair[1][:, 1, 0:NSC]))
            stats(0, 16, 1)
            step(dve.tensor_tensor(EQ.rearrange("p (n s) -> p n s", n=NSC),
                                   idx_row.rearrange("p (n s) -> p n s", n=NSC),
                                   idx_col[:].unsqueeze(2).broadcast_to((P, NSC, P)), op=ALU.is_equal))
            normalise(0, 0)
            dve.wait_ge(weights_in, 16 * 4)
            step(dve.tensor_scalar(WX[:, :, 0:QC], WX[:, :, 0:QC], DH ** -0.5, None, ALU.mult))
            dve.wait_ge(pre["pe"], PE_GATE)
            step(dve.tensor_copy(WX[:, :, WCOLS - E:WCOLS],
                                 pair[1][:, 1, 64:64 + NC * E].rearrange("p (k e) -> p k e", k=NC)))
            dve.wait_ge(consts_in, 16 * 7)
            step(dve.tensor_scalar(hs[:, 0, :], hs[:, 1, :], -1.0, 1.0, ALU.mult, ALU.add))
            step(dve.tensor_copy(identb[:], ident[:]))
            assert count[0] == DVE_WEIGHTS
            normalise(0, 1)
            dve.wait_ge(pre["act"], ACT_SIG)
            step(dve.tensor_scalar(SIG, SIG, 1.0, None, ALU.add))
            step(dve.reciprocal(SIG, SIG))
            rotate(START, 0, 0)
            normalise(0, 2)
            dve.wait_ge(pre["pe"], PE_DELTA)
            step(dve.tensor_tensor(UPD[:].rearrange("p n e -> p (n e)"), O[:, 1, 0:NSC * E], SIG, op=ALU.mult))
            rest = SIG.rearrange("p (n e) -> p n e", e=E)
            step(dve.tensor_copy(UPR[:, :, 0, :], UPD[:]))
            step(dve.tensor_tensor(rest, UPD[:], UPR[:, :, 0, :], op=ALU.subtract))
            step(dve.tensor_copy(UPR[:, :, 1, :], rest))
            step(dve.tensor_tensor(UPR[:, :, 2, :], rest, UPR[:, :, 1, :], op=ALU.subtract))
            assert count[0] == DVE_VALUES
            rotate(START, 0, 1)
            normalise(0, 3)
            dve.wait_ge(pre["pe"], PE_SUM)
            dve.wait_ge(fills, FILLS)
            for m in range(2):
                sums = O[:, m, 0:NSC // 2 * 3 * E].rearrange("p (n a e) -> p n a e", a=3, e=E)
                half = UPD[:, m * (NSC // 2):(m + 1) * (NSC // 2), :]
                step(dve.tensor_copy(half, sums[:, :, 0, :]))
                step(dve.tensor_tensor(half, half, sums[:, :, 1, :], op=ALU.add))
                step(dve.tensor_tensor(half, half, sums[:, :, 2, :], op=ALU.add))
            step(dve.tensor_tensor(EQB.rearrange("p (n s) -> p n s", n=NSC), EQ.rearrange("p (n s) -> p n s", n=NSC),
                                   before[:].unsqueeze(1).broadcast_to((P, NSC, P)), op=ALU.mult))
            assert count[0] == DVE_EARLIER
            rotate(START, 0, 2)
            step(dve.tensor_scalar(ibits[:, 0, :], idx_col[:], C - 1, C.bit_length() - 1,
                                   ALU.bitwise_and, ALU.logical_shift_left))
            step(dve.tensor_scalar(ibits[:, 1, :], idx_col[:], C.bit_length() - 1, None, ALU.logical_shift_right))
            step(dve.tensor_tensor(fcol[:, 0, :], ibits[:, 0, :], ibits[:, 1, :], op=ALU.add))
            step(dve.tensor_scalar(fcol[:, 2, :], fcol[:, 0, :], -1.0, rows_f[:, NJ + E + 1:NJ + E + 2],
                                   ALU.mult, ALU.add))
            dve.wait_ge(pre["pe"], PE_COUNT)
            step(dve.scalar_tensor_tensor(fcol[:, 3, :], O[:, 1, 0:NSC], 1.0, fcol[:, 2, :], ALU.min, ALU.mult))
            step(dve.tensor_tensor(fcol[:, 0, :], fcol[:, 0, :], fcol[:, 3, :], op=ALU.add))
            step(dve.tensor_copy(DSTI[:], fcol[:, 0, :]))
            assert count[0] == DVE_PLACES
            rotate(START, 0, NI - 1)
            choose(0)
            geo_columns(0)
            geo_take(START, 0)
            geo_extremes(0)
            geo_maxima(0)
            geo_k(0)
            geo_rows(0, 0)
            geo_q(0)
            for i in range(NI):
                row_max(START, 0, i)
            minus_max(START, 0, 0)
            geo_rows(0, 1)
            for i in range(NI):
                row_max(START, 1, i)
            minus_max(START, 0, 1)
            with dve.Fori(0, B - 1) as b:
                heads(body_part(b), b, True)
            heads(LAST, B - 1, False)
            chunk_matrix(2)
            dve.wait_ge(ao_out, 16 * (B + 1))
            chunk_matrix(3)
            dve.wait_ge(route_pe, 1)
            dve.tensor_copy(TLI[:], work[0][:, 0:NJ]).then_inc(lists_made, 1)
            dve.tensor_copy(GL[:], work[0][:, 128:128 + NJ]).then_inc(lists_made, 1)
            dve.wait_ge(lists_made, LISTS)

            with dve.Fori(0, NJ // 2) as q:
                for k in range(2):
                    dve.wait_ge(yg_made, q * 2 + (k + 1))
                    dve.tensor_copy(GG[k][:], GL[:, bass.ds(q * 2 + k, 1)]).then_inc(gg_made, 1)
                    dve.wait_ge(gg_made, q * 2 + (k + 1))
                    dve.wait_ge(y_full, q * 2 + (k + 1))
                    dve.wait_ge(y_out[k], q * 16 + 16)
                    dve.tensor_scalar(YG[k][:], pair[k][:, 0, :], GG[k][:, 0:1], None, ALU.mult).then_inc(yg_made, 1)

            with dve.Fori(0, NT // 2) as q:
                for k in range(2):
                    dve.wait_ge(fy_in[k], q * 32 + 32)
                    dve.wait_ge(out_out[k], q * 16 + 16)
                    dve.tensor_tensor(FO[k][:], FY[k][0][:], FY[k][1][:], op=ALU.add).then_inc(z_made, 1)
                for k in range(2):
                    dve.wait_ge(g_made, q * 2 + (k + 1))
                    dve.wait_ge(s_full, q * 2 + (k + 1))
                    dve.tensor_tensor(FO[k][:], FO[k][:], pair[k][:, 0, :], op=ALU.mult).then_inc(sg_made, 1)
                for k in range(2):
                    dve.wait_ge(sg_made, q * 2 + (k + 3))
                    dve.wait_ge(fx_in[k], q * 16 + 16)
                    dve.tensor_tensor(FO[k][:], FO[k][:], FX[k][:], op=ALU.add).then_inc(fo_made, 1)


_INS = ["L0_attn_x", "L0_attn_Wq", "L0_attn_Wk", "L0_attn_Wv", "L0_attn_Wo", "L0_attn_head_scales",
        "L0_ffn_gate_w", "L0_ffn_W", "L0_ffn_atoms", "L0_ffn_expert_atom_weights", "L0_ffn_importance",
        "L0_ffn_mask_idx"]


def constants():
    import numpy as np
    p = np.arange(P)
    inv = (np.float32(1.0) / (10000.0 ** (np.arange(0, DH, 2, dtype=np.float32).astype(np.float64) / DH))
           .astype(np.float32)).astype(np.float32)
    ang = (np.arange(T, dtype=np.float32)[:, None] * inv[None, :]).astype(np.float64)
    cos, sin = np.cos(ang), np.sin(ang)
    rope = np.stack([np.concatenate([cos, cos], -1), np.concatenate([-sin, sin], -1)])
    rope = rope.reshape(2, NI, P, DH).transpose(2, 0, 1, 3).reshape(P, -1).astype(np.float32)
    trig = np.array([[a, b, c] for a in (1.0, -1.0) for b in (1.0, -1.0) for c in (1.0, -1.0)], np.float32)
    dirs = (trig / np.sqrt(3.0)).astype(np.float32)
    dirs = np.broadcast_to(np.stack([dirs, dirs * np.float32(DH ** 0.5)]).reshape(1, -1), (P, 2 * H * 3))
    onehot = np.zeros((P, H), np.float32)
    for r in list(range(24)) + list(range(64, 72)) + list(range(96, 104)):
        onehot[r, r % 8] = 1.0
    rows = np.zeros((P, NJ + E + 2), np.float32)
    rows[:, 0:NJ] = P * np.arange(NJ)
    rows[:, NJ:NJ + E] = np.arange(E)
    rows[:, NJ + E] = p
    rows[:, NJ + E + 1] = C * C + p
    return {"c_ident": np.eye(P, dtype=np.float32), "c_rope": rope, "c_dirs": np.ascontiguousarray(dirs),
            "c_onehot": onehot, "c_rows": rows}


def kernel(**inputs):
    import numpy as np
    import concourse.bacc as bacc
    from concourse.bass_utils import run_bass_kernel_spmd

    nc = bacc.Bacc("TRN2", target_bir_lowering=False, num_devices=1)
    arrays, args = {}, []
    data = [(n, np.ascontiguousarray(inputs[n])) for n in _INS] + list(constants().items())
    for name, a in data:
        arrays[f"in_{name}"] = a
        args.append(nc.dram_tensor(f"in_{name}", a.shape, mybir.dt.from_np(a.dtype), kind="ExternalInput").ap())
    args.append(nc.dram_tensor("out_0", (B, T, C), F32, kind="ExternalOutput").ap())
    build(nc, *args)
    r = run_bass_kernel_spmd(nc, [arrays], core_ids=[0])
    return r.results[0]["out_0"]
```

```python
from collections import namedtuple
from contextlib import ExitStack

import concourse.bass as bass
from concourse import mybir

F32 = mybir.dt.float32
F32R = mybir.dt.float32r
BF16 = mybir.dt.bfloat16
I32 = mybir.dt.int32
U32 = mybir.dt.uint32
ALU = mybir.AluOpType
ACT = mybir.ActivationFunctionType
AX = mybir.AxisListType.X

P = 128
B, T, C = 8, 512, 512
NI = T // P
NC = C // P
NT = B * NI
H, KVH, DH = 8, 2, 64
REP = H // KVH
HALF = DH // 2
QC, KC = H * DH, KVH * DH
E, A, NS = 8, 64, 4096
NSC = NS // P
TOPK = 2
NJ = TOPK * B * T // P + E
CAP = B * T
CT = CAP // P
FS = 4
STAGES = 5
WCOLS = QC + 2 * KC + E
EPS = 1e-5
NEG = -1e30
QROWS = DH + 2
GROWS = 104
SOFF = [sum(T - P * m for m in range(j)) for j in range(NI + 1)]



def _qm(h, *tiles):
    return [("qm", h % H, i) for i in tiles]


def _s(h, *tiles):
    return [("s", h % H, j) for j in tiles]


def _head_uses(full):
    work_uses, pair_uses = [], []
    for h in range(H):
        more, most = full or h + 1 < H, full or h + 2 < H
        work_uses += [("qb", (h + 1) % H)] if more else []
        work_uses += [("kt", 0)] if full and h == H - 2 else []
        pair_uses += _s(h, 2)
        work_uses += [("qa", (h + 2) % H)] if most else []
        work_uses += [("xt", h)] if full and h < NI else []
        pair_uses += _s(h, 3)
        work_uses += _qm(h + 2, 0, 1) if most else []
        pair_uses += [("p", h - 1)] if full and 1 <= h <= NI else []
        work_uses += [("ahead",), ("total",)] if h == 0 else []
        pair_uses += _s(h + 1, 0) if more else []
        work_uses += _qm(h + 2, 2, 3) if most else []
        work_uses += [("kt", 1)] if full and h == H - 1 else []
        work_uses += [("tk",), ("tq",)] if full and h == H - 3 else []
        pair_uses += _s(h + 1, 1) if more else []
    return work_uses, pair_uses


START_WORK = [("xt", i) for i in range(NI)] + [("w", k) for k in range(NC)] + [("tk",), ("tq",), ("kt", 0), ("kt", 1), ("qa", 0), ("qa", 1)] \
    + _qm(0, 0, 1, 2, 3) + [("qb", 0)] + _qm(1, 0, 1, 2, 3)
START_PAIR = [("p", i) for i in range(NI)] + _s(0, 0, 1)
BODY_WORK, BODY_PAIR = _head_uses(True)
LAST_WORK, LAST_PAIR = _head_uses(False)
NWORK, NPAIR = len(BODY_WORK), len(BODY_PAIR)
assert NWORK % 2 == 0 and NPAIR % 2 == 0
Part = namedtuple("Part", "work pair work_ahead pair_ahead b")
START = Part(START_WORK, START_PAIR, 0, 0, 0)


def body_part(b):
    return Part(BODY_WORK, BODY_PAIR, len(START_WORK), len(START_PAIR), b)


LAST = Part(LAST_WORK, LAST_PAIR, len(START_WORK), len(START_PAIR), B - 1)
ALL_WORK = [(len(START_WORK) + (B - 1) * NWORK + len(LAST_WORK) + 1 - k) // 2 for k in range(2)]
ALL_PAIR = [(len(START_PAIR) + (B - 1) * NPAIR + len(LAST_PAIR) + 1 - k) // 2 for k in range(2)]


def build(nc, x, Wq, Wk, Wv, Wo, head_scales, gate_w, ffn_W, atoms, expert_atom_weights, importance,
          mask_idx, c_ident, c_rope, c_dirs, c_onehot, c_rows, out):
    xn_d = nc.dram_tensor("xn_d", (B * T, C), F32, kind="Internal").ap()
    ao_d = nc.dram_tensor("ao_d", (B * T, C), F32, kind="Internal").ap()
    y_d = nc.dram_tensor("y_d", (NJ * P, C), F32, kind="Internal").ap()
    pair_d = nc.dram_tensor("pair_d", ((E * CT + E) * P, 2), F32, kind="Internal").ap()
    upd_d = nc.dram_tensor("upd_d", (C * C + P, E), F32, kind="Internal").ap()

    x_f = x.rearrange("b t c -> (b t) c")
    out_f = out.rearrange("b t c -> (b t) c")

    with ExitStack() as ctx:
        def sem(name):
            return ctx.enter_context(nc.semaphore(name))

        def psum(name, shape, dt=F32):
            return ctx.enter_context(nc.psum_tensor(name, shape, dt))

        def keep(name, shape, dt=F32):
            return ctx.enter_context(nc.sbuf_tensor(name, shape, dt))

        ident = keep("ident", [P, P])
        identb = keep("identb", [P, P], BF16)
        ones_row = keep("ones_row", [P, P], BF16)
        before = keep("before", [P, P], BF16)
        rows_f = keep("rows_f", [P, NJ + 2 * E + 3])
        WT = keep("WT", [P, NC, C])
        LG = keep("LG", [P, NI, E])
        MXB = keep("MXB", [P, NI, E])
        IXB = keep("IXB", [P, NI, E], U32)
        OHB = keep("OHB", [P, NI, TOPK, E])
        CSB = keep("CSB", [P, NI, E], BF16)
        CNT = keep("CNT", [P, NI + 1, E])
        RB = keep("RB", [P, E])
        PB = keep("PB", [P, NI, E])
        selb = keep("selb", [P, NI, TOPK, E])
        posfb = keep("posfb", [P, NI, TOPK])
        posb = keep("posb", [P, NI, TOPK], I32)
        gd = keep("gd", [P, 3, NI])
        prow = keep("prow", [P, NI, TOPK, 2])
        tokn = keep("tokn", [P, NT])
        LPOS = keep("LPOS", [P, NT, TOPK])
        IX = keep("IX", [P, NT, E], U32)
        UPD = keep("UPD", [P, NSC, E])
        DSTI = keep("DSTI", [P, NSC], I32)
        whole = ExitStack()
        DP = whole.enter_context(nc.sbuf_tensor("DP", [P, NC * E * C], F32))
        whole.close()
        DPL = keep("DPL", [P, NC * E * C], F32R)
        DPLv = DPL[:].rearrange("p (c e r) -> p c e r", c=NC, e=E)
        DPv = DP[:].rearrange("p (c e r) -> p c e r", c=NC, e=E)
        idx_row = DP[:, 0:NS].bitcast(I32)
        EQ = DP[:, NS:NS + NS // 2].bitcast(BF16)
        at_sb = DP[0:A, 2 * NS:3 * NS]
        imp_sb = DP[A:A + E, 2 * NS:3 * NS]
        EQB = DP[:, 2 * NS:2 * NS + NS // 2].bitcast(BF16)
        SIG = DP[:, 3 * NS:3 * NS + NSC * E]
        WQ = DP[:, NS + NS // 2:2 * NS].rearrange("p (k n) -> p k n", k=NC)
        WKV = DP[:, 4 * NS - NC * 2 * KC:4 * NS].rearrange("p (k n) -> p k n", k=NC)
        QK_AT = 3 * NS + 512

        pair = [psum(f"pair{k}", [P, 2, 512]) for k in range(2)]
        work = [psum(f"work{k}", [P, 512]) for k in range(2)]
        O = psum("O", [P, 2, 512])

        attn = ExitStack()

        def sb(name, shape, dt=F32):
            return attn.enter_context(nc.sbuf_tensor(name, shape, dt))

        proj = ExitStack()
        top = [0]

        def pb(name, shape, dt=F32):
            n = 1
            for m in shape[1:]:
                n *= m
            top[0] += -(-n * (2 if dt == BF16 else 4) // 32) * 32
            return proj.enter_context(nc.sbuf_tensor(name, shape, dt))

        WXH = pb("WXH", [P, NC, WCOLS], F32R)
        WXL = pb("WXL", [P, NC, WCOLS], F32R)
        rope = pb("rope", [P, 2, NI, DH])
        eaw = pb("eaw", [E, A])
        est = pb("est", [E, 4])
        awT = pb("awT", [A, E])
        idx_col = pb("idx_col", [P, NSC], I32)
        ibits = pb("ibits", [P, 2, NSC], I32)
        fcol = pb("fcol", [P, 4, NSC])
        idx_t = pb("idx_t", [NSC, 2, P], I32)
        UPR = pb("UPR", [P, NSC, 3, E], BF16)
        gw = pb("gw", [E, C])
        X = [pb(f"X{k}", [P, C]) for k in range(2)]
        XN = [pb(f"XN{k}", [P, C]) for k in range(2)]
        XTH = [pb(f"XTH{k}", [P, NC, P], F32R) for k in range(2)]
        XTL = [pb(f"XTL{k}", [P, NC, P], F32R) for k in range(2)]
        bst = pb("bst", [P, 6])
        mv = [pb(f"mv{k}", [P, 2]) for k in range(2)]
        veps = [pb(f"veps{k}", [P, 1]) for k in range(2)]
        rstd = [pb(f"rstd{k}", [P, 1]) for k in range(2)]
        rt1 = pb("rt1", [P, H + KVH, DH])
        rt2 = pb("rt2", [P, H + KVH, DH])
        proj.close()
        proj_end = top[0]

        top[0] = 0

        def rb(name, shape, dt=F32):
            n = 1
            for m in shape[1:]:
                n *= m
            top[0] += -(-n * (2 if dt == BF16 else 4) // 32) * 32
            return keep(name, shape, dt)

        OH = rb("OH", [P, NT, TOPK, E])
        cnti = rb("cnti", [P, 2, E], I32)
        padc = rb("padc", [P, 5, E])
        ones_f = rb("ones_f", [P, E])
        ecol = rb("ecol", [P, 4, E])
        ec1 = rb("ec1", [P, 4])
        TIX = rb("TIX", [P, 1], I32)
        posf = rb("posf", [P, NT, TOPK])
        posi = rb("posi", [P, NT, TOPK], I32)
        cmpj = rb("cmpj", [P, NJ, E])
        ejf = rb("ejf", [P, NJ])
        eji = rb("eji", [P, NJ], I32)
        AOL = rb("AOL", [P, NI, C])
        stage = [rb(f"stage{k}", [P, P, E]) for k in range(STAGES)]
        assert top[0] <= proj_end
        keep("rest_of_proj", [P, (proj_end - top[0]) // 4])

        maskN = sb("maskN", [P, P], BF16)
        maskT = sb("maskT", [P, P], BF16)
        dirs = sb("dirs", [P, 2, H, 3])
        onehot = sb("onehot", [P, H])
        hs = sb("hs", [P, 2, H])
        mhalf = sb("mhalf", [P, 1])
        at = [0]

        def carve(*shape):
            n = 1
            for m in shape:
                n *= m
            at[0] += n
            names = "abcd"[:len(shape)]
            return DP[:, at[0] - n:at[0]].rearrange(f"p ({' '.join(names)}) -> p {' '.join(names)}",
                                                    **dict(zip(names, shape)))

        QK = DP[:, QK_AT:QK_AT + NI * (H + KVH) * DH].rearrange("p (i n) -> p i n", i=NI)
        QH = carve(NI, H, 2, DH)
        QL = carve(NI, H, QROWS)
        KHL = carve(NI, KVH, 2, DH)
        at[0] = 2 * NS
        AO = carve(NI, C)
        V = sb("V", [P, NI, KVH, DH + 1])
        VN = sb("VN", [P, NI, KVH, DH])
        gt = [sb(f"gt{k}", [P, NI, H, 3]) for k in range(2)]
        TQ = sb("TQ", [P, NI, 72])
        TK = sb("TK", [P, NI, 72])
        QA = [sb(f"QA{k}", [P, T], F32R) for k in range(4)]
        KA = sb("KA", [P, KVH, T], F32R)
        KB = sb("KB", [QROWS, KVH, T], F32R)
        QB = [sb(f"QB{k}", [QROWS, T], F32R) for k in range(2)]
        KR = sb("KR", [GROWS, T])
        kpr = sb("kpr", [72, T])
        qpr = sb("qpr", [72, T])
        cmx = sb("cmx", [72, T])
        cmn = sb("cmn", [72, T])
        QG = sb("QG", [GROWS, T], F32R)
        KG = [sb(f"KG{k}", [GROWS, T], F32R) for k in range(2)]
        M = sb("M", [P, H, NI])
        PT = [sb(f"PT{k}", [P, 2, SOFF[NI]]) for k in range(2)]
        rl = sb("rl", [P, 2, NI])
        ab = sb("ab", [P, 2, NI])
        ow = sb("ow", [P, 2, NI, DH])
        sci = [sb(f"sci{k}", [P, 1], I32) for k in range(2)]
        scv = [sb(f"scv{k}", [P, E]) for k in range(2)]
        attn.close()

        WF = PT[1][:].rearrange("p a n -> p (a n)")[:, 0:NC * C].rearrange("p (k c) -> p k c", k=NC)

        PL = cmpj[0:NJ].rearrange("j n e -> j (n e)")[:, 0:2 * P].rearrange("j (p e) -> j p e", e=2)
        TLI = keep("TLI", [P, NJ], I32)
        GL = keep("GL", [P, NJ])
        GI = [keep(f"GI{k}", [P, 1], I32) for k in range(4)]
        GG = [keep(f"GG{k}", [P, 1]) for k in range(2)]
        XG = [stage[k // 2][:].rearrange("p r e -> p (r e)")[:, k % 2 * C:(k % 2 + 1) * C] for k in range(4)]
        YG = [stage[2][:].rearrange("p r e -> p (r e)")[:, k * C:(k + 1) * C] for k in range(2)]
        XGTH = [keep(f"XGTH{k}", [P, NC, P], F32R) for k in range(2)]
        XGTL = [keep(f"XGTL{k}", [P, NC, P], F32R) for k in range(2)]
        experts = ExitStack()
        DPH = experts.enter_context(nc.sbuf_tensor("DPH", [P, NC * E * C], F32R))
        DPHv = DPH[:].rearrange("p (c e r) -> p c e r", c=NC, e=E)
        experts.close()

        WOR = AOL
        WOH = keep("WOH", [P, NC, C], F32R)
        WOL = keep("WOL", [P, NC, C], F32R)
        FI = [[keep(f"FI{k}{m}", [P, 1], I32) for m in range(TOPK)] for k in range(FS)]
        FY = [[keep(f"FY{k}{m}", [P, C]) for m in range(TOPK)] for k in range(FS)]
        FX = [keep(f"FX{k}", [P, C]) for k in range(FS)]
        FA = [keep(f"FA{k}", [P, C]) for k in range(FS)]
        FATH = [keep(f"FATH{k}", [P, NC, P], F32R) for k in range(2)]
        FATL = [keep(f"FATL{k}", [P, NC, P], F32R) for k in range(2)]
        FO = [keep(f"FO{k}", [P, C]) for k in range(FS)]

        early_in = sem("early_in")
        consts_in = sem("consts_in")
        late_in = sem("late_in")
        passed = sem("passed")
        weights_in = sem("weights_in")
        zero_made = sem("zero_made")
        zeroed = sem("zeroed")
        pre = {n: sem("pre_" + n) for n in ("pe", "act", "dve", "pool")}
        fills = sem("fills")
        x_in = [sem(f"x_in{k}") for k in range(2)]
        xn_out = [sem(f"xn_out{k}") for k in range(2)]
        ao_out = sem("ao_out")
        stats_made = sem("stats_made")
        bst_made = sem("bst_made")
        mv_made = sem("mv_made")
        rstd_made = sem("rstd_made")
        xn_made = sem("xn_made")
        xh_made = sem("xh_made")
        work_full = [sem(f"work_full{k}") for k in range(2)]
        work_free = [sem(f"work_free{k}") for k in range(2)]
        pair_full = [sem(f"pair_full{k}") for k in range(2)]
        pair_free = [sem(f"pair_free{k}") for k in range(2)]
        rope_parts = sem("rope_parts")
        top_made = sem("top_made")
        qk_made = sem("qk_made")
        v_made = sem("v_made")
        khi_made = sem("khi_made")
        klo_made = sem("klo_made")
        qhi_made = sem("qhi_made")
        qlo_made = sem("qlo_made")
        geo_a = sem("geo_a")
        geo_b = sem("geo_b")
        geo_cols = sem("geo_cols")
        cum_made = sem("cum_made")
        geo_max = sem("geo_max")
        kr_made = sem("kr_made")
        qpr_made = sem("qpr_made")
        qg_made = sem("qg_made")
        kg_made = sem("kg_made")
        nmax_hi = sem("nmax_hi")
        nmax_made = sem("nmax_made")
        o_full = sem("o_full")
        o_free = sem("o_free")
        rl_made = sem("rl_made")
        ab_made = sem("ab_made")
        ao_made = sem("ao_made")
        sc_slot = sem("sc_slot")
        scattered = sem("scattered")
        routing = sem("routing")
        route_cs = sem("route_cs")
        oh_made = sem("oh_made")
        gate_in = sem("gate_in")
        gate_out = sem("gate_out")
        places = sem("places")
        prow_made = sem("prow_made")
        tix_made = sem("tix_made")
        posi_made = sem("posi_made")
        pl_rows = sem("pl_rows")
        pairs_out = sem("pairs_out")
        pairs_in = sem("pairs_in")
        lists_made = sem("lists_made")
        stage_in = [sem(f"stage_in{k}") for k in range(STAGES)]
        dp_made = sem("dp_made")
        gi_made = sem("gi_made")
        xg_in = [sem(f"xg_in{k}") for k in range(4)]
        xg_read = sem("xg_read")
        xgh_made = sem("xgh_made")
        xgt_made = sem("xgt_made")
        dph_made = sem("dph_made")
        dpl_made = sem("dpl_made")
        wo_in = sem("wo_in")
        wo_made = sem("wo_made")
        fah_made = sem("fah_made")
        gg_made = sem("gg_made")
        yg_made = sem("yg_made")
        y_full = sem("y_full")
        y_out = [sem(f"y_out{k}") for k in range(2)]
        fi_made = sem("fi_made")
        fy_in = [sem(f"fy_in{k}") for k in range(FS)]
        fx_in = [sem(f"fx_in{k}") for k in range(FS)]
        fa_in = [sem(f"fa_in{k}") for k in range(FS)]
        fa_read = sem("fa_read")
        fat_made = sem("fat_made")
        s_full = sem("s_full")
        z_made = sem("z_made")
        g_made = sem("g_made")
        sg_made = sem("sg_made")
        fo_made = sem("fo_made")
        out_out = [sem(f"out_out{k}") for k in range(FS)]

        block = ctx.enter_context(nc.Block())

        def use(part, kind, name):
            u = (part.work.index(name) + part.work_ahead) if kind == "work" \
                else (part.pair.index(name) + part.pair_ahead)
            per_run = (NWORK if kind == "work" else NPAIR) // 2
            return u % 2, lambda more: part.b * per_run + (u // 2 + more)

        def work_wait(eng, sems, part, name):
            k, number = use(part, "work", name)
            eng.wait_ge(sems[k], number(1))

        def pair_wait(eng, sems, part, name):
            k, number = use(part, "pair", name)
            eng.wait_ge(sems[k], number(1))

        def work_emptied(eng, part, name):
            k, number = use(part, "work", name)
            eng.wait_ge(work_free[k], number(2))

        def pair_emptied(eng, part, name):
            k, number = use(part, "pair", name)
            eng.wait_ge(pair_free[k], number(2))

        def wsem(part, name, sems):
            return sems[use(part, "work", name)[0]]

        def psem(part, name, sems):
            return sems[use(part, "pair", name)[0]]

        def wbank(part, name):
            return work[use(part, "work", name)[0]]

        def pbank(part, name):
            return pair[use(part, "pair", name)[0]]

        DVE_SLOTS, DVE_SOFTMAX, DVE_WEIGHTS, DVE_VALUES, DVE_EARLIER, DVE_PLACES = 1, 5, 11, 20, 27, 34
        ACT_SUM, ACT_AWT, ACT_WEIGHTS, ACT_SIG = 1, 2, 4, 5
        PE_SLOTS, PE_AWT, PE_GATE, PE_IMP, PE_DELTA, PE_SUM, PE_COUNT = 1, 2, 3, 4, 5, 6, 7
        FILLS = 12
        DP_ORDER = [(c, r) for c in (3, 2, 0, 1) for r in range(NC)]
        LISTS = 3

        @block.sync
        def _(sp):
            for dst, src in ((ident[:], c_ident), (eaw[:], expert_atom_weights),
                             (idx_t[:, 0, :], mask_idx.rearrange("(n p) -> n p", p=P))):
                sp.dma_start(dst, src).then_inc(early_in, 16)
            sp.dma_start(X[0][:], x_f[0:P, :]).then_inc(x_in[0], 16)
            sp.dma_start(X[1][:], x_f[P:2 * P, :]).then_inc(x_in[1], 16)
            sp.dma_start(gw[:], gate_w).then_inc(weights_in, 16)
            for dst, src in ((WQ, Wq), (WKV[:, :, 0:KC], Wk), (WKV[:, :, KC:2 * KC], Wv)):
                sp.dma_start(dst, src.rearrange("(k p) n -> p k n", p=P)).then_inc(weights_in, 16)
            for dst, src in ((idx_row, mask_idx.rearrange("(a s) -> a s", a=1).broadcast_to((P, NS))),
                             (imp_sb, importance), (at_sb, atoms), (rope[:], c_rope.rearrange("p (a i d) -> p a i d", a=2, i=NI)),
                             (rows_f[:], c_rows), (hs[:, 1, :], head_scales.rearrange("(a h) -> a h", a=1).broadcast_to((P, H))),
                             (dirs[:], c_dirs.rearrange("p (a h d) -> p a h d", a=2, h=H)), (onehot[:], c_onehot)):
                sp.dma_start(dst, src).then_inc(consts_in, 16)
            sp.dma_start(WF[:], ffn_W.rearrange("(k p) c -> p k c", p=P)).then_inc(late_in, 16)
            def project_traffic(n):
                made = [sp.snap(n * NI + (i + 1)) for i in range(NI)]
                row = [sp.snap(n * T + i * P) for i in range(NI)]
                nxt = [sp.snap(((n * NI + (i + 2)) & (NT - 1)) * P) for i in range(NI)]
                for i in range(NI):
                    sp.wait_ge(xn_made, made[i])
                    sp.dma_start(xn_d[bass.ds(row[i], P), :], XN[i % 2][:]).then_inc(xn_out[i % 2], 16)
                    sp.dma_start(X[i % 2][:], x_f[bass.ds(nxt[i], P), :]).then_inc(x_in[i % 2], 16)

            zsrc = PT[0][:].rearrange("p a n -> p (a n)")[:, 0:2048]
            for i in range(NI):
                sp.wait_ge(xn_made, i + 1)
                sp.dma_start(xn_d[i * P:(i + 1) * P, :], XN[i % 2][:]).then_inc(xn_out[i % 2], 16)
                sp.dma_start(X[i % 2][:], x_f[(i + 2) * P:(i + 3) * P, :]).then_inc(x_in[i % 2], 16)
                if i == 0:
                    sp.wait_ge(zero_made, 1)
                    sp.dma_start(pair_d.rearrange("(p n) e -> p (n e)", p=P), zsrc[:, 0:(E * CT + E) * 2]) \
                        .then_inc(zeroed, 16)
                for m in (2 * i, 2 * i + 1):
                    sp.dma_start(upd_d[m * 32768:(m + 1) * 32768, :].rearrange("(p n) e -> p (n e)", p=P),
                                 zsrc).then_inc(zeroed, 16)
            with sp.Fori(0, B - 1) as b:
                ao_done = sp.snap(b * H + H)
                first = sp.snap(b * T)
                project_traffic(b + 1)
                sp.wait_ge(ao_made, ao_done)
                sp.dma_start(ao_d[bass.ds(first, T), :].rearrange("(i p) c -> p i c", p=P), AO).then_inc(ao_out, 16)

            for k in range(2):
                sp.wait_ge(xn_out[k], 16 * (NT // 2 + 1))
                sp.wait_ge(x_in[k], 16 * (NT // 2 + 1))
            sp.wait_ge(rstd_made, NT + 1)
            sp.wait_ge(scattered, 16 * NSC)
            sp.wait_ge(work_full[use(LAST, "work", ("qb", 1))[0]], use(LAST, "work", ("qb", 1))[1](1))
            for n, (c, r) in enumerate(DP_ORDER):
                if n >= STAGES:
                    sp.wait_ge(dp_made, n - STAGES + 1)
                sp.dma_start(stage[n % STAGES][:], upd_d[c * P * C:(c + 1) * P * C, :]
                             .rearrange("(p r) e -> p r e", p=P)[:, r * P:(r + 1) * P, :]) \
                    .then_inc(stage_in[n % STAGES], 16)
            sp.wait_ge(ao_made, B * H)
            sp.dma_start(ao_d[(B - 1) * T:B * T, :].rearrange("(i p) c -> p i c", p=P), AOL[:]).then_inc(ao_out, 16)

            sp.wait_ge(ao_out, 16 * (B + 1))
            sp.dma_start(WOR[:], Wo.rearrange("(k p) n -> p k n", p=P)).then_inc(wo_in, 16)

            with sp.Fori(0, NJ // 2) as q:
                made = [sp.snap(q * 2 + (k + 3)) for k in range(2)]
                row = [sp.snap(q * (2 * P) + k * P) for k in range(2)]
                for k in range(2):
                    sp.wait_ge(yg_made, made[k])
                    sp.dma_start(y_d[bass.ds(row[k], P), :], YG[k]).then_inc(y_out[k], 16)

            sp.wait_ge(yg_made, NJ + 2)
            for k in range(FS):
                sp.dma_start(FA[k][:], ao_d[k * P:(k + 1) * P, :]).then_inc(fa_in[k], 16)
                sp.dma_start(FX[k][:], x_f[k * P:(k + 1) * P, :]).then_inc(fx_in[k], 16)
            with sp.Fori(1, NT // FS) as q:
                made = [sp.snap(q * FS + (k - FS + 1)) for k in range(FS)]
                row = [sp.snap(q * (FS * P) + k * P) for k in range(FS)]
                done = [sp.snap(q * (FS * P) + (k - FS) * P) for k in range(FS)]
                for k in range(FS):
                    sp.wait_ge(fa_read, made[k])
                    sp.dma_start(FA[k][:], ao_d[bass.ds(row[k], P), :]).then_inc(fa_in[k], 16)
                    sp.wait_ge(fo_made, made[k])
                    sp.dma_start(out_f[bass.ds(done[k], P), :], FO[k][:]).then_inc(out_out[k], 16)
                    sp.dma_start(FX[k][:], x_f[bass.ds(row[k], P), :]).then_inc(fx_in[k], 16)
            for k in range(FS):
                n = NT - FS + k
                sp.wait_ge(fo_made, n + 1)
                sp.dma_start(out_f[n * P:(n + 1) * P, :], FO[k][:]).then_inc(out_out[k], 16)
            for k in range(FS):
                sp.wait_ge(out_out[k], 16 * (NT // FS + 1))

        @block.gpsimd
        def _(pool):
            def low_k(n, i):
                pool.wait_ge(khi_made, n * NI + (i + 1))
                pool.tensor_tensor(KHL[:, i, :, 1, :], QK[:, i, QC:].rearrange("p (v d) -> p v d", v=KVH),
                                   KHL[:, i, :, 0, :], op=ALU.subtract).then_inc(klo_made, 1)

            def low_q(n, i):
                pool.wait_ge(qhi_made, n * NI + (i + 1))
                pool.tensor_tensor(QL[:, i, :, 0:DH], QK[:, i, 0:QC].rearrange("p (h d) -> p h d", h=H),
                                   QH[:, i, :, 0, :],
                                   op=ALU.subtract).then_inc(qlo_made, 1)

            def inverse_deviation(n, i):
                pool.wait_ge(stats_made, n * NI + (i + 1))
                pool.tensor_tensor(rstd[i % 2][:], veps[i % 2][:], mhalf[:], op=ALU.pow).then_inc(rstd_made, 1)

            def take_v(n, v):
                pool.wait_ge(qk_made, n * NI + (NI + 1))
                pool.sem_inc(passed, 1)
                pool.tensor_copy(V[:, :, v, 0:DH], VN[:, :, v, :]).then_inc(v_made, 1)

            def scatter(b, i):
                c = b * NI + i
                if isinstance(c, int):
                    idx, val = DSTI[:, c:c + 1], UPD[:, c, :]
                else:
                    idx, val = DSTI[:, bass.ds(c, 1)], UPD[:, bass.ds(c, 1), :].rearrange("p a e -> p (a e)")
                pool.tensor_copy(sci[i % 2][:], idx).then_inc(sc_slot, 1)
                pool.tensor_copy(scv[i % 2][:], val).then_inc(sc_slot, 1)
                pool.wait_ge(sc_slot, b * (2 * NI) + 2 * (i + 1))
                pool.sem_inc(passed, 1)
                pool.indirect_dma_start(
                    out=upd_d, out_offset=bass.IndirectOffsetOnAxis(ap=sci[i % 2][:, 0:1], axis=0),
                    in_=scv[i % 2][:], in_offset=None, compute_op=ALU.add).then_inc(scattered, 16)
                pool.wait_ge(scattered, b * (NI * 16) + 16 * (i + 1))

            pool.memset(PT[0][:], 0.0).then_inc(zero_made, 1)
            for m in (maskN, maskT):
                pool.memset(m[:], 0.0).then_inc(pre["pool"], 1)
            pool.memset(before[:], 1.0).then_inc(pre["pool"], 1)
            pool.memset(KR[:], 0.0).then_inc(pre["pool"], 1)
            pool.wait_ge(pre["pool"], 4)
            pool.affine_select(out=maskN[:], in_=maskN[:], compare_op=ALU.is_ge, fill=NEG, base=0,
                               pattern=[[-1, P]], channel_multiplier=1).then_inc(fills, 1)
            pool.affine_select(out=maskT[:], in_=maskT[:], compare_op=ALU.is_ge, fill=NEG, base=0,
                               pattern=[[1, P]], channel_multiplier=-1).then_inc(fills, 1)
            pool.affine_select(out=before[:], in_=before[:], compare_op=ALU.is_gt, fill=0.0, base=0,
                               pattern=[[1, P]], channel_multiplier=-1).then_inc(fills, 1)
            for n, (dst, value) in enumerate(((KR[64:72, :], 1.0), (KR[96:104, :], 1.0), (ones_row[:], 1.0),
                               (mhalf[:], -0.5), (TQ[:], 0.0), (TK[:], 0.0), (QG[:].bitcast(F32), 0.0),
                               (V[:, :, :, DH:DH + 1], 1.0), (KB[DH:QROWS, :, :].bitcast(F32), 1.0))):
                pool.wait_ge(fills, 3 + n)
                pool.memset(dst, value).then_inc(fills, 1)
            pool.wait_ge(fills, FILLS)
            pool.sem_inc(z_made, FS)
            pool.sem_inc(xg_read, 4)

            for i in range(NI):
                inverse_deviation(0, i)
            pool.wait_ge(pre["dve"], DVE_EARLIER)
            for i in range(NI):
                low_k(0, i)
                low_q(0, i)
            inverse_deviation(1, 0)
            for v in range(KVH):
                take_v(0, v)
            pool.wait_ge(zeroed, 16 * 9)
            pool.wait_ge(pre["dve"], DVE_PLACES)
            for i in range(NI):
                scatter(0, i)
            def scatter_pairs(b):
                pool.wait_ge(prow_made, b + 1)
                pool.sem_inc(passed, 1)
                for i in range(NI):
                    for m in range(TOPK):
                        pool.indirect_dma_start(
                            out=pair_d, out_offset=bass.IndirectOffsetOnAxis(ap=posb[:, i, m:m + 1], axis=0),
                            in_=prow[:, i, m, :], in_offset=None).then_inc(pairs_out, 16)

            with pool.Fori(0, B - 1) as b:
                for i in range(NI):
                    if i + 1 < NI:
                        inverse_deviation(b + 1, i + 1)
                    scatter(b + 1, i)
                scatter_pairs(b)
                for i in range(NI):
                    low_k(b + 1, i)
                take_v(b + 1, 0)
                work_wait(pool, work_full, body_part(b), ("qb", H - 1))
                pool.sem_inc(passed, 1)
                for i in range(NI):
                    low_q(b + 1, i)
                inverse_deviation(b + 2, 0)
                pool.wait_ge(o_full, b * H + H)
                pool.sem_inc(passed, 1)
                take_v(b + 1, 1)
            scatter_pairs(B - 1)
            pool.wait_ge(tix_made, 1)
            pool.wait_ge(lists_made, 1)
            pool.wait_ge(pairs_out, 16 * TOPK * NT)
            pool.indirect_dma_start(
                out=PL.rearrange("j p e -> j (p e)"), out_offset=None, in_=pair_d.rearrange("(j p) e -> j (p e)", p=P),
                in_offset=bass.IndirectOffsetOnAxis(ap=TIX[0:NJ, 0:1], axis=0)).then_inc(pairs_in, 16)
            pool.wait_ge(dp_made, NC * NC)
            for k in range(2):
                pool.wait_ge(pair_free[k], ALL_PAIR[k] + 1)
            pool.wait_ge(ao_made, B * H)
            pool.wait_ge(lists_made, LISTS)
            with pool.Fori(0, NJ // 4) as q:
                for k in range(4):
                    pool.wait_ge(xg_read, q * 4 + (k + 1))
                    pool.tensor_copy(GI[k][:], TLI[:, bass.ds(q * 4 + k, 1)]).then_inc(gi_made, 1)
                    pool.wait_ge(gi_made, q * 4 + (k + 1))
                    pool.sem_inc(passed, 1)
                    pool.indirect_dma_start(
                        out=XG[k], out_offset=None, in_=xn_d,
                        in_offset=bass.IndirectOffsetOnAxis(ap=GI[k][:, 0:1], axis=0)).then_inc(xg_in[k], 16)
            pool.wait_ge(posi_made, 1)
            for k in range(2):
                pool.wait_ge(y_out[k], 16 * (NJ // 2 + 1))
            with pool.Fori(0, NT // FS) as q:
                for k in range(FS):
                    pool.wait_ge(z_made, q * FS + (k + 1))
                    for m in range(TOPK):
                        pool.tensor_copy(FI[k][m][:], posi[:, bass.ds(q * FS + k, 1), m]).then_inc(fi_made, 1)
                    pool.wait_ge(fi_made, q * (2 * FS) + 2 * (k + 1))
                    pool.sem_inc(passed, 1)
                    for m in range(TOPK):
                        pool.indirect_dma_start(
                            out=FY[k][m][:], out_offset=None, in_=y_d,
                            in_offset=bass.IndirectOffsetOnAxis(ap=FI[k][m][:, 0:1], axis=0)).then_inc(fy_in[k], 16)

        @block.tensor
        def _(pe):
            def tr(dst, src, rows=P):
                return pe.transpose(dst, src, ident[0:rows, 0:rows])

            def transpose_x(part, n, i):
                name = ("xt", i)
                pe.wait_ge(xn_made, n * NI + (i + 1))
                work_wait(pe, work_free, part, name)
                for c in range(NC):
                    last = tr(wbank(part, name)[:, c * P:(c + 1) * P], XN[i % 2][:, c * P:(c + 1) * P])
                last.then_inc(wsem(part, name, work_full), 1)

            def project(part, i):
                name = ("p", i)
                work_emptied(pe, part, ("xt", i))
                pair_wait(pe, pair_free, part, name)
                dst = pbank(part, name)
                for m, cols in enumerate((slice(0, 512), slice(512, WCOLS))):
                    w = cols.stop - cols.start
                    for c in range(NC):
                        pe.matmul(dst[:, m, 0:w], XTH[i % 2][:, c, :], WXH[:, c, cols], start=c == 0, stop=False)
                        pe.matmul(dst[:, m, 0:w], XTH[i % 2][:, c, :], WXL[:, c, cols], start=False, stop=False)
                        last = pe.matmul(dst[:, m, 0:w], XTL[i % 2][:, c, :], WXH[:, c, cols],
                                         start=False, stop=c == NC - 1)
                last.then_inc(psem(part, name, pair_full), 1)

            def to_rows(part, name, cols, rows):
                work_wait(pe, work_free, part, name)
                for i in range(NI):
                    last = tr(wbank(part, name)[0:rows, i * P:(i + 1) * P], cols(i))
                last.then_inc(wsem(part, name, work_full), 1)

            def k_rows(part, n, v):
                pe.wait_ge(klo_made, n * NI + NI)
                to_rows(part, ("kt", v), lambda i: KHL[:, i, v, :, :].rearrange("p a d -> p (a d)"), P)

            def geo_k_rows(part, n):
                pe.wait_ge(geo_cols, n * 2 + 2)
                to_rows(part, ("tk",), lambda i: TK[:, i, :], 72)

            def geo_q_rows(part):
                to_rows(part, ("tq",), lambda i: TQ[:, i, :], 72)

            def q_rows(part, n, h):
                if h == 0:
                    pe.wait_ge(qhi_made, n * NI + NI)
                to_rows(part, ("qa", h), lambda i: QH[:, i, h, :, :].rearrange("p a d -> p (a d)"), P)

            def first_scores(part, h, i):
                name = ("qm", h, i)
                n = P * (i + 1)
                if i == 0:
                    work_emptied(pe, part, ("qa", h))
                    if h == 0:
                        work_emptied(pe, part, ("kt", 0))
                work_wait(pe, work_free, part, name)
                pe.matmul(wbank(part, name)[:, 0:n], QA[h % 4][:, i * P:(i + 1) * P], KA[:, h // REP, 0:n],
                          start=True, stop=False)
                pe.matmul(wbank(part, name)[:, n - P:n], identb[:], maskN[:], start=False, stop=True) \
                    .then_inc(wsem(part, name, work_full), 1)

            def rest_rows(part, n, h):
                if h == 0:
                    pe.wait_ge(qlo_made, n * NI + NI)
                pe.wait_ge(nmax_made, n * H + (h + 1))
                to_rows(part, ("qb", h), lambda i: QL[:, i, h, :], QROWS)

            def scores(part, n, h, j):
                name = ("s", h, j)
                w = T - P * j
                v = h // REP
                if j == 0:
                    work_emptied(pe, part, ("qb", h))
                    pe.wait_ge(kg_made, n * H + (h + 1))
                    if h == 0:
                        pe.wait_ge(qg_made, n * 3 + 3)
                pair_wait(pe, pair_free, part, name)
                dst = pbank(part, name)
                st = slice(j * P, (j + 1) * P)
                pe.matmul(dst[:, 0, 0:w], KA[:, v, st], QA[h % 4][:, j * P:T], start=True, stop=False)
                pe.matmul(dst[:, 0, 0:w], KB[:, v, st], QB[h % 2][:, j * P:T], start=False, stop=False)
                pe.matmul(dst[:, 0, 0:P], identb[:], maskT[:], start=False, stop=True)
                pe.matmul(dst[:, 1, 0:w], KG[h % 2][:, st], QG[:, j * P:T], start=True, stop=False)
                pe.matmul(dst[:, 1, 0:P], identb[:], maskT[:], start=False, stop=True) \
                    .then_inc(psem(part, name, pair_full), 1)

            def values(part, b, h, i):
                if i == 0:
                    pe.wait_ge(o_free, b * H + (h + 1))
                if h == 0 and i == 0:
                    pe.wait_ge(v_made, b * KVH + 1)
                if h == REP and i == 0:
                    pe.wait_ge(v_made, b * KVH + 2)
                if h == 0 and i < 2:
                    u = START_PAIR.index(("s", 0, i))
                    pe.wait_ge(pair_free[u % 2], b * (NPAIR // 2) + (u // 2 + 2))
                else:
                    pair_emptied(pe, part, ("s", h, i))
                for m in range(2):
                    for j in range(i + 1):
                        o = SOFF[j] + P * (i - j)
                        last = pe.matmul(O[:, m, i * (DH + 1):(i + 1) * (DH + 1)],
                                         PT[h % 2][:, m, o:o + P], V[:, j, h // REP, :],
                                         start=j == 0, stop=j == i)
                if i == NI - 1:
                    last.then_inc(o_full, 1)

            def heads(part, b, full):
                for h in range(H):
                    more, most = full or h + 1 < H, full or h + 2 < H
                    n1, h1 = (b, h + 1) if h + 1 < H else (b + 1, h + 1 - H)
                    n2, h2 = (b, h + 2) if h + 2 < H else (b + 1, h + 2 - H)
                    if more:
                        rest_rows(part, n1, h1)
                    if full and h == H - 2:
                        k_rows(part, b + 1, 0)
                    scores(part, b, h, 2)
                    values(part, b, h, 0)
                    if most:
                        q_rows(part, n2, h2)
                    if full and h < NI:
                        transpose_x(part, b + 1, h)
                    values(part, b, h, 1)
                    scores(part, b, h, 3)
                    if most:
                        first_scores(part, h2, 0)
                        first_scores(part, h2, 1)
                    if full and 1 <= h <= NI:
                        project(part, h - 1)
                    else:
                        values(part, b, h, 2)
                    if h == 0:
                        route_counts(part, b)
                    if most:
                        first_scores(part, h2, 2)
                        first_scores(part, h2, 3)
                    if full and h == H - 1:
                        k_rows(part, b + 1, 1)
                    if full and 1 <= h <= NI:
                        values(part, b, h, 2)
                    if more and h + 1 < H:
                        scores(part, n1, h1, 0)
                    values(part, b, h, 3)
                    if full and h == H - 3:
                        geo_k_rows(part, b + 1)
                        geo_q_rows(part)
                    if more and h + 1 == H:
                        scores(part, n1, h1, 0)
                    if more:
                        scores(part, n1, h1, 1)

            def route_counts(part, b):
                pe.wait_ge(route_cs, b + 1)
                name = ("ahead",)
                work_wait(pe, work_free, part, name)
                dst = wbank(part, name)
                for i in range(NI):
                    for j in range(i):
                        pe.matmul(dst[:, i * E:(i + 1) * E], ones_row[:], CSB[:, j, :], start=j == 0, stop=False)
                    last = pe.matmul(dst[:, i * E:(i + 1) * E], before[:], CSB[:, i, :], start=i == 0, stop=True)
                last.then_inc(wsem(part, name, work_full), 1)
                name = ("total",)
                work_wait(pe, work_free, part, name)
                for j in range(NI):
                    last = pe.matmul(wbank(part, name)[:, 0:E], ones_row[:], CSB[:, j, :],
                                     start=j == 0, stop=j == NI - 1)
                last.then_inc(wsem(part, name, work_full), 1)

            pe.wait_ge(early_in, 16 * 3)
            pe.wait_ge(pre["dve"], DVE_SLOTS)
            tr(pair[1][:, 1, 0:NSC], idx_t[:, 1, :].bitcast(F32), NSC).then_inc(pre["pe"], 1)
            pe.wait_ge(pre["dve"], DVE_SOFTMAX)
            tr(pair[0][0:A, 0, 0:E], eaw[:], E).then_inc(pre["pe"], 1)
            pe.wait_ge(weights_in, 16 * 4)
            pe.wait_ge(pre["dve"], DVE_SOFTMAX + 1)
            for k in range(NC):
                last = tr(pair[1][:, 1, 64 + k * E:64 + (k + 1) * E], gw[:, k * P:(k + 1) * P], E)
            last.then_inc(pre["pe"], 1)
            transpose_x(START, 0, 0)
            transpose_x(START, 0, 1)
            pe.wait_ge(pre["dve"], DVE_WEIGHTS)
            pe.wait_ge(pre["act"], ACT_AWT)
            project(START, 0)
            pe.wait_ge(consts_in, 16 * 8)
            for n in range(NSC):
                last = pe.transpose(O[:, 0, n * E:(n + 1) * E], imp_sb[:, n * P:(n + 1) * P], ident[A:A + E, A:A + E])
            last.then_inc(pre["pe"], 1)
            for n in range(NSC):
                last = pe.matmul(O[:, 1, n * E:(n + 1) * E], at_sb[:, n * P:(n + 1) * P], awT[:],
                                 start=True, stop=True)
            last.then_inc(pre["pe"], 1)
            transpose_x(START, 0, 2)
            project(START, 1)
            pe.wait_ge(pre["dve"], DVE_VALUES)
            for n in range(NSC):
                m, o = n // (NSC // 2), n % (NSC // 2) * 3 * E
                last = pe.matmul(O[:, m, o:o + 3 * E], EQ[:, n * P:(n + 1) * P],
                                 UPR[:, n, :, :].rearrange("p a e -> p (a e)"), start=True, stop=True)
            last.then_inc(pre["pe"], 1)
            transpose_x(START, 0, 3)
            project(START, 2)
            pe.wait_ge(pre["dve"], DVE_EARLIER)
            pe.wait_ge(fills, FILLS)
            for n in range(NSC):
                last = pe.matmul(O[:, 1, n:n + 1], EQB[:, n * P:(n + 1) * P], ones_row[:, 0:1], start=True, stop=True)
            last.then_inc(pre["pe"], 1)
            project(START, 3)
            pe.wait_ge(late_in, 16)
            for k in range(NC):
                work_wait(pe, work_free, START, ("w", k))
                for r in range(NC):
                    last = tr(wbank(START, ("w", k))[:, r * P:(r + 1) * P], WF[:, r, k * P:(k + 1) * P])
                last.then_inc(wsem(START, ("w", k), work_full), 1)
            geo_k_rows(START, 0)
            geo_q_rows(START)
            for v in range(KVH):
                k_rows(START, 0, v)
            q_rows(START, 0, 0)
            q_rows(START, 0, 1)
            for i in range(NI):
                first_scores(START, 0, i)
            rest_rows(START, 0, 0)
            for i in range(NI):
                first_scores(START, 1, i)
            scores(START, 0, 0, 0)
            scores(START, 0, 0, 1)

            with pe.Fori(0, B - 1) as b:
                heads(body_part(b), b, True)
            heads(LAST, B - 1, False)

            pe.wait_ge(pairs_in, 16)
            for k in range(2):
                pe.wait_ge(work_free[k], ALL_WORK[k] + 1)
            tr(work[0][:, 0:NJ], PL[:, :, 0], NJ)
            tr(work[0][:, 128:128 + NJ], PL[:, :, 1], NJ).then_inc(pl_rows, 1)
            pe.wait_ge(lists_made, LISTS)
            for k in range(2):
                pe.wait_ge(pair_free[k], ALL_PAIR[k] + 1)

            def gathered(q, k):
                pe.wait_ge(xg_in[k], q * 16 + 16)
                pe.wait_ge(xgt_made, q * 4 + (k + 1))
                for c in range(NC):
                    last = tr(work[k % 2][:, c * P:(c + 1) * P], XG[k][:, c * P:(c + 1) * P])
                last.then_inc(xg_read, 1)

            def expert(q, k):
                j = q * 4 + k
                e = pe.value_load(eji[0:1, j:j + 1] if isinstance(j, int) else eji[0:1, bass.ds(j, 1)],
                                  min_val=0, max_val=E - 1)
                pe.wait_ge(dpl_made, e + 1)
                pe.wait_ge(xgt_made, q * 4 + (k + 3))
                pe.wait_ge(yg_made, q * 4 + (k + 1))
                for c in range(NC):
                    hi = DPHv[:, c, bass.ds(e, 1), :].rearrange("p a r -> p (a r)")
                    lo = DPLv[:, c, bass.ds(e, 1), :].rearrange("p a r -> p (a r)")
                    pe.matmul(pair[k % 2][:, 0, :], XGTH[k % 2][:, c, :], hi, start=c == 0, stop=False)
                    pe.matmul(pair[k % 2][:, 0, :], XGTH[k % 2][:, c, :], lo, start=False, stop=False)
                    last = pe.matmul(pair[k % 2][:, 0, :], XGTL[k % 2][:, c, :], hi, start=False, stop=c == NC - 1)
                last.then_inc(y_full, 1)

            gathered(0, 0)
            gathered(0, 1)
            with pe.Fori(0, NJ // 4 - 1) as q:
                for k in range(4):
                    expert(q, k)
                    gathered(*((q, k + 2) if k < 2 else (q + 1, k - 2)))
            for k in range(4):
                expert(NJ // 4 - 1, k)
                if k < 2:
                    gathered(NJ // 4 - 1, k + 2)

            pe.wait_ge(xgt_made, NJ + 2)
            pe.wait_ge(yg_made, NJ + 2)
            pe.wait_ge(wo_made, 2)

            def out_rows(q, k):
                pe.wait_ge(fa_in[k], q * 16 + 16)
                pe.wait_ge(fat_made, q * FS + (k + 1))
                for c in range(NC):
                    last = tr(work[k % 2][:, c * P:(c + 1) * P], FA[k][:, c * P:(c + 1) * P])
                last.then_inc(fa_read, 1)

            def out_project(q, k):
                pe.wait_ge(fat_made, q * FS + (k + 3))
                pe.wait_ge(sg_made, q * FS + (k + 1))
                for c in range(NC):
                    pe.matmul(pair[k % 2][:, 0, :], FATH[k % 2][:, c, :], WOH[:, c, :], start=c == 0, stop=False)
                    pe.matmul(pair[k % 2][:, 0, :], FATH[k % 2][:, c, :], WOL[:, c, :], start=False, stop=False)
                    last = pe.matmul(pair[k % 2][:, 0, :], FATL[k % 2][:, c, :], WOH[:, c, :],
                                     start=False, stop=c == NC - 1)
                last.then_inc(s_full, 1)

            out_rows(0, 0)
            with pe.Fori(0, NT // FS - 1) as q:
                for k in range(FS):
                    out_rows(*((q, k + 1) if k + 1 < FS else (q + 1, 0)))
                    out_project(q, k)
            for k in range(FS):
                if k + 1 < FS:
                    out_rows(NT // FS - 1, k + 1)
                out_project(NT // FS - 1, k)

        @block.scalar
        def _(act):
            act.sem_inc(xgt_made, 2)
            def x_columns(part, i):
                name = ("xt", i)
                work_wait(act, work_full, part, name)
                act.activation(XTH[i % 2][:].rearrange("p c t -> p (c t)"), wbank(part, name)[:], ACT.Copy) \
                    .then_inc(xh_made, 1)

            def gate_exponential(n):
                act.wait_ge(gate_in, n + 1)
                act.activation(gd[:, 1, :], gd[:, 0, :], ACT.Exp).then_inc(gate_out, 1)

            def leading_k(n, i):
                act.wait_ge(qk_made, n * NI + (i + 2))
                act.activation(KHL[:, i, :, 0, :].bitcast(F32R),
                               QK[:, i, QC:].rearrange("p (v d) -> p v d", v=KVH), ACT.Copy).then_inc(khi_made, 1)

            def leading_q(n, i):
                act.wait_ge(qk_made, n * NI + (i + 2))
                act.activation(QH[:, i, :, :, :].bitcast(F32R),
                               QK[:, i, 0:QC].rearrange("p (h d) -> p h d", h=H).unsqueeze(2)
                               .broadcast_to((P, H, 2, DH)), ACT.Copy).then_inc(qhi_made, 1)

            def rows(part, name, dst, n):
                work_wait(act, work_full, part, name)
                act.activation(dst, wbank(part, name)[0:n, :], ACT.Copy) \
                    .then_inc(wsem(part, name, work_free), 1)

            def k_copies(part, v):
                name = ("kt", v)
                work_wait(act, work_full, part, name)
                act.activation(KA[:, v, :], wbank(part, name)[:], ACT.Copy)
                act.activation(KB[0:DH, v, :], wbank(part, name)[0:DH, :], ACT.Copy) \
                    .then_inc(wsem(part, name, work_free), 1)

            def exps(part, h, j):
                name = ("s", h, j)
                w = T - P * j
                pair_wait(act, pair_full, part, name)
                act.activation(PT[h % 2][:, :, SOFF[j]:SOFF[j] + w], pbank(part, name)[:, :, 0:w], ACT.Exp) \
                    .then_inc(psem(part, name, pair_free), 1)

            def heads(part, b, full):
                for h in range(H):
                    more, most = full or h + 1 < H, full or h + 2 < H
                    h1, h2 = (h + 1) % H, (h + 2) % H
                    if more:
                        rows(part, ("qb", h1), QB[h1 % 2][:], QROWS)
                    if full and h == H - 2:
                        k_copies(part, 0)
                    exps(part, h, 2)
                    if most:
                        rows(part, ("qa", h2), QA[h2 % 4][:], P)
                    if full and h < NI:
                        x_columns(part, h)
                    exps(part, h, 3)
                    if full and 2 <= h < NI + 2:
                        leading_k(b + 1, h - 2)
                    if full and h == H - 1:
                        k_copies(part, 1)
                    if full and h == H - 1:
                        gate_exponential(b + 1)
                    if more:
                        exps(part, h1, 0)
                    if full and h == H - 3:
                        for i in range(NI):
                            leading_q(b + 1, i)
                    if more:
                        exps(part, h1, 1)

            act.wait_ge(pre["dve"], DVE_SOFTMAX - 2)
            act.activation(eaw[:], eaw[:], ACT.Exp, bias=est[:, 1:2], accum_out=est[:, 2:3]).then_inc(pre["act"], 1)
            act.wait_ge(pre["pe"], PE_AWT)
            act.activation(awT[:], pair[0][0:A, 0, 0:E], ACT.Copy).then_inc(pre["act"], 1)
            act.wait_ge(weights_in, 16 * 4)
            act.activation(WXH[:, :, 0:QC], WQ, ACT.Copy, scale=DH ** -0.5).then_inc(pre["act"], 1)
            act.activation(WXH[:, :, QC:QC + 2 * KC], WKV, ACT.Copy).then_inc(pre["act"], 1)
            x_columns(START, 0)
            x_columns(START, 1)
            act.wait_ge(pre["pe"], PE_IMP)
            act.activation(SIG, O[:, 0, 0:NSC * E], ACT.Exp, scale=-1.0).then_inc(pre["act"], 1)
            x_columns(START, 2)
            leading_q(0, 0)
            x_columns(START, 3)
            leading_q(0, 1)
            leading_k(0, 0)
            leading_k(0, 1)
            leading_q(0, 2)
            leading_k(0, 2)
            for k in range(NC):
                work_wait(act, work_full, START, ("w", k))
                act.activation(WT[:, k, :], wbank(START, ("w", k))[:], ACT.Copy) \
                    .then_inc(wsem(START, ("w", k), work_free), 1)
            leading_q(0, 3)
            leading_k(0, 3)
            for v in range(KVH):
                k_copies(START, v)
            rows(START, ("qa", 0), QA[0][:], P)
            rows(START, ("qa", 1), QA[1][:], P)
            rows(START, ("qb", 0), QB[0][:], QROWS)
            act.wait_ge(zeroed, 16 * 9)
            gate_exponential(0)
            exps(START, 0, 0)
            exps(START, 0, 1)
            with act.Fori(0, B - 1) as b:
                heads(body_part(b), b, True)
            heads(LAST, B - 1, False)

            act.wait_ge(dp_made, NC * NC)
            act.wait_ge(ao_made, B * H)

            def leading_columns(k, t):
                act.wait_ge(xg_read, t + 5)
                act.activation(XGTH[k][:].rearrange("p c t -> p (c t)"), work[k][:], ACT.Copy).then_inc(xgh_made, 1)

            for e in range(E):
                act.activation(DPHv[:, :, e, :], DPv[:, :, e, :], ACT.Copy).then_inc(dph_made, 1)
                if e in (2, 3):
                    leading_columns(e - 2, e - 2)
            with act.Fori(0, NJ // 2 - 1) as q:
                for k in range(2):
                    leading_columns(k, q * 2 + (k + 2))
            with act.Fori(0, NT // FS) as q:
                for k in range(FS):
                    act.wait_ge(z_made, q * FS + (k + FS + 1))
                    act.activation(FO[k][:], FO[k][:], ACT.Silu).then_inc(g_made, 1)

        @block.vector
        def _(dve):
            for s_, n in ((work_free[0], 1), (work_free[1], 1), (pair_free[0], 1), (pair_free[1], 1), (o_free, 1), (qk_made, 1),
                          (xn_out[0], 16), (xn_out[1], 16), (ao_out, 16), (sg_made, 2), (fat_made, 2),
                          (yg_made, 2), (y_out[0], 16), (y_out[1], 16), *((o, 16) for o in out_out)):
                dve.sem_inc(s_, n)
            count = [0]

            def step(ins):
                count[0] += 1
                ins.then_inc(pre["dve"], 1)
                dve.wait_ge(pre["dve"], count[0])

            def stats(slot, arrived, n):
                dve.wait_ge(x_in[slot], arrived)
                dve.bn_stats(bst[:], X[slot][:]).then_inc(bst_made, 1)
                dve.wait_ge(bst_made, n)
                dve.sem_inc(passed, 1)
                dve.bn_aggr(mv[slot][:], bst[:]).then_inc(mv_made, 1)
                dve.wait_ge(mv_made, n)
                dve.tensor_scalar(veps[slot][:], mv[slot][:, 1:2], EPS, None, ALU.add).then_inc(stats_made, 1)

            def normalise(n, i):
                dve.wait_ge(rstd_made, n * NI + (i + 1))
                dve.wait_ge(xn_out[i % 2], n * (8 * NI) + 16 * (i // 2 + 1))
                dve.tensor_scalar(XN[i % 2][:], X[i % 2][:], mv[i % 2][:, 0:1], rstd[i % 2][:, 0:1],
                                  ALU.subtract, ALU.mult).then_inc(xn_made, 1)
                nxt = i + 1
                dve.wait_ge(xn_made, n * NI + (i + 1))
                dve.wait_ge(stats_made, n * NI + (i + 1))
                stats(nxt % 2, n * (8 * NI) + 16 * (nxt // 2 + 1), n * NI + (nxt + 1))

            def low_x(part, n, i):
                name = ("xt", i)
                dve.wait_ge(xh_made, n * NI + (i + 1))
                dve.tensor_tensor(XTL[i % 2][:].rearrange("p c t -> p (c t)"), wbank(part, name)[:],
                                  XTH[i % 2][:].bitcast(F32).rearrange("p c t -> p (c t)"),
                                  op=ALU.subtract).then_inc(wsem(part, name, work_free), 1)

            def rotate(part, n, i):
                name = ("p", i)
                pair_wait(dve, pair_full, part, name)
                flat = pbank(part, name)[:].rearrange("p a n -> p (a n)")
                qk = flat[:, 0:QC + KC].rearrange("p (h d) -> p h d", d=DH)

                def table(a, lo, hi):
                    return rope[:, a, i, lo:hi].unsqueeze(1).broadcast_to((P, H + KVH, hi - lo))

                dve.wait_ge(qk_made, n * NI + (i + 1))
                if i == 0 and not isinstance(n, int):
                    dve.wait_ge(v_made, n * KVH)
                dve.tensor_tensor(rt1[:], qk, table(0, 0, DH), op=ALU.mult).then_inc(rope_parts, 1)
                dve.tensor_tensor(rt2[:, :, 0:HALF], qk[:, :, HALF:DH], table(1, 0, HALF),
                                  op=ALU.mult).then_inc(rope_parts, 1)
                dve.tensor_tensor(rt2[:, :, HALF:DH], qk[:, :, 0:HALF], table(1, HALF, DH),
                                  op=ALU.mult).then_inc(rope_parts, 1)
                dve.tensor_copy(VN[:, i, :, :],
                                flat[:, QC + KC:QC + 2 * KC].rearrange("p (v d) -> p v d", v=KVH))
                dve.tensor_scalar(LG[:, i, :], flat[:, WCOLS - E:WCOLS], 50.0, -50.0, ALU.min, ALU.max) \
                    .then_inc(psem(part, name, pair_free), 1)
                dve.wait_ge(rope_parts, n * (3 * NI) + 3 * (i + 1))
                dve.tensor_tensor(QK[:, i, :].rearrange("p (h d) -> p h d", d=DH), rt1[:], rt2[:],
                                  op=ALU.add).then_inc(qk_made, 1)

            def geo_columns(n):
                dve.wait_ge(qk_made, n * NI + (NI + 1))
                GA = 9
                q3 = QK[:, :, 0:QC].rearrange("p i (h d) -> p i h d", d=DH)[:, :, :, 0:3]
                dve.tensor_tensor(gt[0][:], q3, dirs[:, 1, :, :].unsqueeze(1).broadcast_to((P, NI, H, 3)),
                                  op=ALU.mult).then_inc(geo_a, 1)
                for v in range(KVH):
                    k3 = QK[:, :, QC + v * DH:QC + v * DH + 3].unsqueeze(2).broadcast_to((P, NI, REP, 3))
                    dve.tensor_tensor(gt[1][:, :, v * REP:(v + 1) * REP, :], k3,
                                      dirs[:, 0, v * REP:(v + 1) * REP, :].unsqueeze(1)
                                      .broadcast_to((P, NI, REP, 3)), op=ALU.mult).then_inc(geo_a, 1)
                dve.wait_ge(geo_a, n * GA + 3)
                dve.reduce_sum(TQ[:, :, 64:72], gt[0][:], AX).then_inc(geo_a, 1)
                dve.reduce_sum(TK[:, :, 64:72], gt[1][:], AX).then_inc(geo_a, 1)
                dve.wait_ge(geo_a, n * GA + 5)
                for t, two in ((TQ, 8), (TK, 16)):
                    dve.tensor_copy(t[:, :, 0:8].bitcast(F32R), t[:, :, 64:72]).then_inc(geo_a, 1)
                    dve.tensor_copy(t[:, :, two:two + 8].bitcast(F32R), t[:, :, 64:72]).then_inc(geo_a, 1)
                dve.wait_ge(geo_a, n * GA + 9)
                for t, rest in ((TQ, 16), (TK, 8)):
                    dve.tensor_tensor(t[:, :, rest:rest + 8], t[:, :, 64:72], t[:, :, 0:8],
                                      op=ALU.subtract).then_inc(geo_cols, 1)

            def geo_take(part, n):
                if not isinstance(n, int):
                    dve.wait_ge(kr_made, n)
                    dve.wait_ge(qg_made, n * 3)
                for name, rows_ in (("tk", kpr), ("tq", qpr)):
                    work_wait(dve, work_full, part, (name,))
                    dve.tensor_copy(rows_[:], wbank(part, (name,))[0:72, :]) \
                        .then_inc(wsem(part, (name,), work_free), 1)
                work_emptied(dve, part, ("tk",))
                work_emptied(dve, part, ("tq",))

            def geo_extremes(n):
                dve.tensor_tensor_scan(cmx[64:72, :], kpr[64:72, :], kpr[64:72, :], -3e38, ALU.max, ALU.max) \
                    .then_inc(cum_made, 1)
                dve.tensor_tensor_scan(cmn[64:72, :], kpr[64:72, :], kpr[64:72, :], 3e38, ALU.min, ALU.min) \
                    .then_inc(cum_made, 1)

            def geo_maxima(n):
                dve.wait_ge(cum_made, n * 2 + 2)
                dve.tensor_tensor(cmx[64:72, :], cmx[64:72, :], qpr[64:72, :], op=ALU.mult).then_inc(geo_b, 1)
                dve.tensor_tensor(cmn[64:72, :], cmn[64:72, :], qpr[64:72, :], op=ALU.mult).then_inc(geo_b, 1)
                dve.wait_ge(geo_b, n * 2 + 2)
                dve.tensor_tensor(cmx[64:72, :], cmx[64:72, :], cmn[64:72, :], op=ALU.max).then_inc(geo_max, 1)

            def geo_k(n):
                if not isinstance(n, int):
                    dve.wait_ge(kg_made, n * H)
                dve.tensor_copy(KR[0:24, :], kpr[0:24, :]).then_inc(kr_made, 1)

            def geo_q(n):
                dve.wait_ge(geo_max, n + 1)
                dve.tensor_copy(QG[0:24, :], qpr[0:24, :]).then_inc(qg_made, 1)
                dve.tensor_scalar(QG[64:72, :], cmx[64:72, :], -1.0, None, ALU.mult).then_inc(qg_made, 1)
                dve.wait_ge(qg_made, n * 3 + 2)
                dve.scalar_tensor_tensor(QG[96:104, :], cmx[64:72, :], -1.0, QG[64:72, :].bitcast(F32),
                                         ALU.mult, ALU.subtract).then_inc(qg_made, 1)

            def geo_rows(n, h):
                if h == 0:
                    dve.wait_ge(kr_made, n + 1)
                dve.tensor_scalar(KG[h % 2][:], KR[:], onehot[0:GROWS, h:h + 1], None, ALU.mult) \
                    .then_inc(kg_made, 1)

            def row_max(part, h, i):
                name = ("qm", h, i)
                work_wait(dve, work_full, part, name)
                dve.reduce_max(M[:, h, i:i + 1], wbank(part, name)[:, 0:P * (i + 1)], AX) \
                    .then_inc(wsem(part, name, work_free), 1)

            def minus_max(part, n, h):
                work_emptied(dve, part, ("qm", h, NI - 2))
                work_emptied(dve, part, ("qm", h, NI - 1))
                dve.tensor_scalar(QL[:, :, h, DH].bitcast(F32R), M[:, h, :], -1.0, None, ALU.mult) \
                    .then_inc(nmax_hi, 1)
                dve.wait_ge(nmax_hi, n * H + (h + 1))
                dve.scalar_tensor_tensor(QL[:, :, h, DH + 1], M[:, h, :], -1.0, QL[:, :, h, DH],
                                         ALU.mult, ALU.subtract).then_inc(nmax_made, 1)

            def mix(b, h):
                if h == 0:
                    dve.wait_ge(ao_out, b * 16 + 16)
                dve.wait_ge(o_full, b * H + (h + 1))
                oh = O[:, :, 0:NI * (DH + 1)].rearrange("p m (i d) -> p m i d", d=DH + 1)
                dve.reciprocal(rl[:], oh[:, :, :, DH]).then_inc(rl_made, 1)
                dve.wait_ge(rl_made, b * H + (h + 1))
                dve.tensor_tensor(ab[:], rl[:], hs[:, :, h].unsqueeze(2).broadcast_to((P, 2, NI)),
                                  op=ALU.mult).then_inc(ab_made, 1)
                dve.wait_ge(ab_made, b * H + (h + 1))
                if h >= 1:
                    dve.wait_ge(ao_made, b * H + h)
                dve.tensor_tensor(ow[:], oh[:, :, :, 0:DH], ab[:].unsqueeze(3).broadcast_to((P, 2, NI, DH)),
                                  op=ALU.mult).then_inc(o_free, 1)
                dve.wait_ge(o_free, b * H + (h + 2))
                dst = AOL if isinstance(b, int) else AO
                dve.tensor_tensor(dst[:, :, h * DH:(h + 1) * DH], ow[:, 0, :, :], ow[:, 1, :, :],
                                  op=ALU.add).then_inc(ao_made, 1)

            rc = [0]

            def route(ins):
                rc[0] += 1
                ins.then_inc(routing, 1)
                dve.wait_ge(routing, rc[0])

            def choose(n):
                dve.wait_ge(qk_made, n * NI + (NI + 1))
                dve.sem_inc(passed, 1)
                for i in range(NI):
                    last = dve.max(MXB[:, i, :], LG[:, i, :])
                last.then_inc(top_made, 1)
                dve.wait_ge(top_made, n * 3 + 1)
                dve.sem_inc(passed, 1)
                for i in range(NI):
                    last = dve.max_index(IXB[:, i, :], MXB[:, i, :], LG[:, i, :])
                last.then_inc(top_made, 1)
                dve.wait_ge(top_made, n * 3 + 2)
                at_ = slice(n * NI, n * NI + NI) if isinstance(n, int) else bass.ds(n * NI, NI)
                dve.tensor_copy(IX[:, at_, :], IXB[:]).then_inc(top_made, 1)

            enum = rows_f[:, NJ:NJ + E]

            def choices(n):
                if not isinstance(n, int):
                    dve.wait_ge(pairs_out, n * (16 * NI * TOPK))
                dve.tensor_tensor(gd[:, 0, :], MXB[:, :, 1], MXB[:, :, 0], op=ALU.subtract).then_inc(gate_in, 1)
                dve.tensor_tensor(OHB[:], IXB[:, :, 0:TOPK].unsqueeze(3).broadcast_to((P, NI, TOPK, E)),
                                  enum.unsqueeze(1).unsqueeze(1).broadcast_to((P, NI, TOPK, E)),
                                  op=ALU.is_equal).then_inc(oh_made, 1)
                at_ = slice(n * NI, n * NI + NI) if isinstance(n, int) else bass.ds(n * NI, NI)
                dve.tensor_copy(prow[:, :, :, 0], tokn[:, at_].unsqueeze(2).broadcast_to((P, NI, TOPK)))
                dve.wait_ge(oh_made, n + 1)
                dve.tensor_tensor(CSB[:], OHB[:, :, 0, :], OHB[:, :, 1, :], op=ALU.add).then_inc(route_cs, 1)

            def take_counts(part):
                work_wait(dve, work_full, part, ("ahead",))
                dve.tensor_copy(CNT[:, 0:NI, :].rearrange("p i e -> p (i e)"), wbank(part, ("ahead",))[:, 0:NI * E]) \
                    .then_inc(wsem(part, ("ahead",), work_free), 1)
                work_wait(dve, work_full, part, ("total",))
                dve.tensor_copy(CNT[:, NI, :], wbank(part, ("total",))[:, 0:E]) \
                    .then_inc(wsem(part, ("total",), work_free), 1)

            def pair_rows(part, b):
                work_emptied(dve, part, ("ahead",))
                work_emptied(dve, part, ("total",))
                dve.wait_ge(gate_out, b + 1)
                dve.tensor_tensor(PB[:], CNT[:, 0:NI, :], RB[:].unsqueeze(1).broadcast_to((P, NI, E)),
                                  op=ALU.add).then_inc(places, 1)
                dve.tensor_scalar(gd[:, 2, :], gd[:, 1, :], 1.0, None, ALU.add).then_inc(places, 1)
                dve.wait_ge(places, b * 7 + 2)
                dve.tensor_tensor(selb[:], OHB[:], PB[:].unsqueeze(2).broadcast_to((P, NI, TOPK, E)),
                                  op=ALU.mult).then_inc(places, 1)
                dve.tensor_tensor(RB[:], RB[:], CNT[:, NI, :], op=ALU.add).then_inc(places, 1)
                dve.reciprocal(prow[:, :, 0, 1], gd[:, 2, :]).then_inc(places, 1)
                dve.wait_ge(places, b * 7 + 5)
                dve.reduce_sum(posfb[:], selb[:], AX).then_inc(places, 1)
                dve.tensor_tensor(prow[:, :, 1, 1], gd[:, 1, :], prow[:, :, 0, 1], op=ALU.mult).then_inc(places, 1)
                dve.wait_ge(places, b * 7 + 7)
                at_ = slice(b * NI, b * NI + NI) if isinstance(b, int) else bass.ds(b * NI, NI)
                dve.tensor_copy(LPOS[:, at_, :], posfb[:])
                dve.tensor_copy(posb[:], posfb[:]).then_inc(prow_made, 1)

            def expert_starts():
                for k in range(2):
                    dve.wait_ge(xn_out[k], 16 * (NT // 2 + 1))
                    dve.wait_ge(x_in[k], 16 * (NT // 2 + 1))
                dve.wait_ge(rstd_made, NT + 1)
                dve.wait_ge(prow_made, B)
                caps = rows_f[:, NJ + E + 2:NJ + 2 * E + 2]
                route(dve.memset(ones_f[:], 1.0))
                route(dve.tensor_tensor(padc[:, 0, :], RB[:], caps, op=ALU.subtract))
                route(dve.tensor_scalar(cnti[:, 0, :], padc[:, 0, :], float(P - 1), None, ALU.add))
                route(dve.tensor_scalar(cnti[:, 1, :], cnti[:, 0, :], -P, None, ALU.bitwise_and))
                route(dve.tensor_copy(padc[:, 1, :], cnti[:, 1, :]))
                route(dve.tensor_tensor_scan(padc[:, 2, :], ones_f[:], padc[:, 1, :], 0.0, ALU.mult, ALU.add))
                route(dve.tensor_tensor(padc[:, 3, :], padc[:, 2, :], padc[:, 1, :], op=ALU.subtract))
                route(dve.tensor_tensor(padc[:, 4, :], padc[:, 3, :], caps, op=ALU.subtract))

            def tile_rows():
                p128 = rows_f[:, NJ + 2 * E + 2:NJ + 2 * E + 3]
                route(dve.tensor_scalar(ecol[:, 0, :], padc[:, 2, :], p128, None, ALU.is_le))
                route(dve.reduce_sum(ec1[:, 0:1], ecol[:, 0, :], AX))
                route(dve.tensor_scalar(ec1[:, 1:2], ec1[:, 0:1], float(E - 1), None, ALU.min))
                route(dve.tensor_scalar(ecol[:, 1, :], enum, ec1[:, 1:2], None, ALU.is_equal))
                route(dve.tensor_tensor(ecol[:, 2, :], ecol[:, 1, :], padc[:, 4, :], op=ALU.mult))
                route(dve.reduce_sum(ec1[:, 2:3], ecol[:, 2, :], AX))
                route(dve.tensor_tensor(ec1[:, 3:4], p128, ec1[:, 2:3], op=ALU.subtract))
                dve.tensor_scalar(TIX[:], ec1[:, 3:4], 1.0 / P, None, ALU.mult).then_inc(tix_made, 1)

            def tile_experts():
                route(dve.tensor_tensor(cmpj[:], rows_f[:, 0:NJ].unsqueeze(2).broadcast_to((P, NJ, E)),
                                        padc[:, 2, :].unsqueeze(1).broadcast_to((P, NJ, E)), op=ALU.is_ge))
                route(dve.reduce_sum(ejf[:], cmpj[:], AX))
                dve.tensor_scalar(eji[:], ejf[:], float(E - 1), None, ALU.min).then_inc(lists_made, 1)

            def row_choices():
                route(dve.tensor_tensor(OH[:], IX[:, :, 0:TOPK].unsqueeze(3).broadcast_to((P, NT, TOPK, E)),
                                        enum.unsqueeze(1).unsqueeze(1).broadcast_to((P, NT, TOPK, E)),
                                        op=ALU.is_equal))

            def row_offsets():
                route(dve.tensor_tensor(OH[:], OH[:], padc[:, 4, :].unsqueeze(1).unsqueeze(1)
                                        .broadcast_to((P, NT, TOPK, E)), op=ALU.mult))
                route(dve.reduce_sum(posf[:], OH[:], AX))

            def row_places():
                route(dve.tensor_tensor(posf[:], posf[:], LPOS[:], op=ALU.add))
                dve.tensor_copy(posi[:], posf[:]).then_inc(posi_made, 1)

            def piece(n):
                c, r = DP_ORDER[n]
                if n == NC:
                    dve.wait_ge(ao_out, 16 * B)
                dve.wait_ge(stage_in[n % STAGES], 16 * (n // STAGES + 1))
                cols = slice(r * P, (r + 1) * P)
                dve.tensor_tensor(DPv[:, c, :, cols], stage[n % STAGES][:].rearrange("p r e -> p e r"),
                                  WT[:, c, cols].unsqueeze(1).broadcast_to((P, E, P)), op=ALU.add).then_inc(dp_made, 1)

            def ready_before(h):
                if h == 1:
                    expert_starts()
                elif h == 2:
                    tile_rows()
                elif h <= 5:
                    piece(2 * h - 5)
                else:
                    piece(4 * h - 16)
                    piece(4 * h - 15)

            def ready_behind(h):
                if h == 1:
                    piece(0)
                elif h == 2:
                    tile_experts()
                elif h <= 4:
                    piece(2 * h - 4)
                else:
                    piece(4 * h - 14)
                    piece(4 * h - 13)

            def heads(part, b, full):
                for h in range(H):
                    n1, h1 = (b, h + 1) if h + 1 < H else (b + 1, h + 1 - H)
                    n2, h2 = (b, h + 2) if h + 2 < H else (b + 1, h + 2 - H)
                    if h >= 1:
                        mix(b, h - 1)
                        if full or h + 1 < H:
                            geo_rows(n1, h1)
                    if full and h == H - 2:
                        geo_k(b + 1)
                        geo_extremes(b + 1)
                    if full and h == H - 1:
                        geo_maxima(b + 1)
                    if full and h < NI:
                        normalise(b + 1, h)
                        low_x(part, b + 1, h)
                    if full and h == H - 3:
                        geo_columns(b + 1)
                    if not full and h >= 1:
                        ready_before(h)
                    if full or h + 2 < H:
                        for i in range(NI):
                            if full and 1 <= h <= NI and i == 2:
                                rotate(part, b + 1, h - 1)
                            if h == 0 and i == 2:
                                take_counts(part)
                            if full and h == H - 1 and i == 2:
                                pair_wait(dve, pair_full, part, ("s", H - 1, NI - 1))
                                geo_q(b + 1)
                            row_max(part, h2, i)
                        minus_max(part, n2, h2)
                    if full and h == H - 3:
                        geo_take(part, b + 1)
                    if full and h == H - 2:
                        choose(b + 1)
                        choices(b + 1)
                    if h == 0:
                        pair_rows(part, b)
                    if not full and h >= 1:
                        ready_behind(h)
                mix(b, H - 1)
                if full:
                    geo_rows(b + 1, 1)

            dve.wait_ge(early_in, 16 * 3)
            step(dve.tensor_copy(idx_t[:, 1, :].bitcast(F32), idx_t[:, 0, :]))
            step(dve.reduce_max(est[:, 0:1], eaw[:], AX))
            step(dve.tensor_scalar(est[:, 1:2], est[:, 0:1], -1.0, None, ALU.mult))
            dve.wait_ge(pre["act"], ACT_SUM)
            step(dve.reciprocal(est[:, 3:4], est[:, 2:3]))
            step(dve.tensor_scalar(eaw[:], eaw[:], est[:, 3:4], None, ALU.mult))
            assert count[0] == DVE_SOFTMAX
            dve.wait_ge(pre["pe"], PE_SLOTS)
            step(dve.tensor_copy(idx_col[:], pair[1][:, 1, 0:NSC]))
            stats(0, 16, 1)
            normalise(0, 0)
            dve.wait_ge(pre["act"], ACT_WEIGHTS)
            step(dve.scalar_tensor_tensor(WXL[:, :, 0:QC], WQ, DH ** -0.5, WXH[:, :, 0:QC].bitcast(F32),
                                          ALU.mult, ALU.subtract))
            step(dve.tensor_tensor(WXL[:, :, QC:QC + 2 * KC], WKV, WXH[:, :, QC:QC + 2 * KC].bitcast(F32),
                                   op=ALU.subtract))
            dve.wait_ge(pre["pe"], PE_GATE)
            gate_t = pair[1][:, 1, 64:64 + NC * E].rearrange("p (k e) -> p k e", k=NC)
            step(dve.tensor_copy(WXH[:, :, WCOLS - E:WCOLS], gate_t))
            step(dve.tensor_tensor(WXL[:, :, WCOLS - E:WCOLS], gate_t, WXH[:, :, WCOLS - E:WCOLS].bitcast(F32),
                                   op=ALU.subtract))
            step(dve.tensor_copy(identb[:], ident[:]))
            assert count[0] == DVE_WEIGHTS
            low_x(START, 0, 0)
            normalise(0, 1)
            low_x(START, 0, 1)
            dve.wait_ge(consts_in, 16 * 8)
            step(dve.tensor_scalar(hs[:, 0, :], hs[:, 1, :], -1.0, 1.0, ALU.mult, ALU.add))
            step(dve.tensor_tensor(EQ.rearrange("p (n s) -> p n s", n=NSC),
                                   idx_row.rearrange("p (n s) -> p n s", n=NSC),
                                   idx_col[:].unsqueeze(2).broadcast_to((P, NSC, P)), op=ALU.is_equal))
            rotate(START, 0, 0)
            normalise(0, 2)
            dve.wait_ge(pre["act"], ACT_SIG)
            step(dve.tensor_scalar(SIG, SIG, 1.0, None, ALU.add))
            step(dve.reciprocal(SIG, SIG))
            dve.wait_ge(pre["pe"], PE_DELTA)
            step(dve.tensor_tensor(UPD[:].rearrange("p n e -> p (n e)"), O[:, 1, 0:NSC * E], SIG, op=ALU.mult))
            rest = SIG.rearrange("p (n e) -> p n e", e=E)
            step(dve.tensor_copy(UPR[:, :, 0, :], UPD[:]))
            step(dve.tensor_tensor(rest, UPD[:], UPR[:, :, 0, :], op=ALU.subtract))
            step(dve.tensor_copy(UPR[:, :, 1, :], rest))
            step(dve.tensor_tensor(UPR[:, :, 2, :], rest, UPR[:, :, 1, :], op=ALU.subtract))
            assert count[0] == DVE_VALUES
            low_x(START, 0, 2)
            rotate(START, 0, 1)
            normalise(0, 3)
            dve.wait_ge(pre["pe"], PE_SUM)
            dve.wait_ge(fills, FILLS)
            for m in range(2):
                sums = O[:, m, 0:NSC // 2 * 3 * E].rearrange("p (n a e) -> p n a e", a=3, e=E)
                half = UPD[:, m * (NSC // 2):(m + 1) * (NSC // 2), :]
                step(dve.tensor_copy(half, sums[:, :, 0, :]))
                step(dve.tensor_tensor(half, half, sums[:, :, 1, :], op=ALU.add))
                step(dve.tensor_tensor(half, half, sums[:, :, 2, :], op=ALU.add))
            step(dve.tensor_tensor(EQB.rearrange("p (n s) -> p n s", n=NSC), EQ.rearrange("p (n s) -> p n s", n=NSC),
                                   before[:].unsqueeze(1).broadcast_to((P, NSC, P)), op=ALU.mult))
            assert count[0] == DVE_EARLIER
            low_x(START, 0, 3)
            rotate(START, 0, 2)
            step(dve.tensor_scalar(ibits[:, 0, :], idx_col[:], C - 1, C.bit_length() - 1,
                                   ALU.bitwise_and, ALU.logical_shift_left))
            step(dve.tensor_scalar(ibits[:, 1, :], idx_col[:], C.bit_length() - 1, None, ALU.logical_shift_right))
            step(dve.tensor_tensor(fcol[:, 0, :], ibits[:, 0, :], ibits[:, 1, :], op=ALU.add))
            step(dve.tensor_scalar(fcol[:, 2, :], fcol[:, 0, :], -1.0, rows_f[:, NJ + E + 1:NJ + E + 2],
                                   ALU.mult, ALU.add))
            dve.wait_ge(pre["pe"], PE_COUNT)
            step(dve.scalar_tensor_tensor(fcol[:, 3, :], O[:, 1, 0:NSC], 1.0, fcol[:, 2, :], ALU.min, ALU.mult))
            step(dve.tensor_tensor(fcol[:, 0, :], fcol[:, 0, :], fcol[:, 3, :], op=ALU.add))
            step(dve.tensor_copy(DSTI[:], fcol[:, 0, :]))
            assert count[0] == DVE_PLACES
            step(dve.tensor_scalar(tokn[:], rows_f[:, 0:NT], rows_f[:, NJ + E:NJ + E + 1], None, ALU.add))
            step(dve.tensor_copy(RB[:], rows_f[:, NJ + E + 2:NJ + 2 * E + 2]))
            rotate(START, 0, NI - 1)
            geo_columns(0)
            choose(0)
            choices(0)
            geo_take(START, 0)
            geo_extremes(0)
            geo_maxima(0)
            for i in range(NI):
                row_max(START, 0, i)
            minus_max(START, 0, 0)
            geo_k(0)
            geo_rows(0, 0)
            geo_q(0)
            geo_rows(0, 1)
            for i in range(NI):
                row_max(START, 1, i)
            minus_max(START, 0, 1)
            with dve.Fori(0, B - 1) as b:
                heads(body_part(b), b, True)
            heads(LAST, B - 1, False)

            def take_lists():
                dve.wait_ge(pl_rows, 1)
                dve.tensor_copy(TLI[:], work[0][:, 0:NJ]).then_inc(lists_made, 1)
                dve.tensor_copy(GL[:], work[0][:, 128:128 + NJ]).then_inc(lists_made, 1)
                dve.wait_ge(lists_made, LISTS)

            def low_columns(k, t):
                dve.wait_ge(xgh_made, t + 1)
                dve.tensor_tensor(XGTL[k][:].rearrange("p c t -> p (c t)"), work[k][:],
                                  XGTH[k][:].bitcast(F32).rearrange("p c t -> p (c t)"),
                                  op=ALU.subtract).then_inc(xgt_made, 1)

            def gated(q, k):
                dve.wait_ge(yg_made, q * 2 + (k + 1))
                column = GL[:, q * 2 + k:q * 2 + k + 1] if isinstance(q, int) else GL[:, bass.ds(q * 2 + k, 1)]
                dve.tensor_copy(GG[k][:], column).then_inc(gg_made, 1)
                dve.wait_ge(gg_made, q * 2 + (k + 1))
                dve.wait_ge(y_full, q * 2 + (k + 1))
                dve.wait_ge(y_out[k], q * 16 + 16)
                dve.tensor_scalar(YG[k], pair[k][:, 0, :], GG[k][:, 0:1], None, ALU.mult).then_inc(yg_made, 1)

            take_lists()
            row_choices()
            row_offsets()
            row_places()
            for e in range(E):
                dve.wait_ge(dph_made, e + 1)
                dve.tensor_tensor(DPLv[:, :, e, :], DPv[:, :, e, :], DPHv[:, :, e, :].bitcast(F32),
                                  op=ALU.subtract).then_inc(dpl_made, 1)
                if e == 1:
                    low_columns(0, 0)
                if e == 2:
                    low_columns(1, 1)
            with dve.Fori(0, NJ // 2 - 1) as q:
                for k in range(2):
                    gated(q, k)
                    low_columns(k, q * 2 + (k + 2))
            for k in range(2):
                gated(NJ // 2 - 1, k)

            dve.wait_ge(wo_in, 16)
            dve.wait_ge(yg_made, NJ + 2)
            dve.tensor_copy(WOH[:], WOR[:]).then_inc(wo_made, 1)
            dve.wait_ge(wo_made, 1)
            dve.tensor_tensor(WOL[:], WOR[:], WOH[:].bitcast(F32), op=ALU.subtract).then_inc(wo_made, 1)

            def mixed(q, k):
                dve.wait_ge(fa_read, q * FS + (k + 1))
                dve.tensor_copy(FATH[k % 2][:].rearrange("p c t -> p (c t)"), work[k % 2][:]).then_inc(fah_made, 1)
                dve.wait_ge(fah_made, q * FS + (k + 1))
                dve.tensor_tensor(FATL[k % 2][:].rearrange("p c t -> p (c t)"), work[k % 2][:],
                                  FATH[k % 2][:].bitcast(F32).rearrange("p c t -> p (c t)"),
                                  op=ALU.subtract).then_inc(fat_made, 1)
                dve.wait_ge(fy_in[k], q * 32 + 32)
                dve.wait_ge(out_out[k], q * 16 + 16)
                dve.tensor_tensor(FO[k][:], FY[k][0][:], FY[k][1][:], op=ALU.add).then_inc(z_made, 1)

            def finished(q, k):
                dve.wait_ge(g_made, q * FS + (k + 1))
                dve.wait_ge(s_full, q * FS + (k + 1))
                dve.tensor_tensor(FO[k][:], FO[k][:], pair[k % 2][:, 0, :], op=ALU.mult).then_inc(sg_made, 1)
                dve.wait_ge(sg_made, q * FS + (k + 3))
                dve.wait_ge(fx_in[k], q * 16 + 16)
                dve.tensor_tensor(FO[k][:], FO[k][:], FX[k][:], op=ALU.add).then_inc(fo_made, 1)

            mixed(0, 0)
            with dve.Fori(0, NT // FS - 1) as q:
                for k in range(FS):
                    mixed(*((q, k + 1) if k + 1 < FS else (q + 1, 0)))
                    finished(q, k)
            for k in range(FS):
                if k + 1 < FS:
                    mixed(NT // FS - 1, k + 1)
                finished(NT // FS - 1, k)


_INS = ["L0_attn_x", "L0_attn_Wq", "L0_attn_Wk", "L0_attn_Wv", "L0_attn_Wo", "L0_attn_head_scales",
        "L0_ffn_gate_w", "L0_ffn_W", "L0_ffn_atoms", "L0_ffn_expert_atom_weights", "L0_ffn_importance",
        "L0_ffn_mask_idx"]


def constants():
    import numpy as np
    p = np.arange(P)
    inv = (np.float32(1.0) / (10000.0 ** (np.arange(0, DH, 2, dtype=np.float32).astype(np.float64) / DH))
           .astype(np.float32)).astype(np.float32)
    ang = (np.arange(T, dtype=np.float32)[:, None] * inv[None, :]).astype(np.float64)
    cos, sin = np.cos(ang), np.sin(ang)
    rope = np.stack([np.concatenate([cos, cos], -1), np.concatenate([-sin, sin], -1)])
    rope = rope.reshape(2, NI, P, DH).transpose(2, 0, 1, 3).reshape(P, -1).astype(np.float32)
    trig = np.array([[a, b, c] for a in (1.0, -1.0) for b in (1.0, -1.0) for c in (1.0, -1.0)], np.float32)
    dirs = (trig / np.sqrt(3.0)).astype(np.float32)
    dirs = np.broadcast_to(np.stack([dirs, dirs * np.float32(DH ** 0.5)]).reshape(1, -1), (P, 2 * H * 3))
    onehot = np.zeros((P, H), np.float32)
    for r in list(range(24)) + list(range(64, 72)) + list(range(96, 104)):
        onehot[r, r % 8] = 1.0
    rows = np.zeros((P, NJ + 2 * E + 3), np.float32)
    rows[:, 0:NJ] = P * np.arange(NJ)
    rows[:, NJ:NJ + E] = np.arange(E)
    rows[:, NJ + E] = p
    rows[:, NJ + E + 1] = C * C + p
    rows[:, NJ + E + 2:NJ + 2 * E + 2] = CAP * np.arange(E)
    rows[:, NJ + 2 * E + 2] = P * p
    return {"c_ident": np.eye(P, dtype=np.float32), "c_rope": rope, "c_dirs": np.ascontiguousarray(dirs),
            "c_onehot": onehot, "c_rows": rows}


def kernel(**inputs):
    import numpy as np
    import concourse.bacc as bacc
    from concourse.bass_utils import run_bass_kernel_spmd

    nc = bacc.Bacc("TRN2", target_bir_lowering=False, num_devices=1)
    arrays, args = {}, []
    data = [(n, np.ascontiguousarray(inputs[n])) for n in _INS] + list(constants().items())
    for name, a in data:
        arrays[f"in_{name}"] = a
        args.append(nc.dram_tensor(f"in_{name}", a.shape, mybir.dt.from_np(a.dtype), kind="ExternalInput").ap())
    args.append(nc.dram_tensor("out_0", (B, T, C), F32, kind="ExternalOutput").ap())
    build(nc, *args)
    r = run_bass_kernel_spmd(nc, [arrays], core_ids=[0])
    return r.results[0]["out_0"]
```
